# Optimizing a Trainium2 kernel written in Bass

```python
import numpy as np
import jax
import jax.numpy as jnp

def _softmax(x, axis=-1):
    return jax.nn.softmax(x, axis=axis)

def _gelu(x):
    return jax.nn.gelu(x, approximate=True)

def _silu(x):
    return jax.nn.silu(x)

def _sigmoid(x):
    return jax.nn.sigmoid(x)

def _layernorm(x, axis=-1, eps=1e-05):
    m = jnp.mean(x, axis=axis, keepdims=True)
    v = jnp.var(x, axis=axis, keepdims=True)
    return (x - m) / jnp.sqrt(v + eps)

def _scatter_add(tgt, idx, src, axis=0):
    return tgt.at[idx].add(src)

def _segment_sum(src, seg, n):
    return jax.ops.segment_sum(src, seg, n)
kernel_name = 'mk_xattn_ffn_d2_seqx_r4_1d46a8'

def setup_inputs(seed: int=0):
    np.random.seed(seed)
    _w = jnp.asarray

    def _rec_inputs():
        import jax
        import jax.numpy as jnp
        _rk = jax.random.key(seed)
        x = 7.22e-05 + 1 * jax.random.normal(jax.random.fold_in(_rk, 1), (2, 1024, 256), jnp.float32)
        _lenS = 1024 - jax.random.randint(jax.random.fold_in(_rk, 7), (2,), 0, max(1, 1024 // 4) + 1, jnp.int32)
        _lenS2 = 77 - jax.random.randint(jax.random.fold_in(_rk, 8), (2,), 0, max(1, 77 // 4) + 1, jnp.int32)
        _ctx_1024P = jax.random.normal(jax.random.fold_in(_rk, 11), (2, 16, 256), jnp.float32)
        _ctx_1024c = jax.random.dirichlet(jax.random.fold_in(_rk, 511), 0.3 * jnp.ones((16,), jnp.float32), (2, 77))
        _ctx_1024t = jnp.einsum('bsk,bkd->bsd', _ctx_1024c, _ctx_1024P)
        _ctx_1024t = _ctx_1024t * jax.lax.rsqrt(jnp.mean(jnp.square(_ctx_1024t)) + 1e-12) * 0.953939
        ctx_1024 = 4.13588e-05 + 0.999923 * (_ctx_1024t + 0.3 * jax.random.normal(jax.random.fold_in(_rk, 611), (2, 77, 256), jnp.float32))
        fside_1x1xSxS2_0 = 0.000376506 + 0.999991 * jax.random.normal(jax.random.fold_in(_rk, 12), (1, 1, 1024, 77), jnp.float32)
        _validS = jnp.arange(1024)[None, :] < _lenS[:, None]
        _validS2 = jnp.arange(77)[None, :] < _lenS2[:, None]
        _causal = jnp.tril(jnp.ones((1024, 1024), dtype=bool))
        mask_BxSxS2_if1 = jnp.where(jnp.ones((2, 1024, 77), dtype=bool), 1, 0).astype(jnp.int32)
        return (x, ctx_1024, fside_1x1xSxS2_0, mask_BxSxS2_if1)
    x, ctx_1024, fside_1x1xSxS2_0, mask_BxSxS2_if1 = _rec_inputs()

    def _L0_xattn_setup():
        import jax, jax.numpy as jnp
        import numpy as np
        B, S, D, H = (4, 512, 256, 16)
        DEPTH = D // H

        def _split_heads(t):
            b, s, _ = t.shape
            return t.reshape(b, s, H, DEPTH).transpose(0, 2, 1, 3)
        key = jax.random.key(seed)
        ks = jax.random.split(key, 7)
        scale = 1.0 / np.sqrt(D)
        return {'x': jax.random.normal(ks[0], (B, S, D), dtype=jnp.float32), 'y': jax.random.normal(ks[1], (B, S, D), dtype=jnp.float32), 'bias': jax.random.normal(ks[2], (1, 1, S, S), dtype=jnp.float32), 'Wq': jax.random.normal(ks[3], (D, D), dtype=jnp.float32) * scale, 'Wk': jax.random.normal(ks[4], (D, D), dtype=jnp.float32) * scale, 'Wv': jax.random.normal(ks[5], (D, D), dtype=jnp.float32) * scale, 'Wo': jax.random.normal(ks[6], (D, D), dtype=jnp.float32) * scale}
    _L0_xattn_all = _L0_xattn_setup()
    _L0_xattn_in = {k: v for k, v in _L0_xattn_all.items() if k in ('Wq', 'Wk', 'Wv', 'Wo')}
    del _L0_xattn_all

    def _L0_ffn_setup():
        import jax, jax.numpy as jnp
        import numpy as np
        TOPK = 4
        key = jax.random.key(seed)
        ks = jax.random.split(key, 9)
        B, T, D = (4, 512, 256)
        E, H = (32, 128)
        HS = H * TOPK
        s = lambda k, shape, fan: jax.random.normal(k, shape, dtype=jnp.float32) / np.sqrt(fan)
        return {'x': jax.random.normal(ks[0], (B, T, D), dtype=jnp.float32), 'router_w': s(ks[1], (E, D), D), 'router_bias': jnp.zeros((E,), dtype=jnp.float32), 'gate_w': s(ks[2], (E, H, D), D), 'up_w': s(ks[3], (E, H, D), D), 'down_w': s(ks[4], (E, D, H), H), 'sgate_w': s(ks[5], (HS, D), D), 'sup_w': s(ks[6], (HS, D), D), 'sdown_w': s(ks[7], (D, HS), HS)}
    _L0_ffn_all = _L0_ffn_setup()
    _L0_ffn_in = {k: v for k, v in _L0_ffn_all.items() if k in ('router_w', 'router_bias', 'gate_w', 'up_w', 'down_w', 'sgate_w', 'sup_w', 'sdown_w')}
    del _L0_ffn_all

    def _L1_xattn_setup():
        import math
        import jax, jax.numpy as jnp
        import numpy as np
        EMB = 256
        H = 16
        D_K = EMB // H
        B = 2
        S = 512

        def _split_heads(x):
            b, s, _ = x.shape
            return x.reshape(b, s, H, D_K).transpose(0, 2, 1, 3)
        key = jax.random.key(seed)
        ks = jax.random.split(key, 12)
        scale = 1.0 / math.sqrt(EMB)
        inp = {'query': jax.random.normal(ks[0], (B, S, EMB), jnp.float32), 'key': jax.random.normal(ks[1], (B, S, EMB), jnp.float32), 'value': jax.random.normal(ks[2], (B, S, EMB), jnp.float32), 'mask': jnp.ones((B, S, S), jnp.int32), 'Wq': jax.random.normal(ks[3], (EMB, EMB), jnp.float32) * scale, 'bq': jnp.zeros((EMB,), jnp.float32), 'Wk': jax.random.normal(ks[4], (EMB, EMB), jnp.float32) * scale, 'bk': jnp.zeros((EMB,), jnp.float32), 'Wv': jax.random.normal(ks[5], (EMB, EMB), jnp.float32) * scale, 'bv': jnp.zeros((EMB,), jnp.float32), 'Wo': jax.random.normal(ks[6], (EMB, EMB), jnp.float32) * scale, 'bo': jnp.zeros((EMB,), jnp.float32)}
        return inp
    _L1_xattn_all = _L1_xattn_setup()
    _L1_xattn_in = {k: v for k, v in _L1_xattn_all.items() if k in ('Wq', 'bq', 'Wk', 'bk', 'Wv', 'bv', 'Wo', 'bo')}
    del _L1_xattn_all

    def _L1_ffn_setup():
        import jax, jax.numpy as jnp
        import numpy as np
        D_MODEL = 256
        D_FF = 1024
        NUM_EXPERTS = 8
        key = jax.random.key(seed)
        ks = jax.random.split(key, 8)
        scale_in = 1.0 / np.sqrt(D_MODEL)
        scale_ff = 1.0 / np.sqrt(D_FF)
        x = jax.random.normal(ks[0], (4, 512, D_MODEL), dtype=jnp.float32)
        gate_w = jax.random.uniform(ks[1], (NUM_EXPERTS, D_MODEL), jnp.float32, -scale_in, scale_in)
        gate_b = jax.random.uniform(ks[2], (NUM_EXPERTS,), jnp.float32, -scale_in, scale_in)
        expert_bias = jnp.zeros((NUM_EXPERTS,), dtype=jnp.float32)
        w1 = jax.random.uniform(ks[3], (NUM_EXPERTS, D_MODEL, D_FF), jnp.float32, -scale_in, scale_in)
        b1 = jax.random.uniform(ks[4], (NUM_EXPERTS, D_FF), jnp.float32, -scale_in, scale_in)
        w2 = jax.random.uniform(ks[5], (NUM_EXPERTS, D_FF, D_MODEL), jnp.float32, -scale_ff, scale_ff)
        b2 = jax.random.uniform(ks[6], (NUM_EXPERTS, D_MODEL), jnp.float32, -scale_ff, scale_ff)
        return {'x': x, 'gate_w': gate_w, 'gate_b': gate_b, 'expert_bias': expert_bias, 'w1': w1, 'b1': b1, 'w2': w2, 'b2': b2}
    _L1_ffn_all = _L1_ffn_setup()
    _L1_ffn_in = {k: v for k, v in _L1_ffn_all.items() if k in ('gate_w', 'gate_b', 'expert_bias', 'w1', 'b1', 'w2', 'b2')}
    del _L1_ffn_all
    return {'x': x, 'ctx_1024': ctx_1024, 'fside_1x1xSxS2_0': fside_1x1xSxS2_0, 'mask_BxSxS2_if1': mask_BxSxS2_if1, 'L0_xattn_Wq': _L0_xattn_in['Wq'], 'L0_xattn_Wk': _L0_xattn_in['Wk'], 'L0_xattn_Wv': _L0_xattn_in['Wv'], 'L0_xattn_Wo': _L0_xattn_in['Wo'], 'L0_ffn_router_w': _L0_ffn_in['router_w'], 'L0_ffn_router_bias': _L0_ffn_in['router_bias'], 'L0_ffn_gate_w': _L0_ffn_in['gate_w'], 'L0_ffn_up_w': _L0_ffn_in['up_w'], 'L0_ffn_down_w': _L0_ffn_in['down_w'], 'L0_ffn_sgate_w': _L0_ffn_in['sgate_w'], 'L0_ffn_sup_w': _L0_ffn_in['sup_w'], 'L0_ffn_sdown_w': _L0_ffn_in['sdown_w'], 'L1_xattn_Wq': _L1_xattn_in['Wq'], 'L1_xattn_bq': _L1_xattn_in['bq'], 'L1_xattn_Wk': _L1_xattn_in['Wk'], 'L1_xattn_bk': _L1_xattn_in['bk'], 'L1_xattn_Wv': _L1_xattn_in['Wv'], 'L1_xattn_bv': _L1_xattn_in['bv'], 'L1_xattn_Wo': _L1_xattn_in['Wo'], 'L1_xattn_bo': _L1_xattn_in['bo'], 'L1_ffn_gate_w': _L1_ffn_in['gate_w'], 'L1_ffn_gate_b': _L1_ffn_in['gate_b'], 'L1_ffn_expert_bias': _L1_ffn_in['expert_bias'], 'L1_ffn_w1': _L1_ffn_in['w1'], 'L1_ffn_b1': _L1_ffn_in['b1'], 'L1_ffn_w2': _L1_ffn_in['w2'], 'L1_ffn_b2': _L1_ffn_in['b2']}

def reference(x, ctx_1024, fside_1x1xSxS2_0, mask_BxSxS2_if1, L0_xattn_Wq, L0_xattn_Wk, L0_xattn_Wv, L0_xattn_Wo, L0_ffn_router_w, L0_ffn_router_bias, L0_ffn_gate_w, L0_ffn_up_w, L0_ffn_down_w, L0_ffn_sgate_w, L0_ffn_sup_w, L0_ffn_sdown_w, L1_xattn_Wq, L1_xattn_bq, L1_xattn_Wk, L1_xattn_bk, L1_xattn_Wv, L1_xattn_bv, L1_xattn_Wo, L1_xattn_bo, L1_ffn_gate_w, L1_ffn_gate_b, L1_ffn_expert_bias, L1_ffn_w1, L1_ffn_b1, L1_ffn_w2, L1_ffn_b2):
    import jax
    import jax.numpy as jnp

    def _L0_xattn_ref(x, y, bias, Wq, Wk, Wv, Wo):
        import jax, jax.numpy as jnp
        import numpy as np
        B, S, D, H = (4, 512, 256, 16)
        DEPTH = D // H

        def _split_heads(t):
            b, s, _ = t.shape
            return t.reshape(b, s, H, DEPTH).transpose(0, 2, 1, 3)
        q = _split_heads(x @ Wq.T) * DEPTH ** (-0.5)
        k = _split_heads(y @ Wk.T)
        v = _split_heads(y @ Wv.T)
        logits = jnp.einsum('bhqd,bhkd->bhqk', q, k) + bias
        weights = jax.nn.softmax(logits, axis=-1)
        attn = jnp.einsum('bhqk,bhkd->bhqd', weights, v)
        attn = attn.transpose(0, 2, 1, 3).reshape(x.shape[0], x.shape[1], D)
        return attn @ Wo.T

    def _L0_ffn_ref(x, router_w, router_bias, gate_w, up_w, down_w, sgate_w, sup_w, sdown_w):
        import jax, jax.numpy as jnp
        import numpy as np
        TOPK = 4
        B, T, D = x.shape
        flat = x.reshape(B * T, D)
        logits = flat.astype(jnp.float32) @ router_w.T + router_bias
        scores = jax.nn.softmax(logits, axis=-1)
        topk_scores, topk_idx = jax.lax.top_k(scores, TOPK)
        topk_scores = topk_scores / jnp.clip(topk_scores.sum(axis=-1, keepdims=True), 1e-12, None)
        h = jax.nn.silu(jnp.einsum('nd,ehd->neh', flat, gate_w)) * jnp.einsum('nd,ehd->neh', flat, up_w)
        expert_out = jnp.einsum('neh,edh->ned', h, down_w)
        sel = jnp.take_along_axis(expert_out, topk_idx[:, :, None], axis=1)
        out = (sel * topk_scores.astype(flat.dtype)[:, :, None]).sum(axis=1)
        out = out + jax.nn.silu(flat @ sgate_w.T) * (flat @ sup_w.T) @ sdown_w.T
        return out.reshape(B, T, D)

    def _L1_xattn_ref(query, key, value, mask, Wq, bq, Wk, bk, Wv, bv, Wo, bo):
        import math
        import jax, jax.numpy as jnp
        import numpy as np
        EMB = 256
        H = 16
        D_K = EMB // H
        B = 2
        S = 512

        def _split_heads(x):
            b, s, _ = x.shape
            return x.reshape(b, s, H, D_K).transpose(0, 2, 1, 3)
        q = _split_heads(query @ Wq.T + bq)
        k = _split_heads(key @ Wk.T + bk)
        v = _split_heads(value @ Wv.T + bv)
        scores = jnp.einsum('bhqd,bhkd->bhqk', q, k) / math.sqrt(D_K)
        scores = jnp.where(mask[:, None, :, :] == 0, -1000000000.0, scores)
        p_attn = jax.nn.softmax(scores, axis=-1)
        x = jnp.einsum('bhqk,bhkd->bhqd', p_attn, v)
        b = x.shape[0]
        x = x.transpose(0, 2, 1, 3).reshape(b, -1, H * D_K)
        return x @ Wo.T + bo

    def _L1_ffn_ref(x, gate_w, gate_b, expert_bias, w1, b1, w2, b2):
        import jax, jax.numpy as jnp
        import numpy as np
        D_MODEL = 256
        D_FF = 1024
        NUM_EXPERTS = 8
        gate_logits = jnp.einsum('bsd,ed->bse', x, gate_w) + gate_b + expert_bias
        top_idx = jnp.argmax(gate_logits, axis=-1)
        out = jnp.zeros_like(x)
        for e in range(NUM_EXPERTS):
            mask = (top_idx == e)[..., None].astype(x.dtype)
            h = jax.nn.relu(jnp.einsum('bsd,df->bsf', x, w1[e]) + b1[e])
            y = jnp.einsum('bsf,fd->bsd', h, w2[e]) + b2[e]
            out = out + mask * y
        return out
    x = x + _L0_xattn_ref(_layernorm(x, axis=-1), ctx_1024, fside_1x1xSxS2_0, L0_xattn_Wq, L0_xattn_Wk, L0_xattn_Wv, L0_xattn_Wo)
    x = x + _L0_ffn_ref(_layernorm(x, axis=-1), L0_ffn_router_w, L0_ffn_router_bias, L0_ffn_gate_w, L0_ffn_up_w, L0_ffn_down_w, L0_ffn_sgate_w, L0_ffn_sup_w, L0_ffn_sdown_w)
    x = x + _L1_xattn_ref(_layernorm(x, axis=-1), ctx_1024, ctx_1024, mask_BxSxS2_if1, L1_xattn_Wq, L1_xattn_bq, L1_xattn_Wk, L1_xattn_bk, L1_xattn_Wv, L1_xattn_bv, L1_xattn_Wo, L1_xattn_bo)
    x = x + _L1_ffn_ref(_layernorm(x, axis=-1), L1_ffn_gate_w, L1_ffn_gate_b, L1_ffn_expert_bias, L1_ffn_w1, L1_ffn_b1, L1_ffn_w2, L1_ffn_b2)
    return x

_drawn_inputs = setup_inputs


def setup_inputs(seed=0):
    import zlib

    import numpy as np

    out = dict(_drawn_inputs(seed))
    spreads = {'L0_ffn_router_bias': (0.0, 0.1),
     'L1_xattn_bq': (0.0, 0.295),
     'L1_xattn_bk': (0.0, 0.8),
     'L1_xattn_bv': (0.0, 0.1),
     'L1_xattn_bo': (0.0, 0.1),
     'L1_ffn_expert_bias': (0.0, 0.1)}
    factors = {'L1_ffn_b1': 6.583, 'L1_ffn_b2': 5.209}
    for name, (base, spread) in spreads.items():
        noise = np.random.default_rng([zlib.crc32(name.encode()), seed]).standard_normal(out[name].shape)
        drawn = base * np.exp(spread * noise) if base else spread * noise
        out[name] = jnp.asarray(drawn.astype(out[name].dtype))
    for name, factor in factors.items():
        out[name] = (out[name] * factor).astype(out[name].dtype)
    return out
```

```python
from contextlib import ExitStack

import concourse.bass as bass
import numpy as np
from concourse import mybir

F32 = mybir.dt.float32
BF16 = mybir.dt.bfloat16
I32 = mybir.dt.int32
U32 = mybir.dt.uint32
ALU = mybir.AluOpType
ACT = mybir.ActivationFunctionType
AX = mybir.AxisListType

P = 128
B, S, D = 2, 1024, 256
S2 = 77
N = B * S
NT = N // P
TB = S // P
KC = D // P
H, DH = 16, 16
HG = 4
NG = H // HG
PC = (H * S2 + P - 1) // P
LASTROWS = H * S2 - (PC - 1) * P
VC = DH + 1
E0, TOPK, F0 = 32, 4, 128
FS = 512
E1, F1 = 8, 1024
FC1 = F1 // P
JT = N // P
COLS0, COLS1 = E0 * JT, E1 * JT
TILES0 = (N * TOPK - E0) // P + E0 + 1
TILES1 = (N - E1) // P + E1 + 1
EPS = 1e-5
MASKED = -1e30
SKIP = 1 << 20
HEAD0 = [P * c // S2 for c in range(PC)]


def need(eng, sem, n):
    if not isinstance(n, int) or n > 0:
        eng.wait_ge(sem, n)


def landed(i, n, per=1):
    return 16 * per * (i // n + 1)


def build(nc, A):
    ctx = ExitStack()
    with ctx:
        def sb(name, shape, dt=F32):
            return ctx.enter_context(nc.sbuf_tensor(name, shape, dt))

        def sem(name):
            return ctx.enter_context(nc.semaphore(name))

        def cut(region, at, shape, dt=F32):
            n = int(np.prod(shape))
            words = n if dt in (F32, I32, U32) else (n + 1) // 2
            v = region[:, at:at + words]
            if dt != F32:
                v = v.bitcast(dt)
            if len(shape) > 1:
                names = "abcd"[:len(shape)]
                v = v.rearrange(f"p ({' '.join(names)}) -> p {' '.join(names)}",
                                **dict(zip(names, shape)))
            return v, at + words

        v_rows = [nc.dram_tensor(f"v_rows{l}", (B, H * S2, DH), F32).ap() for l in range(2)]
        table_d = [nc.dram_tensor(f"table{l}", (P * c, 1), I32).ap() for l, c in enumerate((COLS0, COLS1))]
        xn_d = [nc.dram_tensor(f"normed{l}", (N, D), F32).ap() for l in range(2)]
        x3_d = nc.dram_tensor("x3", (N, D), F32).ap()
        y_d = nc.dram_tensor("expert_out", (TILES0 * P, D), F32).ap()

        R1 = sb("R1", [P, KC * E0 * 2 * F0])
        R2 = sb("R2", [P, E1 * FC1 * D])
        X = sb("X", [P, NT * D])
        U = sb("U", [P, 11600])

        gu_w, _ = cut(R1, 0, (KC, E0, 2 * F0))
        w1_w, _ = cut(R1, 0, (KC, E1, F1))
        down_w, o = cut(R2, 0, (E0, D))
        sgu_w, o = cut(R2, o, (KC, 2 * FS))
        sdown_w, o = cut(R2, o, (FS // P, D))
        attn_w = [{}, {}]
        for name in ("Wq", "Wk", "Wv", "Wo"):
            attn_w[0][name], o = cut(R2, o, (KC, D))
        kbd, vbd, bias = [None, None], [None, None], [None, None]
        kbd[0], o = cut(R2, o, (B * KC, HG, S2))
        vbd[0], o = cut(R2, o, (B * PC, 3 * VC))
        bias[0], o = cut(R2, o, (TB, S2))
        assert o <= E1 * FC1 * D
        w2_w, _ = cut(R2, 0, (E1, FC1, D))
        x, _ = cut(X, 0, (NT, D))

        o = 0
        for name in ("Wq", "Wk", "Wv", "Wo"):
            attn_w[1][name], o = cut(U, o, (KC, D))
        kbd[1], o = cut(U, o, (B * KC, HG, S2))
        vbd[1], o = cut(U, o, (B * PC, 3 * VC))
        bias[1], o = cut(U, o, (NT, S2))
        temp_at = o
        sc = [None, None]
        sc[0], o = cut(U, o, (H * S2,))
        sc[1], o = cut(U, o, (H * S2,))
        pT, o = cut(U, o, (PC, P))
        yg, o = cut(U, o, (2 * TOPK, D))
        k_sb, o2 = cut(U, o - 2 * TOPK * D, (B * S2,))
        zeros, o2 = cut(U, o2, (COLS0,), I32)
        ctxT, o2 = cut(U, o2, (KC, B * S2))
        bv_b, o2 = cut(U, o2, (D,))
        assert o2 <= o - 632
        vf, o2 = cut(U, o - 632, (B * PC, DH))
        v_sb, o2 = cut(U, o2, (B, D))
        bo_row, o3 = cut(U, o, (D,))
        assert o3 <= 11600 and o2 <= 11600
        b1_b, o = cut(U, 0, (E1, F1))
        b2_b, o = cut(U, o, (E1, D))
        x3g, y1 = [], []
        for i in range(2):
            for lst in (x3g, y1):
                v, o = cut(U, o, (D,))
                lst.append(v)
        assert o <= 11600
        hs = [None, None]
        o = temp_at
        hs[0], o = cut(U, o, (FS,))
        hs[1], o = cut(U, o, (FS,))
        th, o = cut(U, o, (FS,))
        hsT, o = cut(U, o, (FS // P, P))
        ge_t, o = cut(U, o, (TILES0, E0))
        assert o <= 10690
        picked, o = cut(U, 10690 - NT * TOPK * E0, (NT * TOPK, E0))
        o = temp_at
        xg0, xgT0, h0, hT0, y0, th0, t0_ = [], [], [], [], [], [], []
        for i in range(2):
            for lst, shape in ((xg0, (D,)), (xg0, (D,)), (xgT0, (KC, P)), (h0, (F0,)), (hT0, (P,)), (y0, (D,)),
                               (th0, (F0,)), (t0_, (F0,))):
                v, o = cut(U, o, shape)
                lst.append(v)
        assert o <= 10690 - NT * TOPK * E0
        o = 0
        xg1, xgT1, h1 = [], [], []
        for i in range(2):
            for lst, shape in ((xg1, (D,)), (xgT1, (KC, P)), (h1, (F1,))):
                v, o = cut(X, o, shape)
                lst.append(v)
        hT1, o = cut(X, o, (FC1, P))
        assert o <= NT * D

        ident = sb("ident", [P, P])
        tri = sb("tri", [P, P], BF16)
        ones16 = sb("ones16", [P, P], BF16)
        ones_row = sb("ones_row", [1, P])
        iota_e = sb("iota_e", [P, E0])
        iota_t = sb("iota_t", [1, TILES0])
        tok_id = sb("tok_id", [P, NT], I32)
        skip_id = sb("skip_id", [P, COLS1], I32)
        mask_k = sb("mask_k", [P, HG])
        mask_v = sb("mask_v", [P, PC, 3])
        neg_half = sb("neg_half", [P, 1])
        ge1 = sb("ge1", [1, TILES1, E1])
        bqk = sb("bqk", [P, 2, KC])
        bq4 = sb("bq4", [P, KC])
        rw = [sb("rw0", [P, KC, E0]), sb("rw1", [P, KC, E1])]
        rb = [sb("rb0", [1, 1, E0]), sb("rb1", [1, 2, E1])]
        xn = [sb(f"xn{i}", [P, D]) for i in range(2)]
        xT = sb("xT", [P, KC, P])
        qz = sb("qz", [P, KC, 2, P])
        o_sb = sb("o_sb", [P, D])
        oT = sb("oT", [P, KC, P])
        stat = sb("stat", [P, 2, 6])
        mv = sb("mv", [P, 2, 2])
        ve = sb("ve", [P, 2])
        rstd = sb("rstd", [P, 2])
        tok_cur = [sb(f"tok_cur{i}", [P, 1], I32) for i in range(2)]
        mx = [sb(f"mx{i}", [P, H]) for i in range(2)]
        rs = sb("rs", [P, H])
        lg = sb("lg", [P, E0])
        m8 = sb("m8", [P, 8])
        i8 = sb("i8", [P, 8], U32)
        nm = sb("nm", [P, 1])
        ew = sb("ew", [P, TOPK])
        es = sb("es", [P, 1])
        er = sb("er", [P, 1])
        ef = sb("ef", [P, TOPK])
        oh = o_sb[:, 0:TOPK * E0].rearrange("p (j e) -> p j e", j=TOPK)
        ohr = oT[:, 0, 0:TOPK * E0].rearrange("p (j e) -> p j e", j=TOPK)
        chosen = sb("chosen", [P, E0], BF16)
        chosen_before = sb("chosen_before", [P, (NT + 1) * E0], BF16)
        rk = sb("rk", [P, TOPK])
        slot = [sb("slot0", [P, NT * TOPK], I32), sb("slot1", [P, NT], I32)]
        adr_a = sb("adr_a", [P, TOPK], I32)
        adr_b = sb("adr_b", [P, TOPK], I32)
        adr = [sb(f"adr{i}", [P, TOPK], I32) for i in range(2)]
        slot_cur = [sb(f"slot_cur{i}", [P, TOPK], I32) for i in range(2)]
        wgt = sb("wgt", [P, NT * TOPK])
        ef_all = sb("ef_all", [P, NT * TOPK], I32)
        shift_of = sb("shift_of", [P, NT * TOPK])
        table = sb("table", [P, COLS0 + TILES0], I32)
        cnt = sb("cnt", [P, E0], I32)
        cntf = sb("cntf", [P, E0])
        end = sb("end", [P, E0])
        shift = sb("shift", [P, E0])
        pe_i, ps_i, pj_i = xT[0:1, 0, 0:TILES0], xT[0:1, 1, 0:TILES0], oT[0:1, 1, 0:TILES0]
        plan_e = sb("plan_e", [1, TILES0], I32)
        plan_c = sb("plan_c", [1, TILES0], I32)
        idx = [sb(f"idx{i}", [P, 1], I32) for i in range(4)]

        bank = [ctx.enter_context(nc.psum_tensor(f"bank{i}", [P, 512], F32)) for i in range(8)]

        phase_end = sem("phase_end")
        phases = [0]

        def phase_barrier(eng, k):
            eng.drain().then_inc(phase_end, 1)
            eng.wait_ge(phase_end, 5 * k)

        consts_in = sem("consts_in")
        tri_in = sem("tri_in")
        ctx_in = sem("ctx_in")
        x_in = sem("x_in")
        route_in = [sem("route0_in"), sem("route1_in")]
        attn_in = [sem("attn0_in"), sem("attn1_in")]
        bias_in = [sem("bias0_in"), sem("bias1_in")]
        shared_in = sem("shared_in")
        experts0_in = sem("experts0_in")
        w1_in = sem("w1_in")
        w2_in = sem("w2_in")
        b12_in = sem("b12_in")
        bo_in = sem("bo_in")
        q_zero = sem("q_zero")
        waited_apart = sem("waited_apart")
        zeros_set = sem("zeros_set")
        table_init = sem("table_init")

        class Sems(dict):

            def __init__(self, prefix, **turns):
                self.prefix, self.turns = prefix, turns

            def __missing__(self, name):
                n = self.turns.get(name)
                full = f"{self.prefix}_{name}"
                self[name] = [sem(f"{full}{i}") for i in range(n)] if n else sem(full)
                return self[name]

        KV = [Sems(f"kv{l}") for l in range(2)]
        AT, ATL = Sems("at"), [Sems(f"at{l}", gath=2) for l in range(2)]
        RT, RTL = Sems("rt", saved=2), [Sems(f"rt{l}", scat=2) for l in range(2)]
        EX = [Sems("ex0", gath=4, out=2), Sems("ex1", gath=2, gath3=2, out=4)]

        block = ctx.enter_context(nc.Block())

        place = [0]

        def steps(eng, step, first, lo, hi, last, unroll):
            assert lo % unroll == 0 and (hi - lo) % unroll == 0
            for t in range(first, lo):
                place[0] = t % unroll
                step(t)
            with eng.Fori(0, (hi - lo) // unroll) as k:
                for u in range(unroll):
                    place[0] = u
                    step(unroll * k + (lo + u))
            for t in range(hi, last + 1):
                place[0] = t % unroll
                step(t)

        def par(j, n=2):
            return (place[0] + j) % n

        def attention_steps(eng, step):
            steps(eng, step, -5, 2, 10, NT, 2)

        def route_steps(eng, step):
            steps(eng, step, -2, 2, NT - 2, NT - 1, 2)

        def experts0_steps(eng, step):
            steps(eng, step, -4, 4, TILES0 - 4, TILES0 - 1, 4)

        def experts1_steps(eng, step):
            steps(eng, step, -3, 4, TILES1 - 4, TILES1 - 1, 4)

        def wait_apart(eng, sem, n):
            eng.wait_ge(sem, n)
            if not isinstance(n, int):
                eng.sem_inc(waited_apart, 1)

        def on(t, j, tiles=NT):
            return not isinstance(t, int) or 0 <= t + j < tiles

        def kv_values(sp, l):
            for b in range(B):
                sp.wait_ge(KV[l]["v_sb"], b + 1)
                sp.dma_start(v_rows[l][b].rearrange("(h k) d -> k h d", h=H),
                             v_sb[0:S2, b, :].rearrange("k (h d) -> k h d", h=H)).then_inc(KV[l]["v_out"], 16)
            sp.wait_ge(KV[l]["v_out"], 16 * B)
            sp.wait_ge(KV[l]["vf_zero"], 1)
            for b in range(B):
                full = (PC - 1) * P
                sp.dma_start(vf[:, b * PC:(b + 1) * PC - 1, :],
                             v_rows[l][b, 0:full].rearrange("(c p) d -> p c d", p=P)).then_inc(KV[l]["v_back"], 16)
                sp.dma_start(vf[0:LASTROWS, (b + 1) * PC - 1, :],
                             v_rows[l][b, full:H * S2]).then_inc(KV[l]["v_back"], 16)

        def route_stores(sp, l):
            R, RL = RT, RTL[l]
            with sp.Fori(0, NT // 2) as k:
                for u in range(2):
                    t = 2 * k + u
                    n = t + NT * l
                    sp.wait_ge(R["xn"], n + 1)
                    sp.dma_start(xn_d[l][bass.ds(t * P, P), :], xn[u][:, :]).then_inc(R["saved"][u], 16)
            if l == 1:
                sp.dma_start(x3_d.rearrange("(t p) d -> p t d", p=P), x).then_inc(RL["x_saved"], 16)
                sp.wait_ge(RL["x_saved"], 16)
            for u in range(2):
                sp.wait_ge(R["saved"][u], 16 * NT // 2 * (l + 1))
            cols = (COLS0, COLS1)[l]
            for u in range(2):
                sp.wait_ge(RL["scat"][u], 16 * NT // 2 * (TOPK, 1)[l])
            sp.dma_start(table[:, 0:cols], table_d[l].rearrange("(p c) a -> p (c a)", p=P)).then_inc(RL["table"], 16)
            sp.wait_ge(RL["table"], 16)

        @block.sync
        def _(sp):
            for name, dst in (("ident", ident), ("mask_k", mask_k), ("mask_v", mask_v), ("neg_half", neg_half),
                              ("tri", None), ("iota_e", iota_e), ("iota_t", iota_t), ("tok_id", tok_id),
                              ("skip_id", skip_id), ("ones_row", ones_row)):
                if dst is not None:
                    sp.dma_start(dst[tuple(slice(None) for _ in dst.shape)], A[name]).then_inc(consts_in, 16)
            sp.dma_start(ctxT, A["ctxT"]).then_inc(ctx_in, 16)
            for name in ("Wk", "Wv", "Wq", "Wo"):
                sp.dma_start(attn_w[0][name], A[f"L0_{name}"]).then_inc(attn_in[0], 16)
            sp.dma_start(bias[0], A["bias0"]).then_inc(bias_in[0], 16)
            sp.dma_start(rw[0][:, :, :], A["rw0"]).then_inc(route_in[0], 16)
            sp.dma_start(rb[0][:, :, :], A["rb0"]).then_inc(route_in[0], 16)
            sp.wait_ge(zeros_set, 1)
            sp.dma_start(table_d[0].rearrange("(p c) a -> p (c a)", p=P), zeros).then_inc(table_init, 16)
            sp.wait_ge(consts_in, 16 * 9)
            sp.dma_start(table_d[1].rearrange("(p c) a -> p (c a)", p=P), skip_id[:, :]).then_inc(table_init, 16)
            kv_values(sp, 0)
            sp.dma_start(sgu_w, A["sgu"]).then_inc(shared_in, 16)
            sp.dma_start(sdown_w, A["sdown"]).then_inc(shared_in, 16)
            for e in range(0, E0, 4):
                sp.dma_start(gu_w[:, :, e:e + 4, :], A["gu"][:, :, e:e + 4, :]).then_inc(experts0_in, 16)
            for e in range(0, E0, 8):
                sp.dma_start(down_w[:, e:e + 8, :], A["down"][:, e:e + 8, :]).then_inc(experts0_in, 16)
            for name in ("Wk", "Wv", "Wq", "Wo"):
                sp.dma_start(attn_w[1][name], A[f"L1_{name}"]).then_inc(attn_in[1], 16)
            sp.dma_start(bqk[:, :, :], A["bqk"]).then_inc(attn_in[1], 16)
            sp.dma_start(bv_b[0:S2, :], A["bv"].partition_broadcast(S2)).then_inc(attn_in[1], 16)
            sp.dma_start(bias[1].bitcast(I32), A["mask1"]).then_inc(bias_in[1], 16)
            sp.dma_start(rw[1][:, :, :], A["rw1"]).then_inc(route_in[1], 16)
            sp.dma_start(rb[1][:, :, :], A["rb1"]).then_inc(route_in[1], 16)
            phase_barrier(sp, 1)
            phase_barrier(sp, 2)
            kv_values(sp, 1)
            sp.dma_start(bo_row[0:1, :], A["bo"]).then_inc(bo_in, 16)
            route_stores(sp, 0)
            phase_barrier(sp, 3)
            with sp.Fori(0, TILES0 // 2) as k:
                for u in range(2):
                    i = 2 * k + u
                    sp.wait_ge(EX[0]["y"], i + 1)
                    sp.dma_start(y_d[bass.ds(i * P, P), :], y0[u]).then_inc(EX[0]["out"][u], 16)
            for u in range(2):
                sp.wait_ge(EX[0]["out"][u], 16 * TILES0 // 2)
            phase_barrier(sp, 4)
            for e in range(0, E1, 2):
                for c in range(KC):
                    sp.dma_start(w1_w[:, c, e:e + 2, :], A["w1"][:, c, e:e + 2, :]).then_inc(w1_in, 16)
            for e in range(0, E1, 2):
                sp.dma_start(w2_w[:, e:e + 2], A["w2"][:, e:e + 2]).then_inc(w2_in, 16)
            phase_barrier(sp, 5)
            sp.dma_start(b1_b, A["b1"].partition_broadcast(P)).then_inc(b12_in, 16)
            sp.dma_start(b2_b, A["b2"].partition_broadcast(P)).then_inc(b12_in, 16)
            route_stores(sp, 1)
            phase_barrier(sp, 6)
            phase_barrier(sp, 7)

        def routing(pool, l):
            R, RL, k_ = RT, RTL[l], (TOPK, 1)[l]
            pool.wait_ge(table_init, 32)

            def step(t):
                n = t + NT * l
                u = par(0)
                if on(t, 2):
                    pool.wait_ge(R["ve"], n + 3)
                    pool.tensor_tensor(rstd[:, u:u + 1], ve[:, u:u + 1], neg_half[:, :],
                                       ALU.pow).then_inc(R["rstd"], 1)
                if on(t, 0):
                    wait_apart(pool, R["adr"], n + 1)
                    for j in range(k_):
                        pool.indirect_dma_start(
                            table_d[l], bass.IndirectOffsetOnAxis(adr[u][:, j:j + 1], 0),
                            tok_cur[u][:, :], None).then_inc(RL["scat"][u], 16)
            route_steps(pool, step)

        @block.gpsimd
        def _(pool):
            pool.memset(zeros, 0).then_inc(zeros_set, 1)
            pool.memset(qz[:, :, :, :], 0.0).then_inc(q_zero, 1)
            pool.memset(ones16[:, :], 1.0)
            pool.memset(chosen_before[:, 0:E0], 0.0)
            pool.memset(table[:, COLS0:COLS0 + TILES0], 0)
            pool.dma_start(o_sb[:, 0:P], A["tri"]).then_inc(tri_in, 16)
            pool.wait_ge(tri_in, 16)
            nc.gpsimd.tensor_copy(tri[:, :], o_sb[:, 0:P])
            phase_barrier(pool, 1)

            def attention(l):
                T, TL = AT, ATL[l]

                def step(t):
                    n = t + NT * l
                    if l == 1 and on(t, 5):
                        u = par(5)
                        need(pool, TL["x_comb"], t + 4)
                        pool.tensor_copy(slot_cur[u][:, :], slot[0][:, bass.ds((t + 5) * TOPK, TOPK)]).then_inc(
                            TL["slots"], 1)
                        wait_apart(pool, TL["slots"], t + 6)
                        for j in range(TOPK):
                            pool.indirect_dma_start(
                                yg[:, u * TOPK + j, :], None, y_d,
                                bass.IndirectOffsetOnAxis(slot_cur[u][:, j:j + 1], 0)).then_inc(TL["gath"][u], 16)
                    if on(t, 4):
                        pool.wait_ge(T["ve"], n + 5)
                        u = par(4)
                        pool.tensor_tensor(rstd[:, u:u + 1], ve[:, u:u + 1], neg_half[:, :], ALU.pow).then_inc(T["rstd"], 1)
                    if on(t, 2):
                        u = par(2)
                        pool.wait_ge(T["mx"], 2 * n + 6)
                        s3 = sc[u].rearrange("p (h k) -> p h k", h=H)
                        pool.tensor_tensor(s3, s3, mx[u][:, :].unsqueeze(2).to_broadcast([P, H, S2]),
                                           ALU.subtract).then_inc(T["sub"], 1)
                attention_steps(pool, step)

            attention(0)
            phase_barrier(pool, 2)
            routing(pool, 0)
            phase_barrier(pool, 3)
            with pool.Fori(0, TILES0 // 4) as k:
                for u in range(4):
                    i = 4 * k + u
                    wait_apart(pool, EX[0]["idx"], i + 1)
                    pool.indirect_dma_start(xg0[u], None, xn_d[0],
                                            bass.IndirectOffsetOnAxis(idx[u][:, :], 0)).then_inc(EX[0]["gath"][u], 16)
            phase_barrier(pool, 4)
            attention(1)
            phase_barrier(pool, 5)
            routing(pool, 1)
            phase_barrier(pool, 6)
            X1, last_row = EX[1], pool.snap(N - 1)

            def gather(dst, src, v, landed_on):
                pool.indirect_dma_start(dst, None, src, bass.IndirectOffsetOnAxis(idx[v][:, :], 0),
                                        bounds_check=last_row, oob_is_err=False).then_inc(landed_on, 16)

            def rows(i, u, v):
                need(pool, X1["xt_mm"], i - 1)
                wait_apart(pool, X1["idx"], i + 1)
                gather(xg1[u], xn_d[1], v, X1["gath"][u])

            def results(i, u, v):
                wait_apart(pool, X1["y2"], i + 1)
                pool.indirect_dma_start(A["out"], bass.IndirectOffsetOnAxis(idx[v][:, :], 0), y1[u], None,
                                        bounds_check=last_row, oob_is_err=False).then_inc(X1["out"][v], 16)

            def residual(i, u, v):
                gather(x3g[u], x3_d, v, X1["gath3"][u])

            def step(s):
                if on(s, 2, TILES1):
                    rows(s + 2, par(2), par(2, 4))
                if on(s, 0, TILES1):
                    results(s, par(0), par(0, 4))
                if on(s, 2, TILES1):
                    residual(s + 2, par(2), par(2, 4))
            experts1_steps(pool, step)
            for v in range(4):
                pool.wait_ge(X1["out"][v], 16 * TILES1 // 4)
            phase_barrier(pool, 7)

        @block.scalar
        def _(act):
            act.dma_start(x, A["x"]).then_inc(x_in, 16)

            def kv(l):
                K = KV[l]
                for b in range(B):
                    act.wait_ge(K["v_mm"], b + 1)
                    if l == 0:
                        act.activation(v_sb[0:S2, b, :], bank[2 + b][0:S2, 0:D], ACT.Copy).then_inc(K["v_sb"], 1)
            kv(0)
            phase_barrier(act, 1)

            def attention(l):
                T, TL = AT, ATL[l]

                def step(t):
                    n = t + NT * l
                    if on(t, 2):
                        act.wait_ge(T["xt_mm"], n + 3)
                        act.activation(xT[:, :, :].rearrange("p c n -> p (c n)"), bank[4][:, 0:D],
                                       ACT.Copy).then_inc(T["xt"], 1)
                    if on(t, 0):
                        for g in range(2):
                            act.wait_ge(T["pt_mm"], 3 * n + g + 1)
                            if g == 0:
                                need(act, T["pv_mm"], n)
                            act.activation(pT[:, 4 * g:4 * g + 4, :].rearrange("p c n -> p (c n)"), bank[5 + g][:, :],
                                           ACT.Copy).then_inc(T["pt"], 1)
                    if on(t, 2):
                        act.wait_ge(T["q_mm"], n + 3)
                        for half in range(2):
                            r = slice(64 * half, 64 * half + 64)
                            if l == 0:
                                ins = act.activation(qz[r, :, half, :],
                                                     bank[4][r, 0:D].rearrange("p (c n) -> p c n", c=KC),
                                                     ACT.Copy, scale=DH ** -0.5)
                            else:
                                for c in range(KC):
                                    ins = act.activation(qz[r, c, half, :], bank[4][r, c * P:(c + 1) * P],
                                                         ACT.Identity, bias=bq4[r, c:c + 1], scale=DH ** -0.5)
                        ins.then_inc(T["q"], 1)
                    if on(t, 0):
                        act.wait_ge(T["pt_mm"], 3 * n + 3)
                        act.activation(pT[:, 8, :], bank[5][:, 0:P], ACT.Copy)
                        act.activation(pT[0:LASTROWS, 9, :], bank[5][0:LASTROWS, P:2 * P],
                                       ACT.Copy).then_inc(T["pt"], 1)
                    if on(t, 1):
                        u = par(1)
                        act.wait_ge(T["sub"], n + 2)
                        act.activation(sc[u], sc[u], ACT.Exp).then_inc(T["p"], 1)
                    if on(t, 0):
                        act.wait_ge(T["ot_mm"], n + 1)
                        act.activation(oT[:, :, :].rearrange("p c n -> p (c n)"), bank[7][:, 0:D],
                                       ACT.Copy).then_inc(T["ot"], 1)
                attention_steps(act, step)

            attention(0)
            phase_barrier(act, 2)

            def route(l):
                R, RL = RT, RTL[l]

                def step(t):
                    n = t + NT * l
                    u = par(0)
                    if on(t, 1):
                        act.wait_ge(R["xt_mm"], n + 2)
                        act.activation(xT[:, :, :].rearrange("p c n -> p (c n)"), bank[4][:, 0:D],
                                       ACT.Copy).then_inc(R["xt"], 1)
                    if l == 0 and on(t, 0):
                        act.wait_ge(R["nm"], n + 1)
                        act.activation(ew[:, :], m8[:, 0:TOPK], ACT.Exp, bias=nm[:, :],
                                       accum_out=es[:, :]).then_inc(R["ew"], 1)
                        act.wait_ge(R["g_mm"], n + 1)
                        need(act, R["act"], n)
                        act.activation(th, bank[2 * u][:, :], ACT.Tanh, scale=0.5).then_inc(R["th"], 1)
                        act.wait_ge(R["ht_mm"], n + 1)
                        act.activation(hsT.rearrange("p c n -> p (c n)"), bank[5][:, :],
                                       ACT.Copy).then_inc(R["ht"], 1)
                route_steps(act, step)

            route(0)
            phase_barrier(act, 3)
            X0 = EX[0]

            def experts0(s):
                u = par(0)
                if on(s, 3, TILES0):
                    act.wait_ge(X0["xt_mm"], s + 4)
                    act.activation(xgT0[(u + 1) % 2].rearrange("p c n -> p (c n)"), bank[(u + 1) % 2][:, 0:D],
                                   ACT.Copy).then_inc(X0["xt"], 1)
                if on(s, 1, TILES0):
                    act.wait_ge(X0["ht_mm"], s + 2)
                    act.activation(hT0[(u + 1) % 2], bank[4 + (u + 1) % 2][:, 0:P], ACT.Copy).then_inc(X0["ht"], 1)
                if on(s, 2, TILES0):
                    act.wait_ge(X0["h_mm"], s + 3)
                    act.activation(th0[u], bank[2 + u][:, 0:F0], ACT.Tanh, scale=0.5).then_inc(X0["th"], 1)
            experts0_steps(act, experts0)
            phase_barrier(act, 4)
            attention(1)
            phase_barrier(act, 5)
            route(1)
            phase_barrier(act, 6)
            X1 = EX[1]

            def experts1(s):
                u = par(0)
                if on(s, 2, TILES1):
                    act.wait_ge(X1["xt_mm"], s + 3)
                    act.activation(xgT1[u].rearrange("p c n -> p (c n)"), bank[0][:, 0:D],
                                   ACT.Copy).then_inc(X1["xt"], 1)
                if on(s, 0, TILES1):
                    for g in range(2):
                        act.wait_ge(X1["ht_mm"], 2 * s + g + 1)
                        if g == 0:
                            need(act, X1["dn_mm"], s)
                        act.activation(hT1[:, 4 * g:4 * g + 4, :].rearrange("p c n -> p (c n)"), bank[5 + g][:, :],
                                       ACT.Relu).then_inc(X1["ht"], 1)
            experts1_steps(act, experts1)
            phase_barrier(act, 7)

        def batch(t, j):
            return (t + j) // TB

        @block.tensor
        def _(pe):
            pe.wait_ge(consts_in, 16 * 9)
            pe.wait_ge(ctx_in, 16)

            def kv(l):
                K, W = KV[l], attn_w[l]
                pe.wait_ge(attn_in[l], 16 * (4, 6)[l])
                for b in range(B):
                    for c in range(KC):
                        mm = pe.matmul(bank[2 + b][0:S2, 0:D], ctxT[:, c, b * S2:(b + 1) * S2], W["Wv"][:, c, :],
                                       start=(c == 0), stop=(c == KC - 1))
                    mm.then_inc(K["v_mm"], 1)
                for m in range(KC):
                    for c in range(KC):
                        mm = pe.matmul(bank[m][:, 0:B * S2], W["Wk"][:, c, m * P:(m + 1) * P], ctxT[:, c, :],
                                       start=(c == 0), stop=(c == KC - 1))
                    mm.then_inc(K["k_mm"], 1)
            kv(0)
            phase_barrier(pe, 1)

            def attention(l):
                T, W = AT, attn_w[l]
                if l == 0:
                    pe.wait_ge(q_zero, 1)
                else:
                    pe.wait_ge(bo_in, 16)

                def step(t):
                    n = t + NT * l
                    if on(t, 2):
                        u = par(2)
                        pe.wait_ge(T["xn"], n + 3)
                        for c in range(KC):
                            mm = pe.transpose(bank[4][:, c * P:(c + 1) * P], xn[u][:, c * P:(c + 1) * P], ident[:, :])
                        mm.then_inc(T["xt_mm"], 1)
                    if on(t, -1):
                        pe.wait_ge(T["ot"], n)
                        for c in range(KC):
                            mm = pe.matmul(bank[7][:, 0:D], oT[:, c, :], W["Wo"][:, c, :], start=(c == 0),
                                           stop=(c == KC - 1 and l == 0))
                        if l == 1:
                            mm = pe.matmul(bank[7][:, 0:D], ones_row[:, :], bo_row[0:1, :], start=False, stop=True)
                        mm.then_inc(T["wo_mm"], 1)
                    if on(t, 0):
                        u = par(0)
                        pe.wait_ge(T["p"], n + 1)
                        for g in range(2):
                            need(pe, T["pt"], 3 * n - g)
                            for c in range(4 * g, 4 * g + 4):
                                mm = pe.transpose(bank[5 + g][:, (c % 4) * P:(c % 4 + 1) * P],
                                                  sc[u][:, c * P:(c + 1) * P], ident[:, :])
                            mm.then_inc(T["pt_mm"], 1)
                    if on(t, 2):
                        pe.wait_ge(T["xt"], n + 3)
                        for m in range(KC):
                            for c in range(KC):
                                mm = pe.matmul(bank[4][:, m * P:(m + 1) * P], W["Wq"][:, c, m * P:(m + 1) * P],
                                               xT[:, c, :], start=(c == 0), stop=(c == KC - 1))
                        mm.then_inc(T["q_mm"], 1)
                    if on(t, 0):
                        pe.wait_ge(T["pt"], 3 * n + 1)
                        pe.transpose(bank[5][:, 0:P], sc[u][:, 8 * P:9 * P], ident[:, :])
                        pe.transpose(bank[5][0:LASTROWS, P:2 * P], sc[u][:, 9 * P:9 * P + LASTROWS],
                                     ident[:, :]).then_inc(T["pt_mm"], 1)
                        need(pe, T["x"], n)
                        for c in range(PC):
                            if c in (0, 4, 8):
                                pe.wait_ge(T["pt"], 3 * n + c // 4 + 1)
                            rows = P if c < PC - 1 else LASTROWS
                            cols = 3 * VC if c < PC - 1 else 2 * VC
                            mm = pe.matmul(bank[7][:, HEAD0[c] * VC:HEAD0[c] * VC + cols], pT[0:rows, c, :],
                                           vbd[l][0:rows, bass.ds(batch(t, 0) * PC + c, 1), 0:cols].rearrange(
                                               "p a n -> p (a n)"),
                                           start=(c == 0), stop=(c == PC - 1), skip_group_check=True)
                        mm.then_inc(T["pv_mm"], 1)
                    if on(t, 2):
                        for g in range(NG):
                            pe.wait_ge(T["q"], n + 3)
                            if g % 2 == 0:
                                need(pe, T["copied"], 2 * n + 3 + g // 2)
                            c, half = g // 2, g % 2
                            mm = pe.matmul(bank[g][:, 0:HG * S2], qz[:, c, half, :],
                                           kbd[l][:, bass.ds(batch(t, 2) * KC + c, 1)].rearrange(
                                               "p a h k -> p (a h k)"), start=True, stop=True)
                            if half:
                                mm.then_inc(T["sc_mm"], 1)
                    if on(t, 0):
                        pe.wait_ge(T["on"], n + 1)
                        for c in range(KC):
                            mm = pe.transpose(bank[7][:, c * P:(c + 1) * P], o_sb[:, c * P:(c + 1) * P], ident[:, :])
                        mm.then_inc(T["ot_mm"], 1)
                attention_steps(pe, step)

            attention(0)
            pe.wait_ge(AT["copied"], 2 * NT)
            kv(1)
            phase_barrier(pe, 2)

            def route(l):
                R, RL, ne = RT, RTL[l], (E0, E1)[l]
                pe.wait_ge(route_in[l], 32)
                if l == 0:
                    pe.wait_ge(shared_in, 32)

                def step(t):
                    n = t + NT * l
                    u = par(0)
                    v = 1 - u
                    if on(t, 1):
                        pe.wait_ge(R["xn"], n + 2)
                        for c in range(KC):
                            mm = pe.transpose(bank[4][:, c * P:(c + 1) * P], xn[v][:, c * P:(c + 1) * P], ident[:, :])
                        mm.then_inc(R["xt_mm"], 1)
                        pe.wait_ge(R["xt"], n + 2)
                        if l == 0:
                            need(pe, R["h"], n)
                            for a in range(2):
                                for c in range(KC):
                                    mm = pe.matmul(bank[2 * v + a][:, :], xT[:, c, :],
                                                   sgu_w[:, c, a * FS:(a + 1) * FS],
                                                   start=(c == 0), stop=(c == KC - 1))
                            mm.then_inc(R["g_mm"], 1)
                    if on(t, 0):
                        pe.wait_ge(R["chosen"], n + 1)
                        pe.matmul(bank[7][:, 0:ne], tri[:, :], chosen[:, 0:ne], start=True, stop=False)
                        pe.wait_ge(RL["before"], t + 1)
                        pe.matmul(bank[7][:, 0:ne], ones16[:, :], chosen_before[:, bass.ds(t * E0, ne)],
                                  start=False, stop=True).then_inc(R["rk_mm"], 1)
                        if l == 0:
                            pe.wait_ge(R["h"], n + 1)
                            need(pe, R["ht"], n)
                            for c in range(FS // P):
                                mm = pe.transpose(bank[5][:, c * P:(c + 1) * P], hs[u][:, c * P:(c + 1) * P],
                                                  ident[:, :])
                            mm.then_inc(R["ht_mm"], 1)
                    if on(t, 1):
                        need(pe, R["ohr"], n + 1)
                        pe.wait_ge(R["xt"], n + 2)
                        for c in range(KC):
                            pe.matmul(bank[7][:, 0:ne], xT[:, c, :], rw[l][:, c, :], start=(c == 0), stop=False)
                        for a in range(1 + l):
                            mm = pe.matmul(bank[7][:, 0:ne], ones_row[:, :], rb[l][:, a, :], start=False,
                                           stop=(a == l))
                        mm.then_inc(R["lg_mm"], 1)
                    if l == 0 and on(t, 0):
                        pe.wait_ge(R["ht"], n + 1)
                        need(pe, R["x"], n)
                        for c in range(FS // P):
                            mm = pe.matmul(bank[6][:, 0:D], hsT[:, c, :], sdown_w[:, c, :], start=(c == 0),
                                           stop=(c == FS // P - 1))
                        mm.then_inc(R["dn_mm"], 1)
                route_steps(pe, step)
                pe.wait_ge(RL["before"], NT + 1)
                pe.wait_ge(R["ohr"], NT * (l + 1))
                pe.matmul(bank[7][:, 0:ne], ones16[:, :], chosen_before[:, NT * E0:NT * E0 + ne], start=True,
                          stop=True).then_inc(RL["c_mm"], 1)

            route(0)
            phase_barrier(pe, 3)
            X0 = EX[0]
            pe.wait_ge(experts0_in, 16 * 12)

            def experts0(s):
                u = par(0)
                v = 1 - u
                if on(s, 3, TILES0):
                    pe.wait_ge(X0["gath"][par(3, 4)], landed(s + 3, 4))
                    need(pe, X0["xt"], s + 2)
                    for c in range(KC):
                        mm = pe.transpose(bank[v][:, c * P:(c + 1) * P], xg0[par(3, 4)][:, c * P:(c + 1) * P],
                                          ident[:, :])
                    mm.then_inc(X0["xt_mm"], 1)
                if on(s, 1, TILES0):
                    pe.wait_ge(X0["h"], s + 2)
                    need(pe, X0["ht"], s)
                    pe.transpose(bank[4 + v][:, 0:P], h0[v], ident[:, :]).then_inc(X0["ht_mm"], 1)
                if on(s, 2, TILES0):
                    e = pe.value_load(plan_e[0:1, bass.ds(s + 2, 1)], min_val=0, max_val=E0 - 1)
                    pe.wait_ge(X0["xt"], s + 3)
                    need(pe, X0["h"], s + 1)
                    for c in range(KC):
                        mm = pe.matmul(bank[2 + u][:, 0:2 * F0], xgT0[u][:, c, :],
                                       gu_w[:, c, bass.ds(e, 1), :].rearrange("p a n -> p (a n)"),
                                       start=(c == 0), stop=(c == KC - 1))
                    mm.then_inc(X0["h_mm"], 1)
                if on(s, 0, TILES0):
                    e = pe.value_load(plan_e[0:1, bass.ds(s, 1)], min_val=0, max_val=E0 - 1)
                    pe.wait_ge(X0["ht"], s + 1)
                    need(pe, X0["y"], s - 1)
                    pe.matmul(bank[6 + u][:, 0:D], hT0[u], down_w[:, bass.ds(e, 1), :].rearrange("p a n -> p (a n)"),
                              start=True, stop=True).then_inc(X0["dn_mm"], 1)
            experts0_steps(pe, experts0)
            phase_barrier(pe, 4)
            attention(1)
            phase_barrier(pe, 5)
            route(1)
            phase_barrier(pe, 6)
            X1 = EX[1]
            pe.wait_ge(w1_in, 16 * (E1 // 2) * KC)
            pe.wait_ge(w2_in, 16 * (E1 // 2))

            def experts1(s):
                u = par(0)
                v = 1 - u
                if on(s, 2, TILES1):
                    pe.wait_ge(X1["gath"][u], landed(s + 2, 2))
                    need(pe, X1["xt"], s + 2)
                    for c in range(KC):
                        mm = pe.transpose(bank[0][:, c * P:(c + 1) * P], xg1[u][:, c * P:(c + 1) * P], ident[:, :])
                    mm.then_inc(X1["xt_mm"], 1)
                if on(s, 1, TILES1):
                    e = pe.value_load(plan_e[0:1, bass.ds(s + 1, 1)], min_val=0, max_val=E1 - 1)
                    pe.wait_ge(X1["xt"], s + 2)
                    need(pe, X1["h"], 2 * s)
                    for a in range(2):
                        for c in range(KC):
                            mm = pe.matmul(bank[1 + 2 * v + a][:, :], xgT1[v][:, c, :],
                                           w1_w[:, c, bass.ds(e, 1), a * 512:(a + 1) * 512].rearrange(
                                               "p a n -> p (a n)"),
                                           start=(c == 0), stop=(c == KC - 1))
                        mm.then_inc(X1["h_mm"], 1)
                if on(s, 0, TILES1):
                    for g in range(2):
                        pe.wait_ge(X1["h"], 2 * s + g + 1)
                        need(pe, X1["ht"], 2 * s + g - 1)
                        for c in range(4 * g, 4 * g + 4):
                            mm = pe.transpose(bank[5 + g][:, (c % 4) * P:(c % 4 + 1) * P],
                                              h1[u][:, c * P:(c + 1) * P], ident[:, :])
                        mm.then_inc(X1["ht_mm"], 1)
                    e = pe.value_load(plan_e[0:1, bass.ds(s, 1)], min_val=0, max_val=E1 - 1)
                    need(pe, X1["y"], s)
                    for c in range(FC1):
                        if c % 4 == 0:
                            pe.wait_ge(X1["ht"], 2 * s + c // 4 + 1)
                        mm = pe.matmul(bank[7][:, 0:D], hT1[:, c, :],
                                       w2_w[:, bass.ds(e, 1), c, :].rearrange("p a n -> p (a n)"),
                                       start=(c == 0), stop=(c == FC1 - 1))
                    mm.then_inc(X1["dn_mm"], 1)
            experts1_steps(pe, experts1)
            phase_barrier(pe, 7)

        @block.vector
        def _(dve):
            def tile_in_batch(t, j):
                return (t + j) % TB

            def column(i, v, l):
                c = dve.value_load(plan_c[0:1, bass.ds(i, 1)], min_val=0, max_val=COLS0 + TILES0 - 1)
                dve.tensor_copy(idx[v][:, :], table[:, bass.ds(c, 1)]).then_inc(EX[l]["idx"], 1)

            def layer_stats(R, n, u, src):
                dve.bn_stats(stat[:, u, :], src).then_inc(R["stats"], 1)
                wait_apart(dve, R["stats"], 2 * n + 1)
                dve.bn_aggr(mv[:, u, :], stat[:, u, :]).then_inc(R["stats"], 1)
                dve.wait_ge(R["stats"], 2 * n + 2)
                dve.tensor_scalar(ve[:, u:u + 1], mv[:, u, 1:2], EPS, None, ALU.add).then_inc(R["ve"], 1)

            def layer_norm(R, t, n, u):
                dve.wait_ge(R["rstd"], n + 1)
                dve.tensor_scalar(xn[u][:, :], x[:, bass.ds(t, 1), :].rearrange("p a n -> p (a n)"),
                                  mv[:, u, 0:1], rstd[:, u:u + 1], ALU.subtract, ALU.mult).then_inc(R["xn"], 1)

            def kv(l):
                K = KV[l]
                dve.memset(vf, 0.0).then_inc(K["vf_zero"], 1)
                if l == 1:
                    dve.wait_ge(attn_in[1], 16 * 6)
                    dve.tensor_scalar(bq4[:, :], bqk[:, 0, :], DH ** -0.5, None, ALU.mult).then_inc(K["bq"], 1)
                    for b in range(B):
                        dve.wait_ge(K["v_mm"], b + 1)
                        dve.tensor_tensor(v_sb[0:S2, b, :], bank[2 + b][0:S2, 0:D], bv_b[0:S2, :],
                                          ALU.add).then_inc(K["v_sb"], 1)
                dve.wait_ge(consts_in, 16 * 9)
                for m in range(KC):
                    dve.wait_ge(K["k_mm"], m + 1)
                    if m:
                        dve.wait_ge(K["k_bd"], B * m)
                    dve.tensor_scalar(k_sb, bank[m][:, 0:B * S2], bqk[:, 1, m:m + 1] if l else 0.0, None,
                                      ALU.add).then_inc(K["k_sb"], 1)
                    dve.wait_ge(K["k_sb"], m + 1)
                    for b in range(B):
                        dve.tensor_tensor(kbd[l][:, b * KC + m],
                                          k_sb[:, b * S2:(b + 1) * S2].unsqueeze(1).to_broadcast([P, HG, S2]),
                                          mask_k[:, :].unsqueeze(2).to_broadcast([P, HG, S2]),
                                          ALU.mult).then_inc(K["k_bd"], 1)

            def values(l):
                K = KV[l]
                if l == 1:
                    dve.wait_ge(bias_in[1], 16)
                    dve.tensor_scalar(bias[1], bias[1].bitcast(I32), 0.0, MASKED, ALU.is_equal,
                                      ALU.mult).then_inc(K["mask"], 1)
                dve.wait_ge(K["v_back"], 16 * 2 * B)
                for b in range(B):
                    for c in range(PC):
                        i = b * PC + c
                        v4 = vbd[l][:, i, :].rearrange("p (j d) -> p j d", j=3)
                        dve.tensor_tensor(v4[:, :, 0:DH], vf[:, i:i + 1, :].to_broadcast([P, 3, DH]),
                                          mask_v[:, c, :].unsqueeze(2).to_broadcast([P, 3, DH]), ALU.mult)
                        dve.tensor_copy(v4[:, :, DH:DH + 1], mask_v[:, c, :].unsqueeze(2)).then_inc(K["v_bd"], 1)
            kv(0)
            values(0)
            phase_barrier(dve, 1)

            def attention(l):
                T, TL = AT, ATL[l]
                if l == 0:
                    dve.wait_ge(x_in, 16)
                dve.wait_ge(bias_in[l], 16)

                def step(t):
                    n = t + NT * l
                    if on(t, -1):
                        dve.wait_ge(T["wo_mm"], n)
                        dve.tensor_tensor(x[:, bass.ds(t - 1, 1), :].rearrange("p a n -> p (a n)"),
                                          bank[7][:, 0:D], x[:, bass.ds(t - 1, 1), :].rearrange("p a n -> p (a n)"),
                                          ALU.add).then_inc(T["x"], 1)
                    if on(t, 4):
                        xt_ = x[:, bass.ds(t + 4, 1), :].rearrange("p a n -> p (a n)")
                        if l == 1:
                            u = par(4)
                            dve.wait_ge(TL["gath"][u], landed(t + 4, 2, TOPK))
                            for j in range(TOPK):
                                s = TL["x_comb"] if j == TOPK - 1 else TL["summing"]
                                if j:
                                    dve.wait_ge(TL["summing"], 3 * (t + 4) + j)
                                dve.scalar_tensor_tensor(
                                    out=xt_, in0=yg[:, u * TOPK + j, :], scalar=wgt[:, bass.ds((t + 4) * TOPK + j, 1)],
                                    in1=xt_, op0=ALU.mult, op1=ALU.add).then_inc(s, 1)
                            wait_apart(dve, TL["x_comb"], t + 5)
                        layer_stats(T, n + 4, par(4), xt_)
                    if on(t, 3):
                        u = par(3)
                        need(dve, T["xt_mm"], n + 2)
                        layer_norm(T, t + 3, n + 3, u)
                    if on(t, 0):
                        dve.wait_ge(T["pv_mm"], n + 1)
                        o3 = bank[7][:, 0:H * VC].rearrange("p (h d) -> p h d", h=H)
                        dve.reciprocal(rs[:, :].unsqueeze(2), o3[:, :, DH:DH + 1]).then_inc(T["rs"], 1)
                        dve.wait_ge(T["rs"], n + 1)
                        dve.tensor_tensor(o_sb[:, :].rearrange("p (h d) -> p h d", h=H), o3[:, :, 0:DH],
                                          rs[:, :].unsqueeze(2).to_broadcast([P, H, DH]),
                                          ALU.mult).then_inc(T["on"], 1)
                    if on(t, 2):
                        u = par(2)
                        if l == 0:
                            bt = bias[0][:, bass.ds(tile_in_batch(t, 2), 1), :]
                        else:
                            bt = bias[1][:, bass.ds(t + 2, 1), :]
                        s3 = sc[u].rearrange("p (h k) -> p h k", h=H)
                        for g in range(2):
                            dve.wait_ge(T["sc_mm"], 2 * n + 5 + g)
                            for a in range(2):
                                q = 2 * g + a
                                ins = dve.tensor_tensor(s3[:, HG * q:HG * q + HG, :],
                                                        bank[q][:, 0:HG * S2].rearrange("p (h k) -> p h k", h=HG),
                                                        bt.to_broadcast([P, HG, S2]), ALU.add)
                            ins.then_inc(T["copied"], 1)
                        for g in range(2):
                            dve.wait_ge(T["copied"], 2 * n + 5 + g)
                            dve.tensor_reduce(mx[u][:, 8 * g:8 * g + 8], s3[:, 8 * g:8 * g + 8, :], AX.X,
                                              ALU.max).then_inc(T["mx"], 1)
                attention_steps(dve, step)

            attention(0)
            kv(1)
            phase_barrier(dve, 2)

            def route(l):
                R, RL, ne, nk = RT, RTL[l], (E0, E1)[l], (TOPK, 1)[l]

                def prepare(t, u):
                    n = t + NT * l
                    xt_ = x[:, bass.ds(t, 1), :].rearrange("p a n -> p (a n)")
                    layer_stats(R, n, u, xt_)
                    need(dve, R["xt_mm"], n - 1)
                    need(dve, R["saved"][u], 16 * (n // 2))
                    layer_norm(R, t, n, u)

                def choose(t, u):
                    n = t + NT * l
                    dve.wait_ge(R["lg_mm"], n + 1)
                    if l == 0:
                        need(dve, R["ew"], n)
                    dve.tensor_copy(lg[:, 0:ne], bank[7][:, 0:ne]).then_inc(R["choosing"], 1)
                    wait_apart(dve, R["choosing"], 5 * n + 1)
                    dve.max(m8[:, :], lg[:, 0:ne]).then_inc(R["choosing"], 1)
                    wait_apart(dve, R["choosing"], 5 * n + 2)
                    if l == 0:
                        dve.tensor_scalar(nm[:, :], m8[:, 0:1], -1.0, None, ALU.mult).then_inc(R["nm"], 1)
                    dve.max_index(i8[:, :], m8[:, :], lg[:, 0:ne]).then_inc(R["choosing"], 1)
                    dve.wait_ge(R["choosing"], 5 * n + 3)
                    dve.tensor_copy(ef[:, 0:nk], i8[:, 0:nk]).then_inc(R["choosing"], 1)
                    dve.wait_ge(R["choosing"], 5 * n + 4)
                    dve.tensor_tensor(oh[:, 0:nk, 0:ne], iota_e[:, 0:ne].unsqueeze(1).to_broadcast([P, nk, ne]),
                                      ef[:, 0:nk].unsqueeze(2).to_broadcast([P, nk, ne]),
                                      ALU.is_equal).then_inc(R["choosing"], 1)
                    dve.wait_ge(R["choosing"], 5 * n + 5)
                    need(dve, R["rk_mm"], n)
                    with nc.allow_low_precision("zeros and ones, exact in bfloat16"):
                        dve.tensor_reduce(chosen[:, 0:ne], oh[:, 0:nk, 0:ne].rearrange("p j e -> p e j"), AX.X,
                                          ALU.add).then_inc(R["chosen"], 1)
                    dve.wait_ge(R["chosen"], n + 1)
                    dve.tensor_tensor(chosen_before[:, bass.ds(t * E0 + E0, ne)],
                                      chosen_before[:, bass.ds(t * E0, ne)], chosen[:, 0:ne],
                                      ALU.add).then_inc(RL["before"], 1)
                    if l == 0:
                        dve.wait_ge(R["ew"], n + 1)
                        dve.reciprocal(er[:, :], es[:, :]).then_inc(R["er"], 1)
                        dve.wait_ge(R["er"], n + 1)
                        dve.tensor_scalar(wgt[:, bass.ds(t * TOPK, TOPK)], ew[:, :], er[:, :], None,
                                          ALU.mult)

                def place(t, u):
                    n = t + NT * l
                    dve.wait_ge(R["rk_mm"], n + 1)
                    dve.tensor_tensor(ohr[:, 0:nk, 0:ne], bank[7][:, 0:ne].unsqueeze(1).to_broadcast([P, nk, ne]),
                                      oh[:, 0:nk, 0:ne], ALU.mult).then_inc(R["ohr"], 1)
                    dve.wait_ge(R["ohr"], n + 1)
                    dve.tensor_reduce(rk[:, 0:nk], ohr[:, 0:nk, 0:ne], AX.X, ALU.add).then_inc(R["placing"], 1)
                    dve.wait_ge(R["placing"], 4 * n + 1)
                    dve.scalar_tensor_tensor(out=slot[l][:, bass.ds(t * nk, nk)], in0=ef[:, 0:nk], scalar=float(N),
                                             in1=rk[:, 0:nk], op0=ALU.mult, op1=ALU.add).then_inc(R["placing"], 1)
                    dve.wait_ge(R["placing"], 4 * n + 2)
                    cols = (COLS0, COLS1)[l]
                    s_ = slot[l][:, bass.ds(t * nk, nk)]
                    dve.tensor_scalar(adr_a[:, 0:nk], s_, P - 1, cols.bit_length() - 1, ALU.bitwise_and,
                                      ALU.logical_shift_left).then_inc(R["placing"], 1)
                    dve.tensor_scalar(adr_b[:, 0:nk], s_, P.bit_length() - 1, None,
                                      ALU.logical_shift_right).then_inc(R["placing"], 1)
                    dve.wait_ge(R["placing"], 4 * n + 4)
                    need(dve, RL["scat"][u], 16 * nk * (t // 2))
                    dve.tensor_copy(tok_cur[u][:, :], tok_id[:, bass.ds(t, 1)]).then_inc(R["tok"], 1)
                    dve.wait_ge(R["tok"], n + 1)
                    dve.tensor_tensor(adr[u][:, 0:nk], adr_a[:, 0:nk], adr_b[:, 0:nk],
                                      ALU.bitwise_or).then_inc(R["adr"], 1)

                def step(t):
                    n = t + NT * l
                    u = par(0)
                    if on(t, 0):
                        choose(t, u)
                    if on(t, 2):
                        prepare(t + 2, u)
                    if l == 0 and on(t, 0):
                        dve.wait_ge(R["th"], n + 1)
                        dve.scalar_tensor_tensor(out=hs[u], in0=th, scalar=1.0, in1=bank[2 * u][:, :],
                                                 op0=ALU.add, op1=ALU.mult).then_inc(R["act"], 1)
                        dve.wait_ge(R["act"], n + 1)
                        dve.scalar_tensor_tensor(out=hs[u], in0=hs[u], scalar=0.5, in1=bank[2 * u + 1][:, :],
                                                 op0=ALU.mult, op1=ALU.mult).then_inc(R["h"], 1)
                    if on(t, 0):
                        place(t, u)
                    if l == 0 and on(t, 0):
                        dve.wait_ge(R["dn_mm"], n + 1)
                        xt_ = x[:, bass.ds(t, 1), :].rearrange("p a n -> p (a n)")
                        dve.tensor_tensor(xt_, bank[6][:, 0:D], xt_, ALU.add).then_inc(R["x"], 1)

                dve.drain().then_inc(RL["before"], 1)
                route_steps(dve, step)
                plan(l, ne)

            def plan(l, ne):
                RL, cols, tiles = RTL[l], (COLS0, COLS1)[l], (TILES0, TILES1)[l]
                if l == 1:
                    dve.tensor_copy(table[:, COLS1:COLS1 + TILES1], skip_id[:, 0:TILES1])
                dve.wait_ge(RL["c_mm"], 1)
                dve.tensor_scalar(cnt[:, 0:ne], bank[7][:, 0:ne], float(P - 1), None, ALU.add).then_inc(RL["planned"], 1)
                dve.wait_ge(RL["planned"], 1)
                dve.tensor_scalar(cnt[:, 0:ne], cnt[:, 0:ne], P.bit_length() - 1, None,
                                  ALU.logical_shift_right).then_inc(RL["planned"], 1)
                dve.wait_ge(RL["planned"], 2)
                dve.tensor_copy(cntf[:, 0:ne], cnt[:, 0:ne]).then_inc(RL["planned"], 1)
                dve.wait_ge(RL["planned"], 3)
                dve.tensor_tensor_scan(end[:, 0:ne], cntf[:, 0:ne], cntf[:, 0:ne], 0.0, ALU.add,
                                       ALU.bypass).then_inc(RL["planned"], 1)
                dve.wait_ge(RL["planned"], 4)
                g = ge_t[0:1, :, :] if l == 0 else ge1[:, :, :]
                dve.tensor_tensor(g, iota_t[:, 0:tiles].unsqueeze(2).to_broadcast([1, tiles, ne]),
                                  end[0:1, 0:ne].unsqueeze(1).to_broadcast([1, tiles, ne]),
                                  ALU.is_ge).then_inc(RL["planned"], 1)
                dve.wait_ge(RL["planned"], 5)
                dve.tensor_reduce(pe_i[:, 0:tiles], g, AX.X, ALU.add).then_inc(RL["planned"], 1)
                dve.wait_ge(RL["planned"], 6)
                dve.tensor_scalar(plan_e[:, 0:tiles], pe_i[:, 0:tiles], float(ne - 1), None,
                                  ALU.min).then_inc(RL["planned"], 1)
                dve.tensor_tensor(g, g, cntf[0:1, 0:ne].unsqueeze(1).to_broadcast([1, tiles, ne]),
                                  ALU.mult).then_inc(RL["planned"], 1)
                dve.wait_ge(RL["planned"], 8)
                dve.tensor_reduce(ps_i[:, 0:tiles], g, AX.X, ALU.add).then_inc(RL["planned"], 1)
                dve.wait_ge(RL["planned"], 9)
                dve.tensor_tensor(pj_i[:, 0:tiles], iota_t[:, 0:tiles], ps_i[:, 0:tiles],
                                  ALU.subtract).then_inc(RL["planned"], 1)
                dve.wait_ge(RL["planned"], 10)
                dve.scalar_tensor_tensor(out=plan_c[:, 0:tiles], in0=pe_i[:, 0:tiles], scalar=float(JT),
                                         in1=pj_i[:, 0:tiles], op0=ALU.mult, op1=ALU.add).then_inc(RL["planned"], 1)
                dve.wait_ge(RL["planned"], 11)
                dve.wait_ge(RL["planned"], 7)

            route(0)
            phase_barrier(dve, 3)
            X0 = EX[0]

            def rows_of_results():
                RL, e_id = RTL[0], ef_all
                dve.tensor_tensor(shift[:, :], end[:, :], cntf[:, :], ALU.subtract).then_inc(RL["shifting"], 1)
                dve.tensor_scalar(e_id[:, :], slot[0][:, :], N.bit_length() - 1, None,
                                  ALU.logical_shift_right).then_inc(RL["shifting"], 1)
                dve.wait_ge(RL["shifting"], 2)
                dve.scalar_tensor_tensor(out=shift[:, :], in0=iota_e[:, :], scalar=float(-JT), in1=shift[:, :],
                                         op0=ALU.mult, op1=ALU.add).then_inc(RL["shifting"], 1)
                dve.tensor_tensor(picked, iota_e[:, :].unsqueeze(1).to_broadcast([P, NT * TOPK, E0]),
                                  e_id[:, :].unsqueeze(2).to_broadcast([P, NT * TOPK, E0]),
                                  ALU.is_equal).then_inc(RL["shifting"], 1)
                dve.wait_ge(RL["shifting"], 4)
                dve.tensor_tensor(picked, picked, shift[:, :].unsqueeze(1).to_broadcast([P, NT * TOPK, E0]),
                                  ALU.mult).then_inc(RL["shifting"], 1)
                dve.wait_ge(RL["shifting"], 5)
                dve.tensor_reduce(shift_of[:, :], picked, AX.X, ALU.add).then_inc(RL["shifting"], 1)
                dve.wait_ge(RL["shifting"], 6)
                dve.scalar_tensor_tensor(out=slot[0][:, :], in0=shift_of[:, :], scalar=float(P), in1=slot[0][:, :],
                                         op0=ALU.mult, op1=ALU.add).then_inc(RL["shifting"], 1)

            def experts0(s):
                u = par(0)
                if isinstance(s, int) and s == -2:
                    rows_of_results()
                if on(s, 4, TILES0):
                    need(dve, X0["xt_mm"], s + 1)
                    column(s + 4, par(0, 4), 0)
                if on(s, 2, TILES0):
                    dve.wait_ge(X0["th"], s + 3)
                    dve.scalar_tensor_tensor(out=t0_[u], in0=th0[u], scalar=1.0, in1=bank[2 + u][:, 0:F0],
                                             op0=ALU.add, op1=ALU.mult).then_inc(X0["act"], 1)
                    dve.wait_ge(X0["act"], s + 3)
                    dve.scalar_tensor_tensor(out=h0[u], in0=t0_[u], scalar=0.5, in1=bank[2 + u][:, F0:2 * F0],
                                             op0=ALU.mult, op1=ALU.mult).then_inc(X0["h"], 1)
                if on(s, 0, TILES0):
                    dve.wait_ge(X0["dn_mm"], s + 1)
                    need(dve, X0["out"][u], 16 * (s // 2))
                    dve.tensor_copy(y0[u], bank[6 + u][:, 0:D]).then_inc(X0["y"], 1)
            experts0_steps(dve, experts0)
            values(1)
            phase_barrier(dve, 4)
            attention(1)
            phase_barrier(dve, 5)
            route(1)
            phase_barrier(dve, 6)
            X1 = EX[1]
            dve.wait_ge(b12_in, 32)

            def experts1(s):
                u = par(0)
                v = 1 - u
                if on(s, 3, TILES1):
                    need(dve, X1["out"][par(3, 4)], 16 * ((s + 3) // 4))
                    column(s + 3, par(3, 4), 1)
                if on(s, 1, TILES1):
                    e = dve.value_load(plan_e[0:1, bass.ds(s + 1, 1)], min_val=0, max_val=E1 - 1)
                    for a in range(2):
                        dve.wait_ge(X1["h_mm"], 2 * s + a + 3)
                        dve.tensor_tensor(h1[v][:, a * 512:(a + 1) * 512], bank[1 + 2 * v + a][:, :],
                                          b1_b[:, bass.ds(e, 1), a * 512:(a + 1) * 512].rearrange("p a n -> p (a n)"),
                                          ALU.add).then_inc(X1["h"], 1)
                if on(s, 0, TILES1):
                    e = dve.value_load(plan_e[0:1, bass.ds(s, 1)], min_val=0, max_val=E1 - 1)
                    dve.wait_ge(X1["dn_mm"], s + 1)
                    need(dve, X1["out"][par(2, 4)], landed(s - 2, 4))
                    dve.tensor_tensor(y1[u], bank[7][:, 0:D], b2_b[:, bass.ds(e, 1), :].rearrange("p a n -> p (a n)"),
                                      ALU.add).then_inc(X1["y"], 1)
                    dve.wait_ge(X1["y"], s + 1)
                    dve.wait_ge(X1["gath3"][u], landed(s, 2))
                    dve.tensor_tensor(y1[u], y1[u], x3g[u], ALU.add).then_inc(X1["y2"], 1)
            experts1_steps(dve, experts1)
            phase_barrier(dve, 7)


def constants():
    p = np.arange(P)
    f = P * np.arange(PC)[None, :] + p[:, None]
    return {
        "ident": np.eye(P, dtype=np.float32),
        "mask_k": ((p[:, None] % 64) // DH == np.arange(HG)).astype(np.float32),
        "mask_v": ((f // S2)[:, :, None] == (np.array(HEAD0)[None, :, None] + np.arange(3))).astype(np.float32)
        * (f < H * S2)[:, :, None].astype(np.float32),
        "neg_half": np.full((P, 1), -0.5, np.float32),
        "tri": (p[:, None] < p[None, :]).astype(np.float32),
        "iota_e": np.tile(np.arange(E0, dtype=np.float32), (P, 1)),
        "iota_t": np.arange(TILES0, dtype=np.float32)[None],
        "tok_id": (P * np.arange(NT)[None, :] + p[:, None]).astype(np.int32),
        "skip_id": np.tile((SKIP + p)[:, None], (1, COLS1)).astype(np.int32),
        "ones_row": np.ones((1, P), np.float32),
    }


def rows_of(a, p=P):
    return a.reshape(-1, p, *a.shape[1:]).swapaxes(0, 1)


def kernel(**inputs):
    import concourse.bacc as bacc
    from concourse.bass_utils import run_bass_kernel_spmd

    a = {k: np.asarray(v) for k, v in inputs.items()}
    arrays = dict(constants())
    arrays["x"] = rows_of(a["x"].reshape(N, D))
    arrays["ctxT"] = rows_of(a["ctx_1024"].reshape(B * S2, D).T)
    for l in range(2):
        for w in ("Wq", "Wk", "Wv", "Wo"):
            arrays[f"L{l}_{w}"] = rows_of(a[f"L{l}_xattn_{w}"].T)
    arrays["bias0"] = rows_of(a["fside_1x1xSxS2_0"].reshape(S, S2))
    arrays["mask1"] = rows_of(a["mask_BxSxS2_if1"].reshape(N, S2))
    arrays["bqk"] = np.stack([a["L1_xattn_bq"].reshape(KC, P).T, a["L1_xattn_bk"].reshape(KC, P).T], 1)
    arrays["bv"] = a["L1_xattn_bv"].reshape(1, D)
    arrays["bo"] = a["L1_xattn_bo"].reshape(1, D)
    arrays["rw0"] = rows_of(a["L0_ffn_router_w"].T)
    arrays["rb0"] = a["L0_ffn_router_bias"].reshape(1, 1, E0)
    arrays["rw1"] = rows_of(a["L1_ffn_gate_w"].T)
    arrays["rb1"] = np.stack([a["L1_ffn_gate_b"], a["L1_ffn_expert_bias"]])[None]
    arrays["gu"] = rows_of(np.concatenate([a["L0_ffn_gate_w"], a["L0_ffn_up_w"]], 1).transpose(2, 0, 1))
    arrays["down"] = a["L0_ffn_down_w"].transpose(2, 0, 1)
    arrays["sgu"] = rows_of(np.concatenate([a["L0_ffn_sgate_w"], a["L0_ffn_sup_w"]], 0).T)
    arrays["sdown"] = rows_of(a["L0_ffn_sdown_w"].T)
    arrays["w1"] = a["L1_ffn_w1"].reshape(E1, KC, P, F1).transpose(2, 1, 0, 3)
    arrays["b1"] = a["L1_ffn_b1"].reshape(1, E1, F1)
    arrays["w2"] = a["L1_ffn_w2"].reshape(E1, FC1, P, D).transpose(2, 0, 1, 3)
    arrays["b2"] = a["L1_ffn_b2"].reshape(1, E1, D)
    arrays = {k: np.ascontiguousarray(v) for k, v in arrays.items()}

    nc = bacc.Bacc("TRN2", target_bir_lowering=False, num_devices=1)
    aps = {k: nc.dram_tensor(f"in_{k}", v.shape, mybir.dt.from_np(v.dtype), kind="ExternalInput").ap()
           for k, v in arrays.items()}
    aps["out"] = nc.dram_tensor("out", (N, D), F32, kind="ExternalOutput").ap()
    build(nc, aps)
    r = run_bass_kernel_spmd(nc, [{f"in_{k}": v for k, v in arrays.items()}], core_ids=[0])
    return r.results[0]["out"].reshape(B, S, D)
```

```python
from contextlib import ExitStack

import concourse.bass as bass
import numpy as np
from concourse import mybir

F32 = mybir.dt.float32
BF16 = mybir.dt.bfloat16
I32 = mybir.dt.int32
U32 = mybir.dt.uint32
ALU = mybir.AluOpType
ACT = mybir.ActivationFunctionType
AX = mybir.AxisListType

P = 128
B, S, D = 2, 1024, 256
S2 = 77
N = B * S
NT = N // P
TB = S // P
KC = D // P
H, DH = 16, 16
HG = 4
NG = H // HG
PC = (H * S2 + P - 1) // P
LASTROWS = H * S2 - (PC - 1) * P
VC = DH + 1
E0, TOPK, F0 = 32, 4, 128
FS = 512
E1, F1 = 8, 1024
FC1 = F1 // P
JT = N // P
ROWS0, ROWS1 = E0 * JT, E1 * JT
TILES0 = (N * TOPK - E0) // P + E0 + 1
TILES1 = (N - E1) // P + E1 + 1
EPS = 1e-5
MASKED = -1e30
SKIP = 1 << 20
HEAD0 = [P * c // S2 for c in range(PC)]


def need(eng, sem, n):
    if not isinstance(n, int) or n > 0:
        eng.wait_ge(sem, n)


def landed(i, n, per=1):
    return 16 * per * (i // n + 1)


def build(nc, A):
    ctx = ExitStack()
    with ctx:
        def sb(name, shape, dt=F32):
            return ctx.enter_context(nc.sbuf_tensor(name, shape, dt))

        def sem(name):
            return ctx.enter_context(nc.semaphore(name))

        def cut(region, at, shape, dt=F32):
            n = int(np.prod(shape))
            words = n if dt in (F32, I32, U32) else (n + 1) // 2
            v = region[:, at:at + words]
            if dt != F32:
                v = v.bitcast(dt)
            if len(shape) > 1:
                names = "abcd"[:len(shape)]
                v = v.rearrange(f"p ({' '.join(names)}) -> p {' '.join(names)}",
                                **dict(zip(names, shape)))
            return v, at + words

        v_rows = [nc.dram_tensor(f"v_rows{l}", (B, H * S2, DH), F32).ap() for l in range(2)]
        table_d = [nc.dram_tensor(f"table{l}", (P * (c + 1), 1), I32).ap() for l, c in enumerate((ROWS0, ROWS1))]
        xn_d = [nc.dram_tensor(f"normed{l}", (N, D), F32).ap() for l in range(2)]
        x3_d = nc.dram_tensor("x3", (N, D), F32).ap()
        y_d = nc.dram_tensor("expert_out", (TILES0 * P, D), F32).ap()

        R1 = sb("R1", [P, KC * E0 * 2 * F0])
        R2 = sb("R2", [P, E1 * FC1 * D])
        X = sb("X", [P, NT * D])
        U = sb("U", [P, 11600])

        gu_w, _ = cut(R1, 0, (KC, E0, 2 * F0))
        w1_w, _ = cut(R1, 0, (KC, E1, F1))
        down_w, o = cut(R2, 0, (E0, D))
        sgu_w, o = cut(R2, o, (KC, 2 * FS))
        sdown_w, o = cut(R2, o, (FS // P, D))
        attn_w = [{}, {}]
        for name in ("Wq", "Wk", "Wv", "Wo"):
            attn_w[0][name], o = cut(R2, o, (KC, D))
        kbd, vbd, bias = [None, None], [None, None], [None, None]
        kbd[0], o = cut(R2, o, (B * KC, HG, S2))
        vbd[0], o = cut(R2, o, (B * PC, 3 * VC))
        bias[0], o = cut(R2, o, (TB, S2))
        assert o <= E1 * FC1 * D
        w2_w, _ = cut(R2, 0, (E1, FC1, D))
        x, _ = cut(X, 0, (NT, D))

        o = 0
        for name in ("Wq", "Wk", "Wv", "Wo"):
            attn_w[1][name], o = cut(U, o, (KC, D))
        kbd[1], o = cut(U, o, (B * KC, HG, S2))
        vbd[1], o = cut(U, o, (B * PC, 3 * VC))
        bias[1], o = cut(U, o, (NT, S2))
        temp_at = o
        sc = [None, None]
        sc[0], o = cut(U, o, (H * S2,))
        sc[1], o = cut(U, o, (H * S2,))
        pT, o = cut(U, o, (PC, P))
        yg, o = cut(U, o, (2 * TOPK, D))
        k_sb, o2 = cut(U, o - 2 * TOPK * D, (B * S2,))
        zeros, o2 = cut(U, o2, (ROWS0,), I32)
        ctxT, o2 = cut(U, o2, (KC, B * S2))
        bv_b, o2 = cut(U, o2, (D,))
        assert o2 <= o - 632
        vf, o2 = cut(U, o - 632, (B * PC, DH))
        v_sb, o2 = cut(U, o2, (B, D))
        bo_row, o3 = cut(U, o, (D,))
        assert o3 <= 11600 and o2 <= 11600
        b1_b, o = cut(U, 0, (E1, F1))
        b2_b, o = cut(U, o, (E1, D))
        x3g, y1 = [], []
        for i in range(2):
            for lst in (x3g, y1):
                v, o = cut(U, o, (D,))
                lst.append(v)
        assert o <= 11600
        hs = [None, None]
        o = temp_at
        hs[0], o = cut(U, o, (FS,))
        hs[1], o = cut(U, o, (FS,))
        th, o = cut(U, o, (FS,))
        hsT, o = cut(U, o, (FS // P, P))
        assert o <= 10690
        picked, o = cut(U, 10690 - NT * TOPK * E0, (NT * TOPK, E0))
        o = temp_at
        xg0, xgT0, h0, hT0, y0, th0, t0_ = [], [], [], [], [], [], []
        for i in range(2):
            for lst, shape in ((xg0, (D,)), (xg0, (D,)), (xgT0, (KC, P)), (h0, (F0,)), (hT0, (P,)), (y0, (D,)),
                               (th0, (F0,)), (t0_, (F0,))):
                v, o = cut(U, o, shape)
                lst.append(v)
        assert o <= 10690 - NT * TOPK * E0
        o = 0
        xg1, xgT1, h1 = [], [], []
        for i in range(2):
            for lst, shape in ((xg1, (D,)), (xgT1, (KC, P)), (h1, (F1,))):
                v, o = cut(X, o, shape)
                lst.append(v)
        hT1, o = cut(X, o, (FC1, P))
        assert o <= NT * D

        ident = sb("ident", [P, P])
        tri = sb("tri", [P, P], BF16)
        ones16 = sb("ones16", [P, P], BF16)
        ones_row = sb("ones_row", [1, P])
        iota_e = sb("iota_e", [P, E0])
        part_id = sb("part_id", [P, 1])
        tok_id = sb("tok_id", [P, NT], I32)
        skip_id = sb("skip_id", [P, ROWS1], I32)
        mask_k = sb("mask_k", [P, HG])
        mask_v = sb("mask_v", [P, PC, 3])
        neg_half = sb("neg_half", [P, 1])
        bqk = sb("bqk", [P, 2, KC])
        bq4 = sb("bq4", [P, KC])
        rw = [sb("rw0", [P, KC, E0]), sb("rw1", [P, KC, E1])]
        rb = [sb("rb0", [1, 1, E0]), sb("rb1", [1, 2, E1])]
        xn = [sb(f"xn{i}", [P, D]) for i in range(2)]
        xT = sb("xT", [P, KC, P])
        qz = sb("qz", [P, KC, 2, P])
        o_sb = sb("o_sb", [P, D])
        oT = sb("oT", [P, KC, P])
        stat = sb("stat", [P, 2, 6])
        mv = sb("mv", [P, 2, 2])
        ve = sb("ve", [P, 2])
        rstd = sb("rstd", [P, 2])
        tok_cur = [sb(f"tok_cur{i}", [P, 1], I32) for i in range(2)]
        mx = [sb(f"mx{i}", [P, H]) for i in range(2)]
        rs = sb("rs", [P, H])
        lg = sb("lg", [P, E0])
        m8 = sb("m8", [P, 8])
        i8 = sb("i8", [P, 8], U32)
        nm = sb("nm", [P, 1])
        ew = sb("ew", [P, TOPK])
        es = sb("es", [P, 1])
        er = sb("er", [P, 1])
        ef = sb("ef", [P, TOPK])
        oh = o_sb[:, 0:TOPK * E0].rearrange("p (j e) -> p j e", j=TOPK)
        ohr = oT[:, 0, 0:TOPK * E0].rearrange("p (j e) -> p j e", j=TOPK)
        chosen = sb("chosen", [P, E0], BF16)
        chosen_before = sb("chosen_before", [P, (NT + 1) * E0], BF16)
        rk = sb("rk", [P, TOPK])
        slot = sb("slot", [P, NT * TOPK], I32)
        adr = [sb(f"adr{i}", [P, TOPK], I32) for i in range(2)]
        slot_cur = [sb(f"slot_cur{i}", [P, TOPK], I32) for i in range(2)]
        wgt = sb("wgt", [P, NT * TOPK])
        ef_all = sb("ef_all", [P, NT * TOPK], I32)
        shift_of = sb("shift_of", [P, NT * TOPK])
        idx_all = sb("idx_all", [P, TILES0], I32)
        cnt = sb("cnt", [P, E0], I32)
        cntf = sb("cntf", [P, E0])
        end = sb("end", [P, E0])
        shift = sb("shift", [P, E0])
        later = sb("later", [P, E0])
        past = sb("past", [P, 1])
        tiles_past = sb("tiles_past", [P, 1])
        tile_row = sb("tile_row", [P, 1])
        tile_e = sb("tile_e", [P, 1])
        plan_row = sb("plan_row", [P, 1], I32)
        plan_e = sb("plan_e", [1, TILES0], I32)
        places = o_sb[:, P:2 * P].bitcast(I32)
        places_f = oT[:, 1, :]
        idx = [sb(f"idx{i}", [P, 1], I32) for i in range(4)]
        idx_out = [sb(f"idx_out{i}", [P, 1], I32) for i in range(4)]
        y0_more = sb("y0_more", [P, 2, D])
        y0 += [y0_more[:, 0, :], y0_more[:, 1, :]]
        xg1 += [xn[0][:, :], xn[1][:, :]]

        bank = [ctx.enter_context(nc.psum_tensor(f"bank{i}", [P, 512], F32)) for i in range(8)]

        phase_end = sem("phase_end")
        phases = [0]

        def phase_barrier(eng, k):
            eng.drain().then_inc(phase_end, 1)
            eng.wait_ge(phase_end, 5 * k)

        consts_in = sem("consts_in")
        tri_in = sem("tri_in")
        ctx_in = sem("ctx_in")
        x_in = sem("x_in")
        route_in = [sem("route0_in"), sem("route1_in")]
        attn_in = [sem("attn0_in"), sem("attn1_in")]
        bias_in = [sem("bias0_in"), sem("bias1_in")]
        shared_in = sem("shared_in")
        experts0_in = sem("experts0_in")
        w1_in = sem("w1_in")
        w2_in = sem("w2_in")
        b12_in = sem("b12_in")
        bo_in = sem("bo_in")
        q_zero = sem("q_zero")
        waited_apart = sem("waited_apart")
        zeros_set = sem("zeros_set")
        table_init = sem("table_init")

        class Sems(dict):

            def __init__(self, prefix, **turns):
                self.prefix, self.turns = prefix, turns

            def __missing__(self, name):
                n = self.turns.get(name)
                full = f"{self.prefix}_{name}"
                self[name] = [sem(f"{full}{i}") for i in range(n)] if n else sem(full)
                return self[name]

        KV = [Sems(f"kv{l}") for l in range(2)]
        AT, ATL = Sems("at"), [Sems(f"at{l}", gath=2) for l in range(2)]
        RT, RTL = Sems("rt", saved=2), [Sems(f"rt{l}", scat=2) for l in range(2)]
        EX = [Sems("ex0", gath=4, out=4), Sems("ex1", gath=4, gath3=2, out=4)]

        block = ctx.enter_context(nc.Block())

        place = [0]

        def steps(eng, step, first, lo, hi, last, unroll):
            assert lo % unroll == 0 and (hi - lo) % unroll == 0
            for t in range(first, lo):
                place[0] = t % unroll
                step(t)
            with eng.Fori(0, (hi - lo) // unroll) as k:
                for u in range(unroll):
                    place[0] = u
                    step(unroll * k + (lo + u))
            for t in range(hi, last + 1):
                place[0] = t % unroll
                step(t)

        def par(j, n=2):
            return (place[0] + j) % n

        def attention_steps(eng, step):
            steps(eng, step, -5, 2, 10, NT, 2)

        def route_steps(eng, step):
            steps(eng, step, -2, 2, NT - 2, NT - 1, 2)

        def experts0_steps(eng, step):
            steps(eng, step, -6, 4, TILES0 - 8, TILES0 - 1, 4)

        def experts1_steps(eng, step):
            steps(eng, step, -5, 4, TILES1 - 8, TILES1 - 1, 4)

        def load_expert(eng, regs, i, v, ne):
            eng.reg_load(regs[v], plan_e[0:1, bass.ds(i, 1)])
            return expert(eng, regs, v, ne)

        def expert(eng, regs, v, ne):
            return eng.snap(regs[v], min_val=0, max_val=ne - 1)

        def wait_apart(eng, sem, n):
            eng.wait_ge(sem, n)
            if not isinstance(n, int):
                eng.sem_inc(waited_apart, 1)

        def on(t, j, tiles=NT):
            return not isinstance(t, int) or 0 <= t + j < tiles

        def kv_values(sp, l):
            for b in range(B):
                sp.wait_ge(KV[l]["v_sb"], b + 1)
                sp.dma_start(v_rows[l][b].rearrange("(h k) d -> k h d", h=H),
                             v_sb[0:S2, b, :].rearrange("k (h d) -> k h d", h=H)).then_inc(KV[l]["v_out"], 16)
            sp.wait_ge(KV[l]["v_out"], 16 * B)
            sp.wait_ge(KV[l]["vf_zero"], 1)
            for b in range(B):
                full = (PC - 1) * P
                sp.dma_start(vf[:, b * PC:(b + 1) * PC - 1, :],
                             v_rows[l][b, 0:full].rearrange("(c p) d -> p c d", p=P)).then_inc(KV[l]["v_back"], 16)
                sp.dma_start(vf[0:LASTROWS, (b + 1) * PC - 1, :],
                             v_rows[l][b, full:H * S2]).then_inc(KV[l]["v_back"], 16)

        def route_stores(sp, l):
            R, RL = RT, RTL[l]
            with sp.Fori(0, NT // 2) as k:
                for u in range(2):
                    t = 2 * k + u
                    n = t + NT * l
                    sp.wait_ge(R["xn"], n + 1)
                    sp.dma_start(xn_d[l][bass.ds(t * P, P), :], xn[u][:, :]).then_inc(R["saved"][u], 16)
            if l == 1:
                sp.dma_start(x3_d.rearrange("(t p) d -> p t d", p=P), x).then_inc(RL["x_saved"], 16)
                sp.wait_ge(RL["x_saved"], 16)
            for u in range(2):
                sp.wait_ge(R["saved"][u], 16 * NT // 2 * (l + 1))

        @block.sync
        def _(sp):
            for name, dst in (("ident", ident), ("mask_k", mask_k), ("mask_v", mask_v), ("neg_half", neg_half),
                              ("tri", None), ("iota_e", iota_e), ("part_id", part_id), ("tok_id", tok_id),
                              ("skip_id", skip_id), ("ones_row", ones_row)):
                if dst is not None:
                    sp.dma_start(dst[tuple(slice(None) for _ in dst.shape)], A[name]).then_inc(consts_in, 16)
            sp.dma_start(ctxT, A["ctxT"]).then_inc(ctx_in, 16)
            for name in ("Wk", "Wv", "Wq", "Wo"):
                sp.dma_start(attn_w[0][name], A[f"L0_{name}"]).then_inc(attn_in[0], 16)
            sp.dma_start(bias[0], A["bias0"]).then_inc(bias_in[0], 16)
            sp.dma_start(rw[0][:, :, :], A["rw0"]).then_inc(route_in[0], 16)
            sp.dma_start(rb[0][:, :, :], A["rb0"]).then_inc(route_in[0], 16)
            sp.wait_ge(zeros_set, 1)
            sp.dma_start(table_d[0][0:ROWS0 * P].rearrange("(p c) a -> p (c a)", p=P), zeros).then_inc(table_init, 16)
            sp.dma_start(table_d[0][ROWS0 * P:].rearrange("c a -> a c"), zeros[0:1, 0:P]).then_inc(table_init, 16)
            sp.wait_ge(consts_in, 16 * 9)
            sp.dma_start(table_d[1][0:ROWS1 * P].rearrange("(p c) a -> p (c a)", p=P),
                         skip_id[:, :]).then_inc(table_init, 16)
            sp.dma_start(table_d[1][ROWS1 * P:].rearrange("c a -> a c"), skip_id[0:1, :]).then_inc(table_init, 16)
            kv_values(sp, 0)
            sp.dma_start(sgu_w, A["sgu"]).then_inc(shared_in, 16)
            sp.dma_start(sdown_w, A["sdown"]).then_inc(shared_in, 16)
            for e in range(0, E0, 4):
                sp.dma_start(gu_w[:, :, e:e + 4, :], A["gu"][:, :, e:e + 4, :]).then_inc(experts0_in, 16)
            for e in range(0, E0, 8):
                sp.dma_start(down_w[:, e:e + 8, :], A["down"][:, e:e + 8, :]).then_inc(experts0_in, 16)
            for name in ("Wk", "Wv", "Wq", "Wo"):
                sp.dma_start(attn_w[1][name], A[f"L1_{name}"]).then_inc(attn_in[1], 16)
            sp.dma_start(bqk[:, :, :], A["bqk"]).then_inc(attn_in[1], 16)
            sp.dma_start(bv_b[0:S2, :], A["bv"].partition_broadcast(S2)).then_inc(attn_in[1], 16)
            sp.dma_start(bias[1].bitcast(I32), A["mask1"]).then_inc(bias_in[1], 16)
            sp.dma_start(rw[1][:, :, :], A["rw1"]).then_inc(route_in[1], 16)
            sp.dma_start(rb[1][:, :, :], A["rb1"]).then_inc(route_in[1], 16)
            phase_barrier(sp, 1)
            phase_barrier(sp, 2)
            kv_values(sp, 1)
            sp.dma_start(bo_row[0:1, :], A["bo"]).then_inc(bo_in, 16)
            route_stores(sp, 0)
            phase_barrier(sp, 3)
            with sp.Fori(0, TILES0 // 4) as k:
                for u in range(4):
                    i = 4 * k + u
                    sp.wait_ge(EX[0]["y"], i + 1)
                    sp.dma_start(y_d[bass.ds(i * P, P), :], y0[u]).then_inc(EX[0]["out"][u], 16)
            for u in range(4):
                sp.wait_ge(EX[0]["out"][u], 16 * TILES0 // 4)
            phase_barrier(sp, 4)
            for e in range(0, E1, 2):
                for c in range(KC):
                    sp.dma_start(w1_w[:, c, e:e + 2, :], A["w1"][:, c, e:e + 2, :]).then_inc(w1_in, 16)
            for e in range(0, E1, 2):
                sp.dma_start(w2_w[:, e:e + 2], A["w2"][:, e:e + 2]).then_inc(w2_in, 16)
            phase_barrier(sp, 5)
            sp.dma_start(b1_b, A["b1"].partition_broadcast(P)).then_inc(b12_in, 16)
            sp.dma_start(b2_b, A["b2"].partition_broadcast(P)).then_inc(b12_in, 16)
            route_stores(sp, 1)
            phase_barrier(sp, 6)
            phase_barrier(sp, 7)

        def routing(pool, l):
            R, RL, k_ = RT, RTL[l], (TOPK, 1)[l]
            pool.wait_ge(table_init, 64)

            def step(t):
                n = t + NT * l
                u = par(0)
                if on(t, 2):
                    pool.wait_ge(R["ve"], n + 3)
                    pool.tensor_tensor(rstd[:, u:u + 1], ve[:, u:u + 1], neg_half[:, :],
                                       ALU.pow).then_inc(R["rstd"], 1)
                if on(t, 0):
                    wait_apart(pool, R["adr"], n + 1)
                    for j in range(k_):
                        pool.indirect_dma_start(
                            table_d[l], bass.IndirectOffsetOnAxis(adr[u][:, j:j + 1], 0),
                            tok_cur[u][:, :], None).then_inc(RL["scat"][u], 16)
            route_steps(pool, step)
            for u in range(2):
                pool.wait_ge(RL["scat"][u], 16 * NT // 2 * k_)
            pool.wait_ge(RL["planned"], 8)
            tiles = (TILES0, TILES1)[l]
            pool.indirect_dma_start(places[0:tiles, :], None, table_d[l].rearrange("(r p) a -> r (p a)", p=P),
                                    bass.IndirectOffsetOnAxis(plan_row[0:tiles, :], 0)).then_inc(RL["table"], 16)

        @block.gpsimd
        def _(pool):
            pool.memset(zeros, 0).then_inc(zeros_set, 1)
            pool.memset(qz[:, :, :, :], 0.0).then_inc(q_zero, 1)
            pool.memset(ones16[:, :], 1.0)
            pool.memset(chosen_before[:, 0:E0], 0.0)
            pool.dma_start(o_sb[:, 0:P], A["tri"]).then_inc(tri_in, 16)
            pool.wait_ge(tri_in, 16)
            nc.gpsimd.tensor_copy(tri[:, :], o_sb[:, 0:P])
            phase_barrier(pool, 1)

            def attention(l):
                T, TL = AT, ATL[l]

                def step(t):
                    n = t + NT * l
                    if l == 1 and on(t, 5):
                        u = par(5)
                        need(pool, TL["x_comb"], t + 4)
                        pool.tensor_copy(slot_cur[u][:, :], slot[:, bass.ds((t + 5) * TOPK, TOPK)]).then_inc(
                            TL["slots"], 1)
                        wait_apart(pool, TL["slots"], t + 6)
                        for j in range(TOPK):
                            pool.indirect_dma_start(
                                yg[:, u * TOPK + j, :], None, y_d,
                                bass.IndirectOffsetOnAxis(slot_cur[u][:, j:j + 1], 0)).then_inc(TL["gath"][u], 16)
                    if on(t, 4):
                        pool.wait_ge(T["ve"], n + 5)
                        u = par(4)
                        pool.tensor_tensor(rstd[:, u:u + 1], ve[:, u:u + 1], neg_half[:, :], ALU.pow).then_inc(T["rstd"], 1)
                    if on(t, 2):
                        u = par(2)
                        pool.wait_ge(T["mx"], 2 * n + 6)
                        s3 = sc[u].rearrange("p (h k) -> p h k", h=H)
                        pool.tensor_tensor(s3, s3, mx[u][:, :].unsqueeze(2).to_broadcast([P, H, S2]),
                                           ALU.subtract).then_inc(T["sub"], 1)
                attention_steps(pool, step)

            attention(0)
            phase_barrier(pool, 2)
            routing(pool, 0)
            phase_barrier(pool, 3)
            with pool.Fori(0, TILES0 // 4) as k:
                for u in range(4):
                    i = 4 * k + u
                    wait_apart(pool, EX[0]["idx"], i + 1)
                    pool.indirect_dma_start(xg0[u], None, xn_d[0],
                                            bass.IndirectOffsetOnAxis(idx[u][:, :], 0)).then_inc(EX[0]["gath"][u], 16)
            phase_barrier(pool, 4)
            attention(1)
            phase_barrier(pool, 5)
            routing(pool, 1)
            phase_barrier(pool, 6)
            X1, last_row = EX[1], pool.snap(N - 1)

            def gather(dst, src, at, landed_on):
                pool.indirect_dma_start(dst, None, src, bass.IndirectOffsetOnAxis(at[:, :], 0),
                                        bounds_check=last_row, oob_is_err=False).then_inc(landed_on, 16)

            def rows(i, v):
                wait_apart(pool, X1["idx"], i + 1)
                gather(xg1[v], xn_d[1], idx[v], X1["gath"][v])

            def residual(i, u, v):
                wait_apart(pool, X1["idx_out"], i + 1)
                if not isinstance(i, int) or i > 1:
                    wait_apart(pool, X1["y2"], i - 1)
                gather(x3g[u], x3_d, idx_out[v], X1["gath3"][u])

            def results(i, u, v):
                wait_apart(pool, X1["y2"], i + 1)
                pool.indirect_dma_start(A["out"], bass.IndirectOffsetOnAxis(idx_out[v][:, :], 0), y1[u], None,
                                        bounds_check=last_row, oob_is_err=False).then_inc(X1["out"][v], 16)

            def step(s):
                if on(s, 5, TILES1):
                    rows(s + 5, par(5, 4))
                if on(s, 1, TILES1):
                    residual(s + 1, par(1), par(1, 4))
                if on(s, 0, TILES1):
                    results(s, par(0), par(0, 4))
            experts1_steps(pool, step)
            for v in range(4):
                pool.wait_ge(X1["out"][v], 16 * TILES1 // 4)
            phase_barrier(pool, 7)

        @block.scalar
        def _(act):
            act.dma_start(x, A["x"]).then_inc(x_in, 16)

            def kv(l):
                K = KV[l]
                for b in range(B):
                    act.wait_ge(K["v_mm"], b + 1)
                    if l == 0:
                        act.activation(v_sb[0:S2, b, :], bank[2 + b][0:S2, 0:D], ACT.Copy).then_inc(K["v_sb"], 1)
            kv(0)
            phase_barrier(act, 1)

            def attention(l):
                T, TL = AT, ATL[l]

                def step(t):
                    n = t + NT * l
                    if on(t, 2):
                        act.wait_ge(T["xt_mm"], n + 3)
                        act.activation(xT[:, :, :].rearrange("p c n -> p (c n)"), bank[4][:, 0:D],
                                       ACT.Copy).then_inc(T["xt"], 1)
                    if on(t, 0):
                        for g in range(2):
                            act.wait_ge(T["pt_mm"], 3 * n + g + 1)
                            if g == 0:
                                need(act, T["pv_mm"], n)
                            act.activation(pT[:, 4 * g:4 * g + 4, :].rearrange("p c n -> p (c n)"), bank[5 + g][:, :],
                                           ACT.Copy).then_inc(T["pt"], 1)
                    if on(t, 2):
                        act.wait_ge(T["q_mm"], n + 3)
                        for half in range(2):
                            r = slice(64 * half, 64 * half + 64)
                            if l == 0:
                                ins = act.activation(qz[r, :, half, :],
                                                     bank[4][r, 0:D].rearrange("p (c n) -> p c n", c=KC),
                                                     ACT.Copy, scale=DH ** -0.5)
                            else:
                                for c in range(KC):
                                    ins = act.activation(qz[r, c, half, :], bank[4][r, c * P:(c + 1) * P],
                                                         ACT.Identity, bias=bq4[r, c:c + 1], scale=DH ** -0.5)
                        ins.then_inc(T["q"], 1)
                    if on(t, 0):
                        act.wait_ge(T["pt_mm"], 3 * n + 3)
                        act.activation(pT[:, 8, :], bank[5][:, 0:P], ACT.Copy)
                        act.activation(pT[0:LASTROWS, 9, :], bank[5][0:LASTROWS, P:2 * P],
                                       ACT.Copy).then_inc(T["pt"], 1)
                    if on(t, 1):
                        u = par(1)
                        act.wait_ge(T["sub"], n + 2)
                        act.activation(sc[u], sc[u], ACT.Exp).then_inc(T["p"], 1)
                    if on(t, 0):
                        act.wait_ge(T["ot_mm"], n + 1)
                        act.activation(oT[:, :, :].rearrange("p c n -> p (c n)"), bank[7][:, 0:D],
                                       ACT.Copy).then_inc(T["ot"], 1)
                attention_steps(act, step)

            attention(0)
            phase_barrier(act, 2)

            def route(l):
                R, RL = RT, RTL[l]

                def step(t):
                    n = t + NT * l
                    u = par(0)
                    if on(t, 1):
                        act.wait_ge(R["xt_mm"], n + 2)
                        act.activation(xT[:, :, :].rearrange("p c n -> p (c n)"), bank[4][:, 0:D],
                                       ACT.Copy).then_inc(R["xt"], 1)
                    if l == 0 and on(t, 0):
                        act.wait_ge(R["nm"], n + 1)
                        act.activation(ew[:, :], m8[:, 0:TOPK], ACT.Exp, bias=nm[:, :],
                                       accum_out=es[:, :]).then_inc(R["ew"], 1)
                        act.wait_ge(R["g_mm"], n + 1)
                        need(act, R["act"], n)
                        act.activation(th, bank[2 * u][:, :], ACT.Tanh, scale=0.5).then_inc(R["th"], 1)
                        act.wait_ge(R["ht_mm"], n + 1)
                        act.activation(hsT.rearrange("p c n -> p (c n)"), bank[5][:, :],
                                       ACT.Copy).then_inc(R["ht"], 1)
                route_steps(act, step)

            route(0)
            phase_barrier(act, 3)
            X0 = EX[0]

            def experts0(s):
                u = par(0)
                if on(s, 3, TILES0):
                    act.wait_ge(X0["xt_mm"], s + 4)
                    act.activation(xgT0[(u + 1) % 2].rearrange("p c n -> p (c n)"), bank[(u + 1) % 2][:, 0:D],
                                   ACT.Copy).then_inc(X0["xt"], 1)
                if on(s, 1, TILES0):
                    act.wait_ge(X0["ht_mm"], s + 2)
                    act.activation(hT0[(u + 1) % 2], bank[4 + (u + 1) % 2][:, 0:P], ACT.Copy).then_inc(X0["ht"], 1)
                if on(s, 2, TILES0):
                    act.wait_ge(X0["h_mm"], s + 3)
                    act.activation(th0[u], bank[2 + u][:, 0:F0], ACT.Tanh, scale=0.5).then_inc(X0["th"], 1)
            experts0_steps(act, experts0)
            phase_barrier(act, 4)
            attention(1)
            phase_barrier(act, 5)
            route(1)
            phase_barrier(act, 6)
            X1 = EX[1]

            def experts1(s):
                u = par(0)
                if on(s, 0, TILES1):
                    for g in range(2):
                        act.wait_ge(X1["ht_mm"], 2 * s + g + 1)
                        if g == 0:
                            need(act, X1["dn_mm"], s)
                        act.activation(hT1[:, 4 * g:4 * g + 4, :].rearrange("p c n -> p (c n)"), bank[5 + g][:, :],
                                       ACT.Relu).then_inc(X1["ht"], 1)
                if on(s, 2, TILES1):
                    act.wait_ge(X1["xt_mm"], s + 3)
                    act.activation(xgT1[u].rearrange("p c n -> p (c n)"), bank[0][:, 0:D],
                                   ACT.Copy).then_inc(X1["xt"], 1)
            experts1_steps(act, experts1)
            phase_barrier(act, 7)

        def batch(t, j):
            return (t + j) // TB

        @block.tensor
        def _(pe):
            pe.wait_ge(consts_in, 16 * 9)
            pe.wait_ge(ctx_in, 16)

            def kv(l):
                K, W = KV[l], attn_w[l]
                pe.wait_ge(attn_in[l], 16 * (4, 6)[l])
                for b in range(B):
                    for c in range(KC):
                        mm = pe.matmul(bank[2 + b][0:S2, 0:D], ctxT[:, c, b * S2:(b + 1) * S2], W["Wv"][:, c, :],
                                       start=(c == 0), stop=(c == KC - 1))
                    mm.then_inc(K["v_mm"], 1)
                for m in range(KC):
                    for c in range(KC):
                        mm = pe.matmul(bank[m][:, 0:B * S2], W["Wk"][:, c, m * P:(m + 1) * P], ctxT[:, c, :],
                                       start=(c == 0), stop=(c == KC - 1))
                    mm.then_inc(K["k_mm"], 1)
            kv(0)
            phase_barrier(pe, 1)

            def attention(l):
                T, W = AT, attn_w[l]
                if l == 0:
                    pe.wait_ge(q_zero, 1)
                else:
                    pe.wait_ge(bo_in, 16)

                def step(t):
                    n = t + NT * l
                    if on(t, 2):
                        u = par(2)
                        pe.wait_ge(T["xn"], n + 3)
                        for c in range(KC):
                            mm = pe.transpose(bank[4][:, c * P:(c + 1) * P], xn[u][:, c * P:(c + 1) * P], ident[:, :])
                        mm.then_inc(T["xt_mm"], 1)
                    if on(t, -1):
                        pe.wait_ge(T["ot"], n)
                        for c in range(KC):
                            mm = pe.matmul(bank[7][:, 0:D], oT[:, c, :], W["Wo"][:, c, :], start=(c == 0),
                                           stop=(c == KC - 1 and l == 0))
                        if l == 1:
                            mm = pe.matmul(bank[7][:, 0:D], ones_row[:, :], bo_row[0:1, :], start=False, stop=True)
                        mm.then_inc(T["wo_mm"], 1)
                    if on(t, 0):
                        u = par(0)
                        pe.wait_ge(T["p"], n + 1)
                        for g in range(2):
                            need(pe, T["pt"], 3 * n - g)
                            for c in range(4 * g, 4 * g + 4):
                                mm = pe.transpose(bank[5 + g][:, (c % 4) * P:(c % 4 + 1) * P],
                                                  sc[u][:, c * P:(c + 1) * P], ident[:, :])
                            mm.then_inc(T["pt_mm"], 1)
                    if on(t, 2):
                        pe.wait_ge(T["xt"], n + 3)
                        for m in range(KC):
                            for c in range(KC):
                                mm = pe.matmul(bank[4][:, m * P:(m + 1) * P], W["Wq"][:, c, m * P:(m + 1) * P],
                                               xT[:, c, :], start=(c == 0), stop=(c == KC - 1))
                        mm.then_inc(T["q_mm"], 1)
                    if on(t, 0):
                        pe.wait_ge(T["pt"], 3 * n + 1)
                        pe.transpose(bank[5][:, 0:P], sc[u][:, 8 * P:9 * P], ident[:, :])
                        pe.transpose(bank[5][0:LASTROWS, P:2 * P], sc[u][:, 9 * P:9 * P + LASTROWS],
                                     ident[:, :]).then_inc(T["pt_mm"], 1)
                        need(pe, T["x"], n)
                        for c in range(PC):
                            if c in (0, 4, 8):
                                pe.wait_ge(T["pt"], 3 * n + c // 4 + 1)
                            rows = P if c < PC - 1 else LASTROWS
                            cols = 3 * VC if c < PC - 1 else 2 * VC
                            mm = pe.matmul(bank[7][:, HEAD0[c] * VC:HEAD0[c] * VC + cols], pT[0:rows, c, :],
                                           vbd[l][0:rows, bass.ds(batch(t, 0) * PC + c, 1), 0:cols].rearrange(
                                               "p a n -> p (a n)"),
                                           start=(c == 0), stop=(c == PC - 1), skip_group_check=True)
                        mm.then_inc(T["pv_mm"], 1)
                    if on(t, 2):
                        for g in range(NG):
                            pe.wait_ge(T["q"], n + 3)
                            if g % 2 == 0:
                                need(pe, T["copied"], 2 * n + 3 + g // 2)
                            c, half = g // 2, g % 2
                            mm = pe.matmul(bank[g][:, 0:HG * S2], qz[:, c, half, :],
                                           kbd[l][:, bass.ds(batch(t, 2) * KC + c, 1)].rearrange(
                                               "p a h k -> p (a h k)"), start=True, stop=True)
                            if half:
                                mm.then_inc(T["sc_mm"], 1)
                    if on(t, 0):
                        pe.wait_ge(T["on"], n + 1)
                        for c in range(KC):
                            mm = pe.transpose(bank[7][:, c * P:(c + 1) * P], o_sb[:, c * P:(c + 1) * P], ident[:, :])
                        mm.then_inc(T["ot_mm"], 1)
                attention_steps(pe, step)

            attention(0)
            pe.wait_ge(AT["copied"], 2 * NT)
            kv(1)
            phase_barrier(pe, 2)

            def route(l):
                R, RL, ne = RT, RTL[l], (E0, E1)[l]
                pe.wait_ge(route_in[l], 32)
                if l == 0:
                    pe.wait_ge(shared_in, 32)

                def step(t):
                    n = t + NT * l
                    u = par(0)
                    v = 1 - u
                    if on(t, 1):
                        pe.wait_ge(R["xn"], n + 2)
                        for c in range(KC):
                            mm = pe.transpose(bank[4][:, c * P:(c + 1) * P], xn[v][:, c * P:(c + 1) * P], ident[:, :])
                        mm.then_inc(R["xt_mm"], 1)
                        pe.wait_ge(R["xt"], n + 2)
                        if l == 0:
                            need(pe, R["h"], n)
                            for a in range(2):
                                for c in range(KC):
                                    mm = pe.matmul(bank[2 * v + a][:, :], xT[:, c, :],
                                                   sgu_w[:, c, a * FS:(a + 1) * FS],
                                                   start=(c == 0), stop=(c == KC - 1))
                            mm.then_inc(R["g_mm"], 1)
                    if on(t, 0):
                        pe.wait_ge(R["chosen"], n + 1)
                        pe.matmul(bank[7][:, 0:ne], tri[:, :], chosen[:, 0:ne], start=True, stop=False)
                        pe.wait_ge(RL["before"], t + 1)
                        pe.matmul(bank[7][:, 0:ne], ones16[:, :], chosen_before[:, bass.ds(t * E0, ne)],
                                  start=False, stop=True).then_inc(R["rk_mm"], 1)
                        if l == 0:
                            pe.wait_ge(R["h"], n + 1)
                            need(pe, R["ht"], n)
                            for c in range(FS // P):
                                mm = pe.transpose(bank[5][:, c * P:(c + 1) * P], hs[u][:, c * P:(c + 1) * P],
                                                  ident[:, :])
                            mm.then_inc(R["ht_mm"], 1)
                    if on(t, 1):
                        need(pe, R["ohr"], n + 1)
                        pe.wait_ge(R["xt"], n + 2)
                        for c in range(KC):
                            pe.matmul(bank[7][:, 0:ne], xT[:, c, :], rw[l][:, c, :], start=(c == 0), stop=False)
                        for a in range(1 + l):
                            mm = pe.matmul(bank[7][:, 0:ne], ones_row[:, :], rb[l][:, a, :], start=False,
                                           stop=(a == l))
                        mm.then_inc(R["lg_mm"], 1)
                    if l == 0 and on(t, 0):
                        pe.wait_ge(R["ht"], n + 1)
                        need(pe, R["x"], n)
                        for c in range(FS // P):
                            mm = pe.matmul(bank[6][:, 0:D], hsT[:, c, :], sdown_w[:, c, :], start=(c == 0),
                                           stop=(c == FS // P - 1))
                        mm.then_inc(R["dn_mm"], 1)
                route_steps(pe, step)
                pe.wait_ge(RL["before"], NT + 1)
                pe.wait_ge(R["ohr"], NT * (l + 1))
                pe.matmul(bank[7][:, 0:ne], ones16[:, :], chosen_before[:, NT * E0:NT * E0 + ne], start=True,
                          stop=True).then_inc(RL["c_mm"], 1)
                tiles = (TILES0, TILES1)[l]
                pe.wait_ge(RL["planned"], 8)
                pe.transpose(bank[6][0:1, 0:tiles], tile_e[0:tiles, :], ident[0:tiles, 0:tiles]).then_inc(
                    RL["turned"], 1)
                pe.wait_ge(RL["places"], 1)
                pe.transpose(bank[5][:, 0:tiles], places_f[0:tiles, :], ident[0:tiles, 0:tiles]).then_inc(
                    RL["turned"], 1)

            route(0)
            phase_barrier(pe, 3)
            X0 = EX[0]
            pe.wait_ge(experts0_in, 16 * 12)
            pe_experts = [pe.alloc_register(f"pe_expert{i}") for i in range(4)]

            def experts0(s):
                u = par(0)
                v = 1 - u
                if on(s, 3, TILES0):
                    pe.wait_ge(X0["gath"][par(3, 4)], landed(s + 3, 4))
                    need(pe, X0["xt"], s + 2)
                    for c in range(KC):
                        mm = pe.transpose(bank[v][:, c * P:(c + 1) * P], xg0[par(3, 4)][:, c * P:(c + 1) * P],
                                          ident[:, :])
                    mm.then_inc(X0["xt_mm"], 1)
                if on(s, 2, TILES0):
                    e = load_expert(pe, pe_experts, s + 2, par(2, 4), E0)
                    pe.wait_ge(X0["xt"], s + 3)
                    need(pe, X0["h"], s + 1)
                    for c in range(KC):
                        mm = pe.matmul(bank[2 + u][:, 0:2 * F0], xgT0[u][:, c, :],
                                       gu_w[:, c, bass.ds(e, 1), :].rearrange("p a n -> p (a n)"),
                                       start=(c == 0), stop=(c == KC - 1))
                    mm.then_inc(X0["h_mm"], 1)
                if on(s, 1, TILES0):
                    pe.wait_ge(X0["h"], s + 2)
                    need(pe, X0["ht"], s)
                    pe.transpose(bank[4 + v][:, 0:P], h0[v], ident[:, :]).then_inc(X0["ht_mm"], 1)
                if on(s, 0, TILES0):
                    e = expert(pe, pe_experts, par(0, 4), E0)
                    pe.wait_ge(X0["ht"], s + 1)
                    need(pe, X0["y"], s - 1)
                    pe.matmul(bank[6 + u][:, 0:D], hT0[u], down_w[:, bass.ds(e, 1), :].rearrange("p a n -> p (a n)"),
                              start=True, stop=True).then_inc(X0["dn_mm"], 1)
            experts0_steps(pe, experts0)
            phase_barrier(pe, 4)
            attention(1)
            phase_barrier(pe, 5)
            route(1)
            phase_barrier(pe, 6)
            X1 = EX[1]
            pe.wait_ge(w1_in, 16 * (E1 // 2) * KC)
            pe.wait_ge(w2_in, 16 * (E1 // 2))

            def experts1(s):
                u = par(0)
                v = 1 - u
                if on(s, 0, TILES1):
                    for g in range(2):
                        pe.wait_ge(X1["h"], 2 * s + g + 1)
                        need(pe, X1["ht"], 2 * s + g - 1)
                        for c in range(4 * g, 4 * g + 4):
                            mm = pe.transpose(bank[5 + g][:, (c % 4) * P:(c % 4 + 1) * P],
                                              h1[u][:, c * P:(c + 1) * P], ident[:, :])
                        mm.then_inc(X1["ht_mm"], 1)
                if on(s, 2, TILES1):
                    pe.wait_ge(X1["gath"][par(2, 4)], landed(s + 2, 4))
                    need(pe, X1["xt"], s + 2)
                    for c in range(KC):
                        mm = pe.transpose(bank[0][:, c * P:(c + 1) * P], xg1[par(2, 4)][:, c * P:(c + 1) * P],
                                          ident[:, :])
                    mm.then_inc(X1["xt_mm"], 1)
                if on(s, 1, TILES1):
                    e = load_expert(pe, pe_experts, s + 1, par(1, 4), E1)
                    pe.wait_ge(X1["xt"], s + 2)
                    need(pe, X1["h"], 2 * s)
                    for a in range(2):
                        for c in range(KC):
                            mm = pe.matmul(bank[1 + 2 * v + a][:, :], xgT1[v][:, c, :],
                                           w1_w[:, c, bass.ds(e, 1), a * 512:(a + 1) * 512].rearrange(
                                               "p a n -> p (a n)"),
                                           start=(c == 0), stop=(c == KC - 1))
                        mm.then_inc(X1["h_mm"], 1)
                if on(s, 0, TILES1):
                    e = expert(pe, pe_experts, par(0, 4), E1)
                    need(pe, X1["y"], s)
                    for c in range(FC1):
                        if c % 4 == 0:
                            pe.wait_ge(X1["ht"], 2 * s + c // 4 + 1)
                        mm = pe.matmul(bank[7][:, 0:D], hT1[:, c, :],
                                       w2_w[:, bass.ds(e, 1), c, :].rearrange("p a n -> p (a n)"),
                                       start=(c == 0), stop=(c == FC1 - 1))
                    mm.then_inc(X1["dn_mm"], 1)
            experts1_steps(pe, experts1)
            phase_barrier(pe, 7)

        @block.vector
        def _(dve):
            def tile_in_batch(t, j):
                return (t + j) % TB

            def column(dst, i, copied):
                dve.tensor_copy(dst[:, :], idx_all[:, bass.ds(i, 1)]).then_inc(copied, 1)

            def layer_stats(R, n, u, src):
                dve.bn_stats(stat[:, u, :], src).then_inc(R["stats"], 1)
                wait_apart(dve, R["stats"], 2 * n + 1)
                dve.bn_aggr(mv[:, u, :], stat[:, u, :]).then_inc(R["stats"], 1)
                dve.wait_ge(R["stats"], 2 * n + 2)
                dve.tensor_scalar(ve[:, u:u + 1], mv[:, u, 1:2], EPS, None, ALU.add).then_inc(R["ve"], 1)

            def layer_norm(R, t, n, u):
                dve.wait_ge(R["rstd"], n + 1)
                dve.tensor_scalar(xn[u][:, :], x[:, bass.ds(t, 1), :].rearrange("p a n -> p (a n)"),
                                  mv[:, u, 0:1], rstd[:, u:u + 1], ALU.subtract, ALU.mult).then_inc(R["xn"], 1)

            def kv(l):
                K = KV[l]
                dve.memset(vf, 0.0).then_inc(K["vf_zero"], 1)
                if l == 1:
                    dve.wait_ge(attn_in[1], 16 * 6)
                    dve.tensor_scalar(bq4[:, :], bqk[:, 0, :], DH ** -0.5, None, ALU.mult).then_inc(K["bq"], 1)
                    for b in range(B):
                        dve.wait_ge(K["v_mm"], b + 1)
                        dve.tensor_tensor(v_sb[0:S2, b, :], bank[2 + b][0:S2, 0:D], bv_b[0:S2, :],
                                          ALU.add).then_inc(K["v_sb"], 1)
                dve.wait_ge(consts_in, 16 * 9)
                for m in range(KC):
                    dve.wait_ge(K["k_mm"], m + 1)
                    if m:
                        dve.wait_ge(K["k_bd"], B * m)
                    dve.tensor_scalar(k_sb, bank[m][:, 0:B * S2], bqk[:, 1, m:m + 1] if l else 0.0, None,
                                      ALU.add).then_inc(K["k_sb"], 1)
                    dve.wait_ge(K["k_sb"], m + 1)
                    for b in range(B):
                        dve.tensor_tensor(kbd[l][:, b * KC + m],
                                          k_sb[:, b * S2:(b + 1) * S2].unsqueeze(1).to_broadcast([P, HG, S2]),
                                          mask_k[:, :].unsqueeze(2).to_broadcast([P, HG, S2]),
                                          ALU.mult).then_inc(K["k_bd"], 1)

            def values(l):
                K = KV[l]
                if l == 1:
                    dve.wait_ge(bias_in[1], 16)
                    dve.tensor_scalar(bias[1], bias[1].bitcast(I32), 0.0, MASKED, ALU.is_equal,
                                      ALU.mult).then_inc(K["mask"], 1)
                dve.wait_ge(K["v_back"], 16 * 2 * B)
                for b in range(B):
                    for c in range(PC):
                        i = b * PC + c
                        v4 = vbd[l][:, i, :].rearrange("p (j d) -> p j d", j=3)
                        dve.tensor_tensor(v4[:, :, 0:DH], vf[:, i:i + 1, :].to_broadcast([P, 3, DH]),
                                          mask_v[:, c, :].unsqueeze(2).to_broadcast([P, 3, DH]), ALU.mult)
                        dve.tensor_copy(v4[:, :, DH:DH + 1], mask_v[:, c, :].unsqueeze(2)).then_inc(K["v_bd"], 1)
            kv(0)
            values(0)
            phase_barrier(dve, 1)

            def attention(l):
                T, TL = AT, ATL[l]
                if l == 0:
                    dve.wait_ge(x_in, 16)
                dve.wait_ge(bias_in[l], 16)

                def step(t):
                    n = t + NT * l
                    if on(t, -1):
                        dve.wait_ge(T["wo_mm"], n)
                        dve.tensor_tensor(x[:, bass.ds(t - 1, 1), :].rearrange("p a n -> p (a n)"),
                                          bank[7][:, 0:D], x[:, bass.ds(t - 1, 1), :].rearrange("p a n -> p (a n)"),
                                          ALU.add).then_inc(T["x"], 1)
                    if on(t, 4):
                        xt_ = x[:, bass.ds(t + 4, 1), :].rearrange("p a n -> p (a n)")
                        if l == 1:
                            u = par(4)
                            dve.wait_ge(TL["gath"][u], landed(t + 4, 2, TOPK))
                            for j in range(TOPK):
                                s = TL["x_comb"] if j == TOPK - 1 else TL["summing"]
                                if j:
                                    dve.wait_ge(TL["summing"], 3 * (t + 4) + j)
                                dve.scalar_tensor_tensor(
                                    out=xt_, in0=yg[:, u * TOPK + j, :], scalar=wgt[:, bass.ds((t + 4) * TOPK + j, 1)],
                                    in1=xt_, op0=ALU.mult, op1=ALU.add).then_inc(s, 1)
                            wait_apart(dve, TL["x_comb"], t + 5)
                        layer_stats(T, n + 4, par(4), xt_)
                    if on(t, 3):
                        u = par(3)
                        need(dve, T["xt_mm"], n + 2)
                        layer_norm(T, t + 3, n + 3, u)
                    if on(t, 0):
                        dve.wait_ge(T["pv_mm"], n + 1)
                        o3 = bank[7][:, 0:H * VC].rearrange("p (h d) -> p h d", h=H)
                        dve.reciprocal(rs[:, :].unsqueeze(2), o3[:, :, DH:DH + 1]).then_inc(T["rs"], 1)
                        dve.wait_ge(T["rs"], n + 1)
                        dve.tensor_tensor(o_sb[:, :].rearrange("p (h d) -> p h d", h=H), o3[:, :, 0:DH],
                                          rs[:, :].unsqueeze(2).to_broadcast([P, H, DH]),
                                          ALU.mult).then_inc(T["on"], 1)
                    if on(t, 2):
                        u = par(2)
                        if l == 0:
                            bt = bias[0][:, bass.ds(tile_in_batch(t, 2), 1), :]
                        else:
                            bt = bias[1][:, bass.ds(t + 2, 1), :]
                        s3 = sc[u].rearrange("p (h k) -> p h k", h=H)
                        for g in range(2):
                            dve.wait_ge(T["sc_mm"], 2 * n + 5 + g)
                            for a in range(2):
                                q = 2 * g + a
                                ins = dve.tensor_tensor(s3[:, HG * q:HG * q + HG, :],
                                                        bank[q][:, 0:HG * S2].rearrange("p (h k) -> p h k", h=HG),
                                                        bt.to_broadcast([P, HG, S2]), ALU.add)
                            ins.then_inc(T["copied"], 1)
                        for g in range(2):
                            dve.wait_ge(T["copied"], 2 * n + 5 + g)
                            dve.tensor_reduce(mx[u][:, 8 * g:8 * g + 8], s3[:, 8 * g:8 * g + 8, :], AX.X,
                                              ALU.max).then_inc(T["mx"], 1)
                attention_steps(dve, step)

            attention(0)
            kv(1)
            phase_barrier(dve, 2)

            def route(l):
                R, RL, ne, nk = RT, RTL[l], (E0, E1)[l], (TOPK, 1)[l]

                def prepare(t, u):
                    n = t + NT * l
                    xt_ = x[:, bass.ds(t, 1), :].rearrange("p a n -> p (a n)")
                    layer_stats(R, n, u, xt_)
                    need(dve, R["xt_mm"], n - 1)
                    need(dve, R["saved"][u], 16 * (n // 2))
                    layer_norm(R, t, n, u)

                def choose(t, u):
                    n = t + NT * l
                    dve.wait_ge(R["lg_mm"], n + 1)
                    if l == 0:
                        need(dve, R["ew"], n)
                    dve.tensor_copy(lg[:, 0:ne], bank[7][:, 0:ne]).then_inc(R["choosing"], 1)
                    wait_apart(dve, R["choosing"], 5 * n + 1)
                    dve.max(m8[:, :], lg[:, 0:ne]).then_inc(R["choosing"], 1)
                    wait_apart(dve, R["choosing"], 5 * n + 2)
                    if l == 0:
                        dve.tensor_scalar(nm[:, :], m8[:, 0:1], -1.0, None, ALU.mult).then_inc(R["nm"], 1)
                    dve.max_index(i8[:, :], m8[:, :], lg[:, 0:ne]).then_inc(R["choosing"], 1)
                    dve.wait_ge(R["choosing"], 5 * n + 3)
                    dve.tensor_copy(ef[:, 0:nk], i8[:, 0:nk]).then_inc(R["choosing"], 1)
                    dve.wait_ge(R["choosing"], 5 * n + 4)
                    dve.tensor_tensor(oh[:, 0:nk, 0:ne], iota_e[:, 0:ne].unsqueeze(1).to_broadcast([P, nk, ne]),
                                      ef[:, 0:nk].unsqueeze(2).to_broadcast([P, nk, ne]),
                                      ALU.is_equal).then_inc(R["choosing"], 1)
                    dve.wait_ge(R["choosing"], 5 * n + 5)
                    need(dve, R["rk_mm"], n)
                    with nc.allow_low_precision("zeros and ones, exact in bfloat16"):
                        dve.tensor_reduce(chosen[:, 0:ne], oh[:, 0:nk, 0:ne].rearrange("p j e -> p e j"), AX.X,
                                          ALU.add).then_inc(R["chosen"], 1)
                    dve.wait_ge(R["chosen"], n + 1)
                    dve.tensor_tensor(chosen_before[:, bass.ds(t * E0 + E0, ne)],
                                      chosen_before[:, bass.ds(t * E0, ne)], chosen[:, 0:ne],
                                      ALU.add).then_inc(RL["before"], 1)
                    if l == 0:
                        dve.wait_ge(R["ew"], n + 1)
                        dve.reciprocal(er[:, :], es[:, :]).then_inc(R["er"], 1)
                        dve.wait_ge(R["er"], n + 1)
                        dve.tensor_scalar(wgt[:, bass.ds(t * TOPK, TOPK)], ew[:, :], er[:, :], None,
                                          ALU.mult)

                def place(t, u):
                    n = t + NT * l
                    dve.wait_ge(R["rk_mm"], n + 1)
                    dve.tensor_tensor(ohr[:, 0:nk, 0:ne], bank[7][:, 0:ne].unsqueeze(1).to_broadcast([P, nk, ne]),
                                      oh[:, 0:nk, 0:ne], ALU.mult).then_inc(R["ohr"], 1)
                    dve.wait_ge(R["ohr"], n + 1)
                    dve.tensor_reduce(rk[:, 0:nk], ohr[:, 0:nk, 0:ne], AX.X, ALU.add).then_inc(R["placing"], 1)
                    dve.wait_ge(R["placing"], n + 1)
                    need(dve, RL["scat"][u], 16 * nk * (t // 2))
                    dve.tensor_copy(tok_cur[u][:, :], tok_id[:, bass.ds(t, 1)]).then_inc(R["tok"], 1)
                    dve.wait_ge(R["tok"], n + 1)
                    dve.scalar_tensor_tensor(out=adr[u][:, 0:nk], in0=ef[:, 0:nk], scalar=float(N),
                                             in1=rk[:, 0:nk], op0=ALU.mult, op1=ALU.add).then_inc(R["adr"], 1)
                    if l == 0:
                        dve.wait_ge(R["adr"], n + 1)
                        dve.tensor_copy(slot[:, bass.ds(t * nk, nk)], adr[u][:, 0:nk])

                def step(t):
                    n = t + NT * l
                    u = par(0)
                    if on(t, 0):
                        choose(t, u)
                    if on(t, 2):
                        prepare(t + 2, u)
                    if l == 0 and on(t, 0):
                        dve.wait_ge(R["th"], n + 1)
                        dve.scalar_tensor_tensor(out=hs[u], in0=th, scalar=1.0, in1=bank[2 * u][:, :],
                                                 op0=ALU.add, op1=ALU.mult).then_inc(R["act"], 1)
                        dve.wait_ge(R["act"], n + 1)
                        dve.scalar_tensor_tensor(out=hs[u], in0=hs[u], scalar=0.5, in1=bank[2 * u + 1][:, :],
                                                 op0=ALU.mult, op1=ALU.mult).then_inc(R["h"], 1)
                    if on(t, 0):
                        place(t, u)
                    if l == 0 and on(t, 0):
                        dve.wait_ge(R["dn_mm"], n + 1)
                        xt_ = x[:, bass.ds(t, 1), :].rearrange("p a n -> p (a n)")
                        dve.tensor_tensor(xt_, bank[6][:, 0:D], xt_, ALU.add).then_inc(R["x"], 1)

                dve.drain().then_inc(RL["before"], 1)
                route_steps(dve, step)
                plan(l, ne)

            def plan(l, ne):
                RL, rows, tiles = RTL[l], (ROWS0, ROWS1)[l], (TILES0, TILES1)[l]
                RL_ = RL["planned"]
                dve.wait_ge(RL["c_mm"], 1)
                dve.tensor_scalar(cnt[:, 0:ne], bank[7][:, 0:ne], float(P - 1), None, ALU.add).then_inc(RL_, 1)
                dve.wait_ge(RL_, 1)
                dve.tensor_scalar(cnt[:, 0:ne], cnt[:, 0:ne], P.bit_length() - 1, None,
                                  ALU.logical_shift_right).then_inc(RL_, 1)
                dve.wait_ge(RL_, 2)
                dve.tensor_copy(cntf[:, 0:ne], cnt[:, 0:ne]).then_inc(RL_, 1)
                dve.wait_ge(RL_, 3)
                dve.tensor_tensor_scan(end[:, 0:ne], cntf[:, 0:ne], cntf[:, 0:ne], 0.0, ALU.add,
                                       ALU.bypass).then_inc(RL_, 1)
                dve.wait_ge(RL_, 4)
                dve.tensor_tensor(later[:, 0:ne], part_id[:, :].to_broadcast([P, ne]), end[:, 0:ne],
                                  ALU.is_ge).then_inc(RL_, 1)
                dve.wait_ge(RL_, 5)
                dve.tensor_reduce(past[:, :], later[:, 0:ne], AX.X, ALU.add).then_inc(RL["past"], 1)
                dve.tensor_tensor(later[:, 0:ne], later[:, 0:ne], cntf[:, 0:ne], ALU.mult).then_inc(RL["past"], 1)
                dve.wait_ge(RL["past"], 2)
                dve.tensor_reduce(tiles_past[:, :], later[:, 0:ne], AX.X, ALU.add).then_inc(RL["past"], 1)
                dve.tensor_scalar(tile_e[:, :], past[:, :], float(ne - 1), None, ALU.min).then_inc(RL_, 1)
                dve.wait_ge(RL["past"], 3)
                dve.tensor_tensor(tiles_past[:, :], part_id[:, :], tiles_past[:, :], ALU.subtract).then_inc(RL["past"], 1)
                dve.wait_ge(RL["past"], 4)
                dve.scalar_tensor_tensor(out=tile_row[:, :], in0=past[:, :], scalar=float(JT),
                                         in1=tiles_past[:, :], op0=ALU.mult, op1=ALU.add).then_inc(RL_, 1)
                dve.wait_ge(RL_, 7)
                dve.tensor_scalar(plan_row[:, :], tile_row[:, :], float(rows), None, ALU.min).then_inc(RL_, 1)
                dve.wait_ge(RL["turned"], 1)
                dve.tensor_copy(plan_e[:, 0:tiles], bank[6][0:1, 0:tiles])
                dve.wait_ge(RL["table"], 16)
                dve.tensor_copy(places_f[0:tiles, :], places[0:tiles, :]).then_inc(RL["places"], 1)
                dve.wait_ge(RL["turned"], 2)
                dve.tensor_copy(idx_all[:, 0:tiles], bank[5][:, 0:tiles])

            route(0)
            phase_barrier(dve, 3)
            X0 = EX[0]

            def rows_of_results():
                RL, e_id = RTL[0], ef_all
                dve.tensor_tensor(shift[:, :], end[:, :], cntf[:, :], ALU.subtract).then_inc(RL["shifting"], 1)
                dve.tensor_scalar(e_id[:, :], slot[:, :], N.bit_length() - 1, None,
                                  ALU.logical_shift_right).then_inc(RL["shifting"], 1)
                dve.wait_ge(RL["shifting"], 2)
                dve.scalar_tensor_tensor(out=shift[:, :], in0=iota_e[:, :], scalar=float(-JT), in1=shift[:, :],
                                         op0=ALU.mult, op1=ALU.add).then_inc(RL["shifting"], 1)
                dve.tensor_tensor(picked, iota_e[:, :].unsqueeze(1).to_broadcast([P, NT * TOPK, E0]),
                                  e_id[:, :].unsqueeze(2).to_broadcast([P, NT * TOPK, E0]),
                                  ALU.is_equal).then_inc(RL["shifting"], 1)
                dve.wait_ge(RL["shifting"], 4)
                dve.tensor_tensor(picked, picked, shift[:, :].unsqueeze(1).to_broadcast([P, NT * TOPK, E0]),
                                  ALU.mult).then_inc(RL["shifting"], 1)
                dve.wait_ge(RL["shifting"], 5)
                dve.tensor_reduce(shift_of[:, :], picked, AX.X, ALU.add).then_inc(RL["shifting"], 1)
                dve.wait_ge(RL["shifting"], 6)
                dve.scalar_tensor_tensor(out=slot[:, :], in0=shift_of[:, :], scalar=float(P), in1=slot[:, :],
                                         op0=ALU.mult, op1=ALU.add).then_inc(RL["shifting"], 1)

            def experts0(s):
                u = par(0)
                if isinstance(s, int) and s == -2:
                    rows_of_results()
                if on(s, 6, TILES0):
                    need(dve, X0["xt_mm"], s + 3)
                    column(idx[par(6, 4)], s + 6, X0["idx"])
                if on(s, 2, TILES0):
                    dve.wait_ge(X0["th"], s + 3)
                    dve.scalar_tensor_tensor(out=t0_[u], in0=th0[u], scalar=1.0, in1=bank[2 + u][:, 0:F0],
                                             op0=ALU.add, op1=ALU.mult).then_inc(X0["act"], 1)
                    dve.wait_ge(X0["act"], s + 3)
                    dve.scalar_tensor_tensor(out=h0[u], in0=t0_[u], scalar=0.5, in1=bank[2 + u][:, F0:2 * F0],
                                             op0=ALU.mult, op1=ALU.mult).then_inc(X0["h"], 1)
                if on(s, 0, TILES0):
                    dve.wait_ge(X0["dn_mm"], s + 1)
                    need(dve, X0["out"][par(0, 4)], 16 * (s // 4))
                    dve.tensor_copy(y0[par(0, 4)], bank[6 + u][:, 0:D]).then_inc(X0["y"], 1)
            experts0_steps(dve, experts0)
            values(1)
            phase_barrier(dve, 4)
            attention(1)
            phase_barrier(dve, 5)
            route(1)
            phase_barrier(dve, 6)
            X1 = EX[1]
            dve.wait_ge(b12_in, 32)
            dve_experts = [dve.alloc_register(f"dve_expert{i}") for i in range(4)]

            def experts1(s):
                u = par(0)
                v = 1 - u
                if on(s, 5, TILES1):
                    need(dve, X1["xt_mm"], s + 2)
                    column(idx[par(5, 4)], s + 5, X1["idx"])
                if on(s, 1, TILES1):
                    need(dve, X1["out"][par(1, 4)], 16 * ((s + 1) // 4))
                    column(idx_out[par(1, 4)], s + 1, X1["idx_out"])
                if on(s, 1, TILES1):
                    e = load_expert(dve, dve_experts, s + 1, par(1, 4), E1)
                    for a in range(2):
                        dve.wait_ge(X1["h_mm"], 2 * s + a + 3)
                        dve.tensor_tensor(h1[v][:, a * 512:(a + 1) * 512], bank[1 + 2 * v + a][:, :],
                                          b1_b[:, bass.ds(e, 1), a * 512:(a + 1) * 512].rearrange("p a n -> p (a n)"),
                                          ALU.add).then_inc(X1["h"], 1)
                if on(s, 0, TILES1):
                    e = expert(dve, dve_experts, par(0, 4), E1)
                    dve.wait_ge(X1["dn_mm"], s + 1)
                    need(dve, X1["out"][par(2, 4)], landed(s - 2, 4))
                    dve.tensor_tensor(y1[u], bank[7][:, 0:D], b2_b[:, bass.ds(e, 1), :].rearrange("p a n -> p (a n)"),
                                      ALU.add).then_inc(X1["y"], 1)
                    dve.wait_ge(X1["y"], s + 1)
                    dve.wait_ge(X1["gath3"][u], landed(s, 2))
                    dve.tensor_tensor(y1[u], y1[u], x3g[u], ALU.add).then_inc(X1["y2"], 1)
            experts1_steps(dve, experts1)
            phase_barrier(dve, 7)


def constants():
    p = np.arange(P)
    f = P * np.arange(PC)[None, :] + p[:, None]
    return {
        "ident": np.eye(P, dtype=np.float32),
        "mask_k": ((p[:, None] % 64) // DH == np.arange(HG)).astype(np.float32),
        "mask_v": ((f // S2)[:, :, None] == (np.array(HEAD0)[None, :, None] + np.arange(3))).astype(np.float32)
        * (f < H * S2)[:, :, None].astype(np.float32),
        "neg_half": np.full((P, 1), -0.5, np.float32),
        "tri": (p[:, None] < p[None, :]).astype(np.float32),
        "iota_e": np.tile(np.arange(E0, dtype=np.float32), (P, 1)),
        "part_id": p[:, None].astype(np.float32),
        "tok_id": (P * np.arange(NT)[None, :] + p[:, None]).astype(np.int32),
        "skip_id": np.tile((SKIP + p)[:, None], (1, ROWS1)).astype(np.int32),
        "ones_row": np.ones((1, P), np.float32),
    }


def rows_of(a, p=P):
    return a.reshape(-1, p, *a.shape[1:]).swapaxes(0, 1)


def kernel(**inputs):
    import concourse.bacc as bacc
    from concourse.bass_utils import run_bass_kernel_spmd

    a = {k: np.asarray(v) for k, v in inputs.items()}
    arrays = dict(constants())
    arrays["x"] = rows_of(a["x"].reshape(N, D))
    arrays["ctxT"] = rows_of(a["ctx_1024"].reshape(B * S2, D).T)
    for l in range(2):
        for w in ("Wq", "Wk", "Wv", "Wo"):
            arrays[f"L{l}_{w}"] = rows_of(a[f"L{l}_xattn_{w}"].T)
    arrays["bias0"] = rows_of(a["fside_1x1xSxS2_0"].reshape(S, S2))
    arrays["mask1"] = rows_of(a["mask_BxSxS2_if1"].reshape(N, S2))
    arrays["bqk"] = np.stack([a["L1_xattn_bq"].reshape(KC, P).T, a["L1_xattn_bk"].reshape(KC, P).T], 1)
    arrays["bv"] = a["L1_xattn_bv"].reshape(1, D)
    arrays["bo"] = a["L1_xattn_bo"].reshape(1, D)
    arrays["rw0"] = rows_of(a["L0_ffn_router_w"].T)
    arrays["rb0"] = a["L0_ffn_router_bias"].reshape(1, 1, E0)
    arrays["rw1"] = rows_of(a["L1_ffn_gate_w"].T)
    arrays["rb1"] = np.stack([a["L1_ffn_gate_b"], a["L1_ffn_expert_bias"]])[None]
    arrays["gu"] = rows_of(np.concatenate([a["L0_ffn_gate_w"], a["L0_ffn_up_w"]], 1).transpose(2, 0, 1))
    arrays["down"] = a["L0_ffn_down_w"].transpose(2, 0, 1)
    arrays["sgu"] = rows_of(np.concatenate([a["L0_ffn_sgate_w"], a["L0_ffn_sup_w"]], 0).T)
    arrays["sdown"] = rows_of(a["L0_ffn_sdown_w"].T)
    arrays["w1"] = a["L1_ffn_w1"].reshape(E1, KC, P, F1).transpose(2, 1, 0, 3)
    arrays["b1"] = a["L1_ffn_b1"].reshape(1, E1, F1)
    arrays["w2"] = a["L1_ffn_w2"].reshape(E1, FC1, P, D).transpose(2, 0, 1, 3)
    arrays["b2"] = a["L1_ffn_b2"].reshape(1, E1, D)
    arrays = {k: np.ascontiguousarray(v) for k, v in arrays.items()}

    nc = bacc.Bacc("TRN2", target_bir_lowering=False, num_devices=1)
    aps = {k: nc.dram_tensor(f"in_{k}", v.shape, mybir.dt.from_np(v.dtype), kind="ExternalInput").ap()
           for k, v in arrays.items()}
    aps["out"] = nc.dram_tensor("out", (N, D), F32, kind="ExternalOutput").ap()
    build(nc, aps)
    r = run_bass_kernel_spmd(nc, [{f"in_{k}": v for k, v in arrays.items()}], core_ids=[0])
    return r.results[0]["out"].reshape(B, S, D)
```

```python
from contextlib import ExitStack

import concourse.bass as bass
import numpy as np
from concourse import mybir

F32 = mybir.dt.float32
BF16 = mybir.dt.bfloat16
I32 = mybir.dt.int32
U32 = mybir.dt.uint32
ALU = mybir.AluOpType
ACT = mybir.ActivationFunctionType
AX = mybir.AxisListType

P = 128
B, S, D = 2, 1024, 256
S2 = 77
N = B * S
NT = N // P
RK = 64
FIRST = 4
TB = S // P
KC = D // P
H, DH = 16, 16
HG = 4
NG = H // HG
PC = (H * S2 + P - 1) // P
LASTROWS = H * S2 - (PC - 1) * P
VC = DH + 1
E0, TOPK, F0 = 32, 4, 128
FS = 512
EP = E0 // (NT // 2)
E1, F1 = 8, 1024
FC1 = F1 // P
JT = N // P
ROWS0, ROWS1 = E0 * JT, E1 * JT
TILES0 = (N * TOPK - E0) // P + E0
TILES1 = (N - E1) // P + E1
PLAN0, PLAN1 = -(-TILES0 // 4) * 4, -(-TILES1 // 4) * 4
EPS = 1e-5
MASKED = -1e30
SKIP = 1 << 20
HEAD0 = [P * c // S2 for c in range(PC)]
UW = 11600
PICKED_END = 10690
VF_BACK = 632


def need(eng, sem, n):
    if not isinstance(n, int) or n > 0:
        eng.wait_ge(sem, n)


def landed(i, n, per=1):
    return 16 * per * (i // n + 1)


def turns(tiles, v, n=4):
    return (tiles - v + n - 1) // n


def build(nc, A):
    ctx = ExitStack()
    with ctx:
        def sb(name, shape, dt=F32):
            return ctx.enter_context(nc.sbuf_tensor(name, shape, dt))

        def sem(name):
            return ctx.enter_context(nc.semaphore(name))

        def cut(region, at, shape, dt=F32):
            n = int(np.prod(shape))
            words = n if dt in (F32, I32, U32) else (n + 1) // 2
            v = region[:, at:at + words]
            if dt != F32:
                v = v.bitcast(dt)
            if len(shape) > 1:
                names = "abcd"[:len(shape)]
                v = v.rearrange(f"p ({' '.join(names)}) -> p {' '.join(names)}",
                                **dict(zip(names, shape)))
            return v, at + words

        v_rows = [nc.dram_tensor(f"v_rows{l}", (B, H * S2, DH), F32).ap() for l in range(2)]
        table_d = [nc.dram_tensor(f"table{l}", (P * (c + 1), 1), I32).ap() for l, c in enumerate((ROWS0, ROWS1))]
        xn_d = [nc.dram_tensor(f"normed{l}", (N, D), F32).ap() for l in range(2)]
        x3_d = nc.dram_tensor("x3", (N, D), F32).ap()
        y_d = nc.dram_tensor("expert_out", (TILES0 * P, D), F32).ap()

        R1 = sb("R1", [P, KC * E0 * 2 * F0])
        R2 = sb("R2", [P, E1 * FC1 * D])
        X = sb("X", [P, NT * D])
        U = sb("U", [P, UW])

        gu_w, _ = cut(R1, 0, (KC, E0, 2 * F0))
        w1_w, _ = cut(R1, 0, (KC, E1, F1))
        down_w, o = cut(R2, 0, (E0, D))
        sgu_w, o = cut(R2, o, (KC, 2 * FS))
        sdown_w, o = cut(R2, o, (FS // P, D))
        attn_w = [{}, {}]
        for name in ("Wq", "Wk", "Wv", "Wo"):
            attn_w[0][name], o = cut(R2, o, (KC, D))
        kbd, vbd, bias = [None, None], [None, None], [None, None]
        kbd[0], o = cut(R2, o, (B * KC, HG, S2))
        vbd[0], o = cut(R2, o, (B * PC, 3 * VC))
        bias[0], o = cut(R2, o, (TB, S2))
        assert o <= E1 * FC1 * D
        w2_w, _ = cut(R2, 0, (E1, FC1, D))
        x, _ = cut(X, 0, (NT, D))

        o = 0
        for name in ("Wq", "Wk", "Wv", "Wo"):
            attn_w[1][name], o = cut(U, o, (KC, D))
        kbd[1], o = cut(U, o, (B * KC, HG, S2))
        vbd[1], o = cut(U, o, (B * PC, 3 * VC))
        bias[1], o = cut(U, o, (NT, S2))
        temp_at = o
        sc = [None, None]
        sc[0], o = cut(U, o, (H * S2,))
        sc[1], o = cut(U, o, (H * S2,))
        pT, o = cut(U, o, (PC, P))
        yg, o = cut(U, o, (2 * TOPK, D))
        k_sb, o2 = cut(U, o - 2 * TOPK * D, (B * S2,))
        zeros, o2 = cut(U, o2, (ROWS0,), I32)
        ctxT, o2 = cut(U, o2, (KC, B * S2))
        bv_b, o2 = cut(U, o2, (D,))
        assert o2 <= o - VF_BACK
        vf, o2 = cut(U, o - VF_BACK, (B * PC, DH))
        v_sb, o2 = cut(U, o2, (B, D))
        bo_row, o3 = cut(U, o, (D,))
        assert o3 <= UW and o2 <= UW
        b2_b, o = cut(U, 0, (E1, D))
        b1_of = []
        for i in range(2):
            v, o = cut(U, o, (FC1,))
            b1_of.append(v)
        x3g, y1 = [], []
        for i in range(2):
            for lst in (x3g, y1):
                v, o = cut(U, o, (D,))
                lst.append(v)
        assert o + 2 * NT * E1 <= UW
        hs = [None, None]
        o = temp_at
        hs[0], o = cut(U, o, (FS,))
        hs[1], o = cut(U, o, (FS,))
        th, o = cut(U, o, (FS,))
        hsT, o = cut(U, o, (FS // P, P))
        assert o <= PICKED_END
        picked, o = cut(U, PICKED_END - NT * TOPK * E0, (NT * TOPK, E0))
        o = temp_at
        xg0, xgT0, h0, hT0, y0, th0, t0_ = [], [], [], [], [], [], []
        for i in range(2):
            for lst, shape in ((xgT0, (KC, P)), (h0, (F0,)), (hT0, (P,)), (y0, (D,)), (th0, (F0,)), (t0_, (F0,))):
                v, o = cut(U, o, shape)
                lst.append(v)
        o = max(o, temp_at + 4 * FS + 2 * NT)
        for i in range(4):
            v, o = cut(U, o, (D,))
            xg0.append(v)
        assert o <= PICKED_END - NT * TOPK * E0
        o = 0
        xg1, xgT1, h1 = [], [], []
        for i in range(2):
            for lst, shape in ((xg1, (D,)), (xgT1, (KC, P)), (h1, (F1,))):
                v, o = cut(X, o, shape)
                lst.append(v)
        hT1, o = cut(X, o, (FC1, P))
        assert o <= NT * D

        ident = sb("ident", [P, P])
        tri = sb("tri", [P, P], BF16)
        ones16 = sb("ones16", [P, P], BF16)
        ones_row = sb("ones_row", [1, P])
        iota_e = sb("iota_e", [P, E0])
        part_id = sb("part_id", [P, 1])
        tok_id = sb("tok_id", [P, NT], I32)
        skip_id = sb("skip_id", [P, ROWS1], I32)
        mask_k = sb("mask_k", [P, HG])
        mask_v = sb("mask_v", [P, PC, 3])
        neg_half = sb("neg_half", [P, 1])
        bqk = sb("bqk", [P, 2, KC])
        bq4 = sb("bq4", [P, KC])
        b1T = sb("b1T", [P, E1, FC1])
        rw = [sb("rw0", [P, KC, E0]), sb("rw1", [P, KC, E1])]
        rb = [sb("rb0", [P, 1, E0]), sb("rb1", [P, 2, E1])]
        xn = [sb(f"xn{i}", [P, D]) for i in range(2)]
        xr = [sb(f"xr{i}", [P, D]) for i in range(2)]
        xT = sb("xT", [P, KC, P])
        xrT = sb("xrT", [P, KC, P])
        qz = sb("qz", [P, KC, 2, P])
        o_sb = sb("o_sb", [P, D])
        oT = sb("oT", [P, KC, P])
        stat = sb("stat", [P, 4, 6])
        mv = sb("mv", [P, 4, 2])
        ve = sb("ve", [P, 4])
        rstd = sb("rstd", [P, 4])
        tok_cur = [sb(f"tok_cur{i}", [P, 1], I32) for i in range(2)]
        mx = [sb(f"mx{i}", [P, H]) for i in range(2)]
        rs = sb("rs", [P, H])
        lg = sb("lg", [P, E0])
        m8 = [sb(f"m8_{i}", [P, 8]) for i in range(2)]
        i8 = [sb(f"i8_{i}", [P, 8], U32) for i in range(2)]
        ef = sb("ef", [P, NT * TOPK])
        at_r2 = E0 * D + KC * 2 * FS + FS // P * D
        oh = cut(R2, at_r2, (NT * TOPK, E0))[0]
        ohr = cut(R2, at_r2 + NT * TOPK * E0, (NT * TOPK, E0))[0]
        last16 = UW - 2 * E1
        oh1 = [cut(U, last16 + i * E1 // 2, (E1,), BF16)[0] for i in range(2)]
        ohr1 = cut(U, last16 + E1, (E1,))[0]
        chosen = sb("chosen", [P, NT, E0], BF16)
        before1 = chosen[:, :, :].rearrange("p t e -> p (t e)")
        o = temp_at + 4 * FS
        es, o = cut(U, o, (NT,))
        er, o = cut(U, o, (NT,))
        rk = sb("rk", [P, NT * TOPK])[:, :]
        later = sb("later", [P, E0])[:, :]
        plan_cols = sb("plan_cols", [P, 3])
        past, tiles_past, tile_row = (plan_cols[:, i:i + 1] for i in range(3))
        slot = sb("slot", [P, NT * TOPK], I32)
        slot_cur = [sb(f"slot_cur{i}", [P, TOPK], I32) for i in range(2)]
        wgt = sb("wgt", [P, NT * TOPK])
        shift_of = sb("shift_of", [P, NT * TOPK])
        idx_all = sb("idx_all", [P, PLAN0], I32)
        cnt = sb("cnt", [P, E0], I32)
        cntf = sb("cntf", [P, E0])
        end = sb("end", [P, E0])
        shift = sb("shift", [P, E0])
        tile_e = sb("tile_e", [P, 1])
        plan_row = sb("plan_row", [P, 1], I32)
        plan_e = sb("plan_e", [1, PLAN0], I32)
        places = o_sb[:, P:2 * P].bitcast(I32)
        places_f = oT[:, 1, :]
        idx = [sb(f"idx{i}", [P, 1], I32) for i in range(4)]
        idx_out = [sb(f"idx_out{i}", [P, 1], I32) for i in range(4)]
        y0 += [xr[0][:, :], xr[1][:, :]]
        xg1 += [xn[0][:, :], xn[1][:, :]]
        rows_in = [xn[0][:, :], xn[1][:, :], xr[0][:, :], xr[1][:, :]]

        bank = [ctx.enter_context(nc.psum_tensor(f"bank{i}", [P, 512], F32)) for i in range(8)]

        phase_end = sem("phase_end")
        phases = [0]

        def phase_barrier(eng, k):
            eng.drain().then_inc(phase_end, 1)
            eng.wait_ge(phase_end, 5 * k)

        consts_in = sem("consts_in")
        tri_in = sem("tri_in")
        ctx_in = sem("ctx_in")
        kv_w_in = sem("kv_w_in")
        x_rest_in = sem("x_rest_in")
        x_in = sem("x_in")
        route_in = [sem("route0_in"), sem("route1_in")]
        attn_in = [sem("attn0_in"), sem("attn1_in")]
        bias_in = [sem("bias0_in"), sem("bias1_in")]
        shared_in = sem("shared_in")
        experts0_in = sem("experts0_in")
        w1_in = sem("w1_in")
        w2_in = sem("w2_in")
        b12_in = sem("b12_in")
        bo_in = sem("bo_in")
        q_zero = sem("q_zero")
        waited_apart = sem("waited_apart")
        zeros_set = sem("zeros_set")
        table_init = sem("table_init")

        class Sems(dict):

            def __init__(self, prefix, **turns):
                self.prefix, self.turns = prefix, turns

            def __missing__(self, name):
                n = self.turns.get(name)
                full = f"{self.prefix}_{name}"
                self[name] = [sem(f"{full}{i}") for i in range(n)] if n else sem(full)
                return self[name]

        KV = Sems("kv")
        AT, ATL = Sems("at"), [Sems(f"at{l}", gath=2) for l in range(2)]
        RT, RTL = Sems("rt", saved=2), [Sems("rt0", scat=2), Sems("rt1")]
        SH = Sems("sh", rows=4, gu_mm=2)
        EX = [Sems("ex0", gath=4, out=4), Sems("ex1", gath=4, gath3=2, out=4)]

        block = ctx.enter_context(nc.Block())

        place = [0]

        def steps(eng, step, first, lo, hi, last, unroll):
            assert lo % unroll == 0 and (hi - lo) % unroll == 0
            for t in range(first, lo):
                place[0] = t % unroll
                step(t)
            with eng.Fori(0, (hi - lo) // unroll) as k:
                for u in range(unroll):
                    place[0] = u
                    step(unroll * k + (lo + u))
            for t in range(hi, last + 1):
                place[0] = t % unroll
                step(t)

        def par(j, n=2):
            return (place[0] + j) % n

        def attention_steps(eng, step):
            steps(eng, step, -5, 4, 10, NT + 2, 2)

        def shared_steps(eng, step):
            steps(eng, step, -2, 4, NT - 4, NT - 1, 4)

        def experts0_steps(eng, step):
            steps(eng, step, -6, 4, PLAN0 - 8, TILES0 - 1, 4)

        def experts1_steps(eng, step):
            steps(eng, step, -5, 4, PLAN1 - 8, TILES1 - 1, 4)

        def load_expert(eng, regs, i, v, ne):
            eng.reg_load(regs[v], plan_e[0:1, bass.ds(i, 1)])
            return expert(eng, regs, v, ne)

        def load_experts(eng, regs, before, i, v):
            if v == 0:
                if not isinstance(i, int) or i > 0:
                    for a in range(2):
                        eng.reg_mov(before[a], regs[2 + a])
                eng.reg_load(regs, plan_e[0:1, bass.ds(i, 4)])

        def expert(eng, regs, v, ne):
            return eng.snap(regs[v], min_val=0, max_val=ne - 1)

        def wait_apart(eng, sem, n):
            eng.wait_ge(sem, n)
            if not isinstance(n, int):
                eng.sem_inc(waited_apart, 1)

        def on(t, j, tiles=NT):
            return not isinstance(t, int) or 0 <= t + j < tiles

        def kv_values(sp, l):
            for b in range(B):
                sp.wait_ge(KV["v_sb"], B * l + b + 1)
                sp.dma_start(v_rows[l][b].rearrange("(h k) d -> k h d", h=H),
                             v_sb[0:S2, b, :].rearrange("k (h d) -> k h d", h=H)).then_inc(KV["v_out"], 16)
            sp.wait_ge(KV["v_out"], 16 * B * (l + 1))
            sp.wait_ge(KV["vf_zero"], l + 1)
            for b in range(B):
                full = (PC - 1) * P
                sp.dma_start(vf[:, b * PC:(b + 1) * PC - 1, :],
                             v_rows[l][b, 0:full].rearrange("(c p) d -> p c d", p=P)).then_inc(KV["v_back"], 16)
                sp.dma_start(vf[0:LASTROWS, (b + 1) * PC - 1, :],
                             v_rows[l][b, full:H * S2]).then_inc(KV["v_back"], 16)

        def save_rows(sp, l, t, u):
            sp.wait_ge(RT["xn"], t + NT * l + 1)
            sp.dma_start(xn_d[l][bass.ds(t * P, P), :], xr[u][:, :]).then_inc(RT["saved"][u], 16)

        @block.sync
        def _(sp):
            sp.dma_start(ctxT, A["ctxT"]).then_inc(ctx_in, 16)
            for name, dst in (("neg_half", neg_half), ("ident", ident)):
                sp.dma_start(dst[:, :], A[name]).then_inc(ctx_in, 16)
            for name in ("Wv", "Wk"):
                sp.dma_start(attn_w[0][name], A[f"L0_{name}"]).then_inc(kv_w_in, 16)
            sp.dma_start(attn_w[0]["Wq"], A["L0_Wq"]).then_inc(attn_in[0], 16)
            for name, dst in (("mask_k", mask_k), ("mask_v", mask_v),
                              ("iota_e", iota_e), ("part_id", part_id), ("tok_id", tok_id), ("skip_id", skip_id),
                              ("ones_row", ones_row)):
                sp.dma_start(dst[tuple(slice(None) for _ in dst.shape)], A[name]).then_inc(consts_in, 16)
            sp.dma_start(attn_w[0]["Wo"], A["L0_Wo"]).then_inc(bias_in[0], 16)
            sp.dma_start(bias[0], A["bias0"]).then_inc(bias_in[0], 16)
            sp.dma_start(rw[0][:, :, :], A["rw0"]).then_inc(route_in[0], 16)
            sp.dma_start(rb[0][:, :, :], A["rb0"].partition_broadcast(P)).then_inc(route_in[0], 16)
            sp.wait_ge(zeros_set, 1)
            sp.dma_start(table_d[0][0:ROWS0 * P].rearrange("(p c) a -> p (c a)", p=P), zeros).then_inc(table_init, 16)
            sp.dma_start(table_d[0][ROWS0 * P:].rearrange("c a -> a c"), zeros[0:1, 0:P]).then_inc(table_init, 16)
            sp.wait_ge(consts_in, 16 * 7)
            sp.dma_start(table_d[1][0:ROWS1 * P].rearrange("(p c) a -> p (c a)", p=P),
                         skip_id[:, :]).then_inc(table_init, 16)
            sp.dma_start(table_d[1][ROWS1 * P:].rearrange("c a -> a c"), skip_id[0:1, :]).then_inc(table_init, 16)
            kv_values(sp, 0)
            sp.dma_start(sgu_w, A["sgu"]).then_inc(shared_in, 16)
            sp.dma_start(sdown_w, A["sdown"]).then_inc(shared_in, 16)
            for name in ("Wk", "Wv", "Wq", "Wo"):
                sp.dma_start(attn_w[1][name], A[f"L1_{name}"]).then_inc(attn_in[1], 16)
            sp.dma_start(b1T[:, :, :], A["b1"]).then_inc(b12_in, 16)
            sp.dma_start(bqk[:, :, :], A["bqk"]).then_inc(attn_in[1], 16)
            sp.dma_start(bv_b[0:S2, :], A["bv"].partition_broadcast(S2)).then_inc(attn_in[1], 16)
            sp.dma_start(bias[1].bitcast(I32), A["mask1"]).then_inc(bias_in[1], 16)
            sp.dma_start(rw[1][:, :, :], A["rw1"]).then_inc(route_in[1], 16)
            sp.dma_start(rb[1][:, :, :], A["rb1"].partition_broadcast(P)).then_inc(route_in[1], 16)
            with sp.Fori(0, NT // 2) as k:
                e = bass.ds(k * EP, EP)
                save_rows(sp, 0, 2 * k, 0)
                sp.dma_start(gu_w[:, :, e, :], A["gu"][:, :, e, :]).then_inc(experts0_in, 16)
                save_rows(sp, 0, 2 * k + 1, 1)
                sp.dma_start(down_w[:, e, :], A["down"][:, e, :]).then_inc(experts0_in, 16)
            kv_values(sp, 1)
            sp.dma_start(bo_row[0:1, :], A["bo"]).then_inc(bo_in, 16)
            for u in range(2):
                sp.wait_ge(RT["saved"][u], 16 * NT // 2)
            sp.wait_ge(AT["xt_mm"], NT)
            for t in range(4):
                if t == 2:
                    phase_barrier(sp, 1)
                sp.dma_start(rows_in[t], xn_d[0][t * P:(t + 1) * P, :]).then_inc(SH["rows"][t], 16)
            with sp.Fori(1, NT // 4) as k:
                for u in range(4):
                    t = 4 * k + u
                    sp.wait_ge(SH["xt_mm"], t - 3)
                    sp.dma_start(rows_in[u], xn_d[0][bass.ds(t * P, P), :]).then_inc(SH["rows"][u], 16)
            phase_barrier(sp, 2)
            def store(i):
                sp.wait_ge(EX[0]["y"], i + 1)
                sp.dma_start(y_d[bass.ds(i * P, P), :], y0[par(0, 4)]).then_inc(EX[0]["out"][par(0, 4)], 16)
            steps(sp, store, 0, 0, PLAN0 - 4, TILES0 - 1, 4)
            for u in range(4):
                sp.wait_ge(EX[0]["out"][u], 16 * turns(TILES0, u))
            phase_barrier(sp, 3)
            def save_x3(t):
                sp.wait_ge(AT["x"], NT + t + 1)
                sp.dma_start(x3_d[bass.ds(t * P, P), :],
                             x[:, bass.ds(t, 1), :].rearrange("p a n -> p (a n)")).then_inc(RTL[1]["x_saved"], 16)

            with sp.Fori(0, E1) as e:
                save_rows(sp, 1, 2 * e, 0)
                save_x3(2 * e)
                sp.dma_start(w1_w[:, :, bass.ds(e, 1), :], A["w1"][:, :, bass.ds(e, 1), :]).then_inc(w1_in, 16)
                save_rows(sp, 1, 2 * e + 1, 1)
                save_x3(2 * e + 1)
                sp.dma_start(w2_w[:, bass.ds(e, 1)], A["w2"][:, bass.ds(e, 1)]).then_inc(w2_in, 16)
            for u in range(2):
                sp.wait_ge(RT["saved"][u], 16 * NT)
            sp.wait_ge(RTL[1]["x_saved"], 16 * NT)
            phase_barrier(sp, 4)
            sp.dma_start(b2_b, A["b2"].partition_broadcast(P)).then_inc(b12_in, 16)
            phase_barrier(sp, 5)
            phase_barrier(sp, 6)

        def routing(pool, l):
            RL = RTL[l]
            if l == 0:
                pool.wait_ge(table_init, 64)
                pool.wait_ge(RT["slot"], 1)

                def step(t):
                    u = par(0)
                    need(pool, RL["scat"][u], 16 * TOPK * (t // 2))
                    pool.tensor_copy(tok_cur[u][:, :], tok_id[:, bass.ds(t, 1)]).then_inc(RL["cur"], 1)
                    pool.tensor_copy(slot_cur[u][:, :], slot[:, bass.ds(t * TOPK, TOPK)]).then_inc(RL["cur"], 1)
                    wait_apart(pool, RL["cur"], 2 * t + 2)
                    for j in range(TOPK):
                        pool.indirect_dma_start(
                            table_d[l], bass.IndirectOffsetOnAxis(slot_cur[u][:, j:j + 1], 0),
                            tok_cur[u][:, :], None).then_inc(RL["scat"][u], 16)
                steps(pool, step, 0, 2, NT, NT - 1, 2)
            if l == 0:
                for u in range(2):
                    pool.wait_ge(RL["scat"][u], 16 * TOPK * NT // 2)
            else:
                pool.wait_ge(RL["scattered"], 16 * NT)
            pool.wait_ge(RT["planned"], 8 * (l + 1))
            tiles = (PLAN0, PLAN1)[l]
            pool.indirect_dma_start(places[0:tiles, :], None, table_d[l].rearrange("(r p) a -> r (p a)", p=P),
                                    bass.IndirectOffsetOnAxis(plan_row[0:tiles, :], 0)).then_inc(RT["table"], 16)

        @block.gpsimd
        def _(pool):
            pool.memset(zeros, 0).then_inc(zeros_set, 1)
            pool.memset(qz[:, :, :, :], 0.0).then_inc(q_zero, 1)
            pool.memset(ones16[:, :], 1.0)
            tri_f = chosen[:, 0:2 * P // E0, :].rearrange("p t e -> p (t e)").bitcast(F32)
            pool.dma_start(tri_f, A["tri"]).then_inc(tri_in, 16)
            pool.wait_ge(tri_in, 16)
            nc.gpsimd.tensor_copy(tri[:, :], tri_f)

            def attention(l):
                T, TL = AT, ATL[l]

                def scatter(a):
                    pool.wait_ge(TL["slot"], a + 1)
                    pool.indirect_dma_start(
                        table_d[1], bass.IndirectOffsetOnAxis(slot[:, a:a + 1], 0),
                        tok_id[:, a:a + 1], None).then_inc(RTL[1]["scattered"], 16)

                def step(t):
                    n = t + NT * l
                    if on(t, -1):
                        pool.wait_ge(RT["ve"], n)
                        u = 2 + par(-1)
                        pool.tensor_tensor(rstd[:, u:u + 1], ve[:, u:u + 1], neg_half[:, :],
                                           ALU.pow).then_inc(RT["rstd"], 1)
                    if on(t, 3):
                        pool.wait_ge(T["ve"], n + 4)
                        u = par(3)
                        pool.tensor_tensor(rstd[:, u:u + 1], ve[:, u:u + 1], neg_half[:, :],
                                           ALU.pow).then_inc(T["rstd"], 1)
                    if l == 1 and isinstance(t, int) and t >= NT - 6:
                        for a in range(min(2 * (t - NT + 6), t - 4), min(2 * (t - NT + 7), t - 3)):
                            scatter(a)
                    if l == 1 and on(t, 5):
                        u = par(5)
                        need(pool, TL["x_comb"], t + 4)
                        pool.tensor_copy(slot_cur[u][:, :], slot[:, bass.ds((t + 5) * TOPK, TOPK)]).then_inc(
                            TL["slots"], 1)
                        wait_apart(pool, TL["slots"], t + 6)
                        for j in range(TOPK):
                            pool.indirect_dma_start(
                                yg[:, u * TOPK + j, :], None, y_d,
                                bass.IndirectOffsetOnAxis(slot_cur[u][:, j:j + 1], 0)).then_inc(TL["gath"][u], 16)
                    if on(t, 2):
                        u = par(2)
                        pool.wait_ge(T["mx"], 2 * n + 6)
                        s3 = sc[u].rearrange("p (h k) -> p h k", h=H)
                        pool.tensor_tensor(s3, s3, mx[u][:, :].unsqueeze(2).to_broadcast([P, H, S2]),
                                           ALU.subtract).then_inc(T["sub"], 1)

                attention_steps(pool, step)
                if l == 1:
                    scatter(NT - 1)

            pool.wait_ge(ctx_in, 16 * 3)
            attention(0)
            phase_barrier(pool, 1)
            routing(pool, 0)
            def rows_of_tile(i):
                u = par(0, 4)
                wait_apart(pool, EX[0]["idx"], i + 1)
                pool.indirect_dma_start(xg0[u], None, xn_d[0],
                                        bass.IndirectOffsetOnAxis(idx[u][:, :], 0)).then_inc(EX[0]["gath"][u], 16)
            pool.drain().then_inc(phase_end, 1)
            for i in range(4):
                place[0] = i
                rows_of_tile(i)
            pool.wait_ge(phase_end, 5 * 2)
            steps(pool, rows_of_tile, 4, 4, PLAN0 - 4, TILES0 - 1, 4)
            phase_barrier(pool, 3)
            attention(1)
            phase_barrier(pool, 4)
            routing(pool, 1)
            phase_barrier(pool, 5)
            X1, last_row = EX[1], pool.snap(N - 1)

            def gather(dst, src, at, landed_on):
                pool.indirect_dma_start(dst, None, src, bass.IndirectOffsetOnAxis(at[:, :], 0),
                                        bounds_check=last_row, oob_is_err=False).then_inc(landed_on, 16)

            def rows(i, v):
                wait_apart(pool, X1["idx"], i + 1)
                gather(xg1[v], xn_d[1], idx[v], X1["gath"][v])

            def residual(i, u, v):
                wait_apart(pool, X1["idx_out"], i + 1)
                if not isinstance(i, int) or i > 1:
                    wait_apart(pool, X1["y2"], i - 1)
                gather(x3g[u], x3_d, idx_out[v], X1["gath3"][u])

            def results(i, u, v):
                wait_apart(pool, X1["y2"], i + 1)
                pool.indirect_dma_start(A["out"], bass.IndirectOffsetOnAxis(idx_out[v][:, :], 0), y1[u], None,
                                        bounds_check=last_row, oob_is_err=False).then_inc(X1["out"][v], 16)

            def step(s):
                if on(s, 5, TILES1):
                    rows(s + 5, par(5, 4))
                if on(s, 1, TILES1):
                    residual(s + 1, par(1), par(1, 4))
                if on(s, 0, TILES1):
                    results(s, par(0), par(0, 4))
            experts1_steps(pool, step)
            for v in range(4):
                pool.wait_ge(X1["out"][v], 16 * turns(TILES1, v))
            phase_barrier(pool, 6)

        @block.scalar
        def _(act):
            act.dma_start(x[:, 0:FIRST, :], A["x"][:, 0:FIRST, :]).then_inc(x_in, 16)
            act.wait_ge(kv_w_in, 32)
            act.dma_start(x[:, FIRST:, :], A["x"][:, FIRST:, :]).then_inc(x_rest_in, 16)

            def kv(l):
                K = KV
                for b in range(B):
                    act.wait_ge(K["v_mm"], B * l + b + 1)
                    if l == 0:
                        act.activation(v_sb[0:S2, b, :], bank[2 + b][0:S2, 0:D], ACT.Copy).then_inc(K["v_sb"], 1)
            kv(0)

            def attention(l):
                T, TL = AT, ATL[l]

                def transposed(n, g):
                    act.wait_ge(T["pt_mm"], 3 * n + g + 1)
                    act.activation(pT[:, 4 * g:4 * g + 4, :].rearrange("p c n -> p (c n)"), bank[5 + g][:, :],
                                   ACT.Copy).then_inc(T["pt"], 1)

                def step(t):
                    n = t + NT * l
                    if on(t, 0):
                        need(act, T["pv_mm"], n)
                        transposed(n, 0)
                    if on(t, 2):
                        act.wait_ge(T["xt_mm"], n + 3)
                        act.activation(xT[:, :, :].rearrange("p c n -> p (c n)"), bank[4][:, 0:D],
                                       ACT.Copy).then_inc(T["xt"], 1)
                    if on(t, 0):
                        transposed(n, 1)
                        act.wait_ge(T["pt_mm"], 3 * n + 3)
                        act.activation(pT[:, 8, :], bank[5][:, 0:P], ACT.Copy)
                        act.activation(pT[0:LASTROWS, 9, :], bank[5][0:LASTROWS, P:2 * P],
                                       ACT.Copy).then_inc(T["pt"], 1)
                    if on(t, 2):
                        act.wait_ge(T["q_mm"], n + 3)
                        for half in range(2):
                            r = slice(64 * half, 64 * half + 64)
                            if l == 0:
                                ins = act.activation(qz[r, :, half, :],
                                                     bank[4][r, 0:D].rearrange("p (c n) -> p c n", c=KC),
                                                     ACT.Copy, scale=DH ** -0.5)
                            else:
                                for c in range(KC):
                                    ins = act.activation(qz[r, c, half, :], bank[4][r, c * P:(c + 1) * P],
                                                         ACT.Identity, bias=bq4[r, c:c + 1], scale=DH ** -0.5)
                        ins.then_inc(T["q"], 1)
                    if on(t, 1):
                        u = par(1)
                        act.wait_ge(T["sub"], n + 2)
                        act.activation(sc[u], sc[u], ACT.Exp).then_inc(T["p"], 1)
                    if on(t, -1):
                        act.wait_ge(RT["xt_mm"], n)
                        act.activation(xrT[:, :, :].rearrange("p c n -> p (c n)"), bank[4][:, 0:D],
                                       ACT.Copy).then_inc(RT["xt"], 1)
                    if on(t, 0):
                        act.wait_ge(T["ot_mm"], n + 1)
                        act.activation(oT[:, :, :].rearrange("p c n -> p (c n)"), bank[7][:, 0:D],
                                       ACT.Copy).then_inc(T["ot"], 1)
                attention_steps(act, step)

            act.wait_ge(q_zero, 1)
            attention(0)
            phase_barrier(act, 1)

            act.wait_ge(RT["below"], NT)
            act.activation(wgt[:, :], wgt[:, :], ACT.Exp).then_inc(RTL[0]["exp"], 1)

            def shared(t):
                if on(t, 1):
                    act.wait_ge(SH["gu_mm"][0], t + 2)
                    need(act, SH["act"], t + 1)
                    act.activation(th, bank[2 * par(1)][:, :], ACT.Tanh, scale=0.5).then_inc(SH["th"], 1)
                if on(t, 0):
                    act.wait_ge(SH["ht_mm"], t + 1)
                    need(act, SH["dn_mm"], t)
                    act.activation(hsT.rearrange("p c n -> p (c n)"), bank[5][:, :], ACT.Copy).then_inc(SH["ht"], 1)
                if on(t, 2):
                    act.wait_ge(SH["xt_mm"], t + 3)
                    act.activation(xT[:, :, :].rearrange("p c n -> p (c n)"), bank[4][:, 0:D],
                                   ACT.Copy).then_inc(SH["xt"], 1)
            shared_steps(act, shared)
            phase_barrier(act, 2)
            X0 = EX[0]

            def experts0(s):
                u = par(0)
                if on(s, 3, TILES0):
                    act.wait_ge(X0["xt_mm"], s + 4)
                    act.activation(xgT0[(u + 1) % 2].rearrange("p c n -> p (c n)"), bank[(u + 1) % 2][:, 0:D],
                                   ACT.Copy).then_inc(X0["xt"], 1)
                if on(s, 1, TILES0):
                    act.wait_ge(X0["ht_mm"], s + 2)
                    act.activation(hT0[(u + 1) % 2], bank[4 + (u + 1) % 2][:, 0:P], ACT.Copy).then_inc(X0["ht"], 1)
                if on(s, 2, TILES0):
                    act.wait_ge(X0["h_mm"], s + 3)
                    act.activation(th0[u], bank[2 + u][:, 0:F0], ACT.Tanh, scale=0.5).then_inc(X0["th"], 1)
            experts0_steps(act, experts0)
            phase_barrier(act, 3)
            attention(1)
            phase_barrier(act, 4)
            phase_barrier(act, 5)
            X1 = EX[1]

            def experts1(s):
                u = par(0)
                if on(s, 0, TILES1):
                    for g in range(2):
                        act.wait_ge(X1["ht_mm"], 2 * s + g + 1)
                        if g == 0:
                            need(act, X1["dn_mm"], s)
                            act.wait_ge(X1["b1"], s + 1)
                        for c in range(4 * g, 4 * g + 4):
                            ins = act.activation(hT1[:, c, :], bank[5 + g][:, (c % 4) * P:(c % 4 + 1) * P], ACT.Relu,
                                                 bias=b1_of[u][:, c:c + 1])
                        ins.then_inc(X1["ht"], 1)
                if on(s, 2, TILES1):
                    act.wait_ge(X1["xt_mm"], s + 3)
                    act.activation(xgT1[u].rearrange("p c n -> p (c n)"), bank[0][:, 0:D],
                                   ACT.Copy).then_inc(X1["xt"], 1)
            experts1_steps(act, experts1)
            phase_barrier(act, 6)

        def batch(t, j):
            return (t + j) // TB

        @block.tensor
        def _(pe):
            pe.wait_ge(ctx_in, 16 * 3)

            def kv(l):
                K, W = KV, attn_w[l]
                if l == 0:
                    pe.wait_ge(kv_w_in, 32)
                else:
                    pe.wait_ge(attn_in[1], 16 * 6)
                for b in range(B):
                    for c in range(KC):
                        mm = pe.matmul(bank[2 + b][0:S2, 0:D], ctxT[:, c, b * S2:(b + 1) * S2], W["Wv"][:, c, :],
                                       start=(c == 0), stop=(c == KC - 1))
                    mm.then_inc(K["v_mm"], 1)
                for m in range(KC):
                    for c in range(KC):
                        mm = pe.matmul(bank[m][:, 0:B * S2], W["Wk"][:, c, m * P:(m + 1) * P], ctxT[:, c, :],
                                       start=(c == 0), stop=(c == KC - 1))
                    mm.then_inc(K["k_mm"], 1)
            kv(0)

            def attention(l):
                T, W = AT, attn_w[l]
                if l == 0:
                    pe.wait_ge(ctx_in, 16 * 3)
                    pe.wait_ge(attn_in[0], 16)
                else:
                    pe.wait_ge(bo_in, 16)

                def transpose_p(n, u, g):
                    need(pe, T["pt"], 3 * n - g)
                    for c in range(4 * g, 4 * g + 4):
                        mm = pe.transpose(bank[5 + g][:, (c % 4) * P:(c % 4 + 1) * P],
                                          sc[u][:, c * P:(c + 1) * P], ident[:, :])
                    mm.then_inc(T["pt_mm"], 1)

                def step(t):
                    n = t + NT * l
                    u = par(0)
                    if on(t, 0):
                        pe.wait_ge(T["p"], n + 1)
                        transpose_p(n, u, 0)
                    if l == 1 and on(t, -3):
                        TL = ATL[1]
                        if on(t, -2):
                            pe.wait_ge(RT["xt"], n - 1)
                        else:
                            pe.wait_ge(RT["lg"], NT * (l + 1))
                        pe.wait_ge(TL["chosen"], t - 2)
                        pe.matmul(bank[4][:, RK:RK + E1], tri[:, :], oh1[par(-3)], start=True, stop=False)
                        pe.wait_ge(TL["before"], t - 2)
                        pe.matmul(bank[4][:, RK:RK + E1], ones16[:, :], before1[:, bass.ds((t - 3) * E1, E1)],
                                  start=False, stop=True).then_inc(TL["rk_mm"], 1)
                    if on(t, -2):
                        R, ne = RT, (E0, E1)[l]
                        pe.wait_ge(R["xt"], n - 1)
                        for c in range(KC):
                            mm = pe.matmul(bank[4][:, 0:ne], xrT[:, c, :], rw[l][:, c, :], start=(c == 0),
                                           stop=(c == KC - 1))
                        mm.then_inc(R["lg_mm"], 1)
                    if on(t, -1):
                        if l == 0 and isinstance(t, int) and t == 1:
                            pe.wait_ge(bias_in[0], 32)
                        pe.wait_ge(T["ot"], n)
                        for c in range(KC):
                            mm = pe.matmul(bank[7][:, 0:D], oT[:, c, :], W["Wo"][:, c, :], start=(c == 0),
                                           stop=(c == KC - 1 and l == 0))
                        if l == 1:
                            mm = pe.matmul(bank[7][:, 0:D], ones_row[:, :], bo_row[0:1, :], start=False, stop=True)
                        mm.then_inc(T["wo_mm"], 1)
                    if on(t, 2):
                        v = par(2)
                        if on(t, -2):
                            pe.wait_ge(RT["lg"], n - 1)
                        pe.wait_ge(T["xn"], n + 3)
                        for c in range(KC):
                            mm = pe.transpose(bank[4][:, c * P:(c + 1) * P], xn[v][:, c * P:(c + 1) * P], ident[:, :])
                        mm.then_inc(T["xt_mm"], 1)
                    if on(t, 0):
                        transpose_p(n, u, 1)
                        pe.wait_ge(T["pt"], 3 * n + 1)
                        pe.transpose(bank[5][:, 0:P], sc[u][:, 8 * P:9 * P], ident[:, :])
                        pe.transpose(bank[5][0:LASTROWS, P:2 * P], sc[u][:, 9 * P:9 * P + LASTROWS],
                                     ident[:, :]).then_inc(T["pt_mm"], 1)
                    if on(t, 2):
                        pe.wait_ge(T["xt"], n + 3)
                        for m in range(KC):
                            for c in range(KC):
                                mm = pe.matmul(bank[4][:, m * P:(m + 1) * P], W["Wq"][:, c, m * P:(m + 1) * P],
                                               xT[:, c, :], start=(c == 0), stop=(c == KC - 1))
                        mm.then_inc(T["q_mm"], 1)
                    if on(t, 0):
                        need(pe, T["x"], n)
                        if isinstance(t, int) and t in (0, 1):
                            pe.wait_ge(KV["v_bd"], PC * (t + 1) if l == 0 else 2 * B * PC)
                        for c in range(PC):
                            if c in (0, 4, 8):
                                pe.wait_ge(T["pt"], 3 * n + c // 4 + 1)
                            rows = P if c < PC - 1 else LASTROWS
                            cols = 3 * VC if c < PC - 1 else 2 * VC
                            mm = pe.matmul(bank[7][:, HEAD0[c] * VC:HEAD0[c] * VC + cols], pT[0:rows, c, :],
                                           vbd[l][0:rows, bass.ds(batch(t, 0) * PC + c, 1), 0:cols].rearrange(
                                               "p a n -> p (a n)"),
                                           start=(c == 0), stop=(c == PC - 1), skip_group_check=True)
                        mm.then_inc(T["pv_mm"], 1)
                    if on(t, 2):
                        if l == 0 and isinstance(t, int) and t == -2:
                            pe.wait_ge(KV["v_sb"], B)
                            pe.wait_ge(KV["k_bd"], B * KC)
                        for g in range(NG):
                            pe.wait_ge(T["q"], n + 3)
                            if g % 2 == 0:
                                need(pe, T["copied"], 2 * n + 3 + g // 2)
                            c, half = g // 2, g % 2
                            mm = pe.matmul(bank[g][:, 0:HG * S2], qz[:, c, half, :],
                                           kbd[l][:, bass.ds(batch(t, 2) * KC + c, 1)].rearrange(
                                               "p a h k -> p (a h k)"), start=True, stop=True)
                            if half:
                                mm.then_inc(T["sc_mm"], 1)
                    if on(t, -1):
                        v = par(-1)
                        pe.wait_ge(RT["xn"], n)
                        if on(t, 2):
                            pe.wait_ge(T["q"], n + 3)
                        elif on(t, -2):
                            pe.wait_ge(RT["lg"], n - 1)
                        for c in range(KC):
                            mm = pe.transpose(bank[4][:, c * P:(c + 1) * P], xr[v][:, c * P:(c + 1) * P], ident[:, :])
                        mm.then_inc(RT["xt_mm"], 1)
                    if on(t, 0):
                        pe.wait_ge(T["on"], n + 1)
                        for c in range(KC):
                            mm = pe.transpose(bank[7][:, c * P:(c + 1) * P], o_sb[:, c * P:(c + 1) * P], ident[:, :])
                        mm.then_inc(T["ot_mm"], 1)
                pe.wait_ge(route_in[l], 32)
                attention_steps(pe, step)

            attention(0)
            pe.wait_ge(AT["copied"], 2 * NT)
            kv(1)
            phase_barrier(pe, 1)

            def ranks():
                dst = bank[7][:, :].rearrange("p (t e) -> p t e", t=NT)
                pe.wait_ge(RT["chosen"], 1)
                pe.matmul(dst, tri[:, :], chosen[:, :, :], start=True, stop=True, skip_group_check=True)
                for t in range(NT - 1):
                    mm = pe.matmul(dst[:, t + 1:, :], ones16[:, :],
                                   chosen[:, t:t + 1, :].to_broadcast([P, NT - 1 - t, E0]),
                                   start=False, stop=True, skip_group_check=True)
                mm.then_inc(RT["rk_mm"], 1)

            def counts(l):
                if l == 0:
                    pe.wait_ge(RT["ohr"], 1)
                    for t in range(NT):
                        mm = pe.matmul(bank[7][:, 0:E0], ones16[:, :], chosen[:, t, :], start=(t == 0),
                                       stop=(t == NT - 1))
                else:
                    pe.wait_ge(ATL[1]["before"], NT + 1)
                    mm = pe.matmul(bank[7][:, 0:E1], ones16[:, :], before1[:, NT * E1:(NT + 1) * E1], start=True,
                                   stop=True)
                mm.then_inc(RT["c_mm"], 1)

            def plan_experts(l):
                RL, tiles = RTL[l], (PLAN0, PLAN1)[l]
                pe.wait_ge(RT["planned"], 8 * (l + 1))
                pe.transpose(bank[7][0:1, 0:tiles], tile_e[0:tiles, :], ident[0:tiles, 0:tiles]).then_inc(
                    RT["turned"], 1)

            def plan_places(l):
                RL, tiles = RTL[l], (PLAN0, PLAN1)[l]
                pe.wait_ge(RT["places"], l + 1)
                pe.transpose(bank[7][:, 0:tiles], places_f[0:tiles, :], ident[0:tiles, 0:tiles]).then_inc(
                    RT["turned"], 1)

            pe.wait_ge(shared_in, 32)

            def shared(t):
                u = par(0)
                v = 1 - u

                def hidden(a):
                    for c in range(KC):
                        mm = pe.matmul(bank[2 * v + a][:, :], xT[:, c, :], sgu_w[:, c, a * FS:(a + 1) * FS],
                                       start=(c == 0), stop=(c == KC - 1))
                    mm.then_inc(SH["gu_mm"][a], 1)

                if on(t, 1):
                    pe.wait_ge(SH["xt"], t + 2)
                    need(pe, SH["h"], t)
                    hidden(0)
                if on(t, 0):
                    pe.wait_ge(SH["h"], t + 1)
                    need(pe, SH["ht"], t)
                    for c in range(FS // P):
                        mm = pe.transpose(bank[5][:, c * P:(c + 1) * P], hs[u][:, c * P:(c + 1) * P], ident[:, :])
                    mm.then_inc(SH["ht_mm"], 1)
                if on(t, 1):
                    hidden(1)
                if on(t, 2):
                    pe.wait_ge(SH["rows"][par(2, 4)], landed(t + 2, 4))
                    need(pe, SH["xt"], t + 2)
                    for c in range(KC):
                        mm = pe.transpose(bank[4][:, c * P:(c + 1) * P], rows_in[par(2, 4)][:, c * P:(c + 1) * P],
                                          ident[:, :])
                    mm.then_inc(SH["xt_mm"], 1)
                if isinstance(t, int) and t == -1:
                    ranks()
                if isinstance(t, int) and t == 0:
                    counts(0)
                if isinstance(t, int) and t == 3:
                    plan_experts(0)
                if isinstance(t, int) and t == NT - 1:
                    plan_places(0)
                if on(t, 0):
                    pe.wait_ge(SH["ht"], t + 1)
                    need(pe, SH["x"], t)
                    for c in range(FS // P):
                        mm = pe.matmul(bank[6][:, 0:D], hsT[:, c, :], sdown_w[:, c, :], start=(c == 0),
                                       stop=(c == FS // P - 1))
                    mm.then_inc(SH["dn_mm"], 1)
            shared_steps(pe, shared)
            phase_barrier(pe, 2)
            X0 = EX[0]
            pe.wait_ge(experts0_in, 16 * NT)
            pe_experts = [pe.alloc_register(f"pe_expert{i}") for i in range(4)]
            pe_before = [pe.alloc_register(f"pe_before{i}") for i in range(2)]

            def experts0(s):
                u = par(0)
                v = 1 - u
                if on(s, 3, TILES0):
                    pe.wait_ge(X0["gath"][par(3, 4)], landed(s + 3, 4))
                    need(pe, X0["xt"], s + 2)
                    for c in range(KC):
                        mm = pe.transpose(bank[v][:, c * P:(c + 1) * P], xg0[par(3, 4)][:, c * P:(c + 1) * P],
                                          ident[:, :])
                    mm.then_inc(X0["xt_mm"], 1)
                if on(s, 2, TILES0):
                    load_experts(pe, pe_experts, pe_before, s + 2, par(2, 4))
                    e = expert(pe, pe_experts, par(2, 4), E0)
                    pe.wait_ge(X0["xt"], s + 3)
                    need(pe, X0["h"], s + 1)
                    for c in range(KC):
                        mm = pe.matmul(bank[2 + u][:, 0:2 * F0], xgT0[u][:, c, :],
                                       gu_w[:, c, bass.ds(e, 1), :].rearrange("p a n -> p (a n)"),
                                       start=(c == 0), stop=(c == KC - 1))
                    mm.then_inc(X0["h_mm"], 1)
                if on(s, 1, TILES0):
                    pe.wait_ge(X0["h"], s + 2)
                    need(pe, X0["ht"], s)
                    pe.transpose(bank[4 + v][:, 0:P], h0[v], ident[:, :]).then_inc(X0["ht_mm"], 1)
                if on(s, 0, TILES0):
                    same = par(2, 4) >= 2 or not on(s, 2, TILES0)
                    e = expert(pe, pe_experts, par(0, 4), E0) if same else expert(pe, pe_before, par(-2, 4), E0)
                    pe.wait_ge(X0["ht"], s + 1)
                    need(pe, X0["y"], s - 1)
                    pe.matmul(bank[6 + u][:, 0:D], hT0[u], down_w[:, bass.ds(e, 1), :].rearrange("p a n -> p (a n)"),
                              start=True, stop=True).then_inc(X0["dn_mm"], 1)
            experts0_steps(pe, experts0)
            phase_barrier(pe, 3)
            attention(1)
            phase_barrier(pe, 4)
            counts(1)
            plan_experts(1)
            plan_places(1)
            phase_barrier(pe, 5)
            X1 = EX[1]
            pe.wait_ge(w1_in, 16 * E1)
            pe.wait_ge(w2_in, 16 * E1)

            def experts1(s):
                u = par(0)
                v = 1 - u
                if on(s, 0, TILES1):
                    for g in range(2):
                        pe.wait_ge(X1["h"], 2 * s + g + 1)
                        need(pe, X1["ht"], 2 * s + g - 1)
                        for c in range(4 * g, 4 * g + 4):
                            mm = pe.transpose(bank[5 + g][:, (c % 4) * P:(c % 4 + 1) * P],
                                              h1[u][:, c * P:(c + 1) * P], ident[:, :])
                        mm.then_inc(X1["ht_mm"], 1)
                if on(s, 2, TILES1):
                    pe.wait_ge(X1["gath"][par(2, 4)], landed(s + 2, 4))
                    need(pe, X1["xt"], s + 2)
                    for c in range(KC):
                        mm = pe.transpose(bank[0][:, c * P:(c + 1) * P], xg1[par(2, 4)][:, c * P:(c + 1) * P],
                                          ident[:, :])
                    mm.then_inc(X1["xt_mm"], 1)
                if on(s, 1, TILES1):
                    e = load_expert(pe, pe_experts, s + 1, par(1, 4), E1)
                    pe.wait_ge(X1["xt"], s + 2)
                    need(pe, X1["h"], 2 * s)
                    for a in range(2):
                        for c in range(KC):
                            mm = pe.matmul(bank[1 + 2 * v + a][:, :], xgT1[v][:, c, :],
                                           w1_w[:, c, bass.ds(e, 1), a * 512:(a + 1) * 512].rearrange(
                                               "p a n -> p (a n)"),
                                           start=(c == 0), stop=(c == KC - 1))
                        mm.then_inc(X1["h_mm"], 1)
                if on(s, 0, TILES1):
                    e = expert(pe, pe_experts, par(0, 4), E1)
                    need(pe, X1["y"], s)
                    for c in range(FC1):
                        if c % 4 == 0:
                            pe.wait_ge(X1["ht"], 2 * s + c // 4 + 1)
                        mm = pe.matmul(bank[7][:, 0:D], hT1[:, c, :],
                                       w2_w[:, bass.ds(e, 1), c, :].rearrange("p a n -> p (a n)"),
                                       start=(c == 0), stop=(c == FC1 - 1))
                    mm.then_inc(X1["dn_mm"], 1)
            experts1_steps(pe, experts1)
            phase_barrier(pe, 6)

        @block.vector
        def _(dve):
            def tile_in_batch(t, j):
                return (t + j) % TB

            def column(dst, i, copied):
                dve.tensor_copy(dst[:, :], idx_all[:, bass.ds(i, 1)]).then_inc(copied, 1)

            def row_stats(R, u, t):
                dve.bn_stats(stat[:, u, :], x[:, bass.ds(t, 1), :].rearrange("p a n -> p (a n)")).then_inc(
                    R["stats"], 1)

            def mean_var(R, n, u):
                wait_apart(dve, R["stats"], 2 * n + 1)
                dve.bn_aggr(mv[:, u, :], stat[:, u, :]).then_inc(R["stats"], 1)

            def var_eps(R, n, u):
                dve.wait_ge(R["stats"], 2 * n + 2)
                dve.tensor_scalar(ve[:, u:u + 1], mv[:, u, 1:2], EPS, None, ALU.add).then_inc(R["ve"], 1)

            def layer_norm(R, dst, t, n, u):
                dve.wait_ge(R["rstd"], n + 1)
                dve.tensor_scalar(dst[:, :], x[:, bass.ds(t, 1), :].rearrange("p a n -> p (a n)"),
                                  mv[:, u, 0:1], rstd[:, u:u + 1], ALU.subtract, ALU.mult).then_inc(R["xn"], 1)

            def kv(l):
                K = KV
                if l == 1:
                    dve.memset(vf, 0.0).then_inc(K["vf_zero"], 1)
                    dve.wait_ge(attn_in[1], 16 * 6)
                    dve.tensor_scalar(bq4[:, :], bqk[:, 0, :], DH ** -0.5, None, ALU.mult).then_inc(K["bq"], 1)
                    for b in range(B):
                        dve.wait_ge(K["v_mm"], B * l + b + 1)
                        dve.tensor_tensor(v_sb[0:S2, b, :], bank[2 + b][0:S2, 0:D], bv_b[0:S2, :],
                                          ALU.add).then_inc(K["v_sb"], 1)
                dve.wait_ge(consts_in, 16 * 7)
                for m in range(KC):
                    dve.wait_ge(K["k_mm"], KC * l + m + 1)
                    if m:
                        dve.wait_ge(K["k_bd"], B * (KC * l + m))
                    dve.tensor_scalar(k_sb, bank[m][:, 0:B * S2], bqk[:, 1, m:m + 1] if l else 0.0, None,
                                      ALU.add).then_inc(K["k_sb"], 1)
                    dve.wait_ge(K["k_sb"], KC * l + m + 1)
                    for b in range(B):
                        dve.tensor_tensor(kbd[l][:, b * KC + m],
                                          k_sb[:, b * S2:(b + 1) * S2].unsqueeze(1).to_broadcast([P, HG, S2]),
                                          mask_k[:, :].unsqueeze(2).to_broadcast([P, HG, S2]),
                                          ALU.mult).then_inc(K["k_bd"], 1)

            def values(l, lo, hi):
                K = KV
                dve.wait_ge(K["v_back"], 16 * 2 * B * (l + 1))
                for i in range(lo, hi):
                    c = i % PC
                    v4 = vbd[l][:, i, :].rearrange("p (j d) -> p j d", j=3)
                    dve.tensor_tensor(v4[:, :, 0:DH], vf[:, i:i + 1, :].to_broadcast([P, 3, DH]),
                                      mask_v[:, c, :].unsqueeze(2).to_broadcast([P, 3, DH]), ALU.mult)
                    dve.tensor_copy(v4[:, :, DH:DH + 1], mask_v[:, c, :].unsqueeze(2)).then_inc(K["v_bd"], 1)

            dve.memset(vf, 0.0).then_inc(KV["vf_zero"], 1)

            def attention(l):
                T, TL = AT, ATL[l]
                if l == 0:
                    dve.wait_ge(x_in, 16)
                if l == 1:
                    dve.wait_ge(bias_in[1], 16)
                    dve.wait_ge(route_in[1], 32)
                    dve.tensor_tensor(rb[1][:, 0, :], rb[1][:, 0, :], rb[1][:, 1, :], ALU.add).then_inc(
                        RTL[1]["bias"], 1)
                    dve.wait_ge(RTL[1]["bias"], 1)
                    dve.memset(before1[:, 0:E1], 0.0).then_inc(TL["before"], 1)

                def combine(t, j):
                    u = par(4) if j < 2 else par(3)
                    xt_ = x[:, bass.ds(t, 1), :].rearrange("p a n -> p (a n)")
                    if j == 0:
                        dve.wait_ge(TL["gath"][u], landed(t, 2, TOPK))
                    else:
                        dve.wait_ge(TL["summing"], 3 * t + j)
                    dve.scalar_tensor_tensor(
                        out=xt_, in0=yg[:, u * TOPK + j, :], scalar=wgt[:, bass.ds(t * TOPK + j, 1)],
                        in1=xt_, op0=ALU.mult, op1=ALU.add).then_inc(
                            TL["x_comb"] if j == TOPK - 1 else TL["summing"], 1)

                def maxima(n, u, g):
                    s3 = sc[u].rearrange("p (h k) -> p h k", h=H)
                    dve.wait_ge(T["copied"], 2 * n + g + 1)
                    dve.tensor_reduce(mx[u][:, 8 * g:8 * g + 8], s3[:, 8 * g:8 * g + 8, :], AX.X,
                                      ALU.max).then_inc(T["mx"], 1)

                def step(t):
                    n = t + NT * l
                    ne, nk = (E0, E1)[l], (TOPK, 1)[l]
                    w, m = par(-2), n - 1
                    if l == 0 and isinstance(t, int) and t == -2:
                        kv(0)
                        dve.wait_ge(bias_in[0], 32)
                        dve.wait_ge(route_in[0], 32)
                    if l == 0 and isinstance(t, int) and t == -1:
                        values(0, 0, PC)
                    if l == 0 and isinstance(t, int) and t == 1:
                        values(0, PC, B * PC)
                    if l == 0 and isinstance(t, int) and t == FIRST - 4:
                        dve.wait_ge(x_rest_in, 16)
                    if l == 1 and on(t, -3):
                        if on(t, -2):
                            dve.wait_ge(RT["lg_mm"], m)
                        else:
                            dve.wait_ge(TL["rk_mm"], t - 2)
                        dve.tensor_tensor(ohr1, bank[4][:, RK:RK + E1], oh1[par(-3)], ALU.mult).then_inc(TL["ohr"], 1)
                    if on(t, -2):
                        dve.wait_ge(RT["lg_mm"], m)
                        dve.tensor_tensor(lg[:, 0:ne], bank[4][:, 0:ne], rb[l][:, 0, :], ALU.add).then_inc(RT["lg"], 1)
                    if on(t, 1):
                        maxima(n + 1, par(1), 1)
                    if on(t, -2):
                        wait_apart(dve, RT["lg"], m)
                        dve.max(m8[w][:, :], lg[:, 0:ne]).then_inc(RT["mx"], 1)
                    if l == 1 and on(t, -3):
                        dve.wait_ge(TL["ohr"], t - 2)
                        dve.tensor_reduce(rk[:, 0:1], ohr1, AX.X, ALU.add).then_inc(TL["rank"], 1)
                    if on(t, -1):
                        dve.wait_ge(T["wo_mm"], n)
                        dve.tensor_tensor(x[:, bass.ds(t - 1, 1), :].rearrange("p a n -> p (a n)"),
                                          bank[7][:, 0:D], x[:, bass.ds(t - 1, 1), :].rearrange("p a n -> p (a n)"),
                                          ALU.add).then_inc(T["x"], 1)
                    if l == 1 and on(t, 3):
                        combine(t + 3, 2)
                    if on(t, -2):
                        wait_apart(dve, RT["mx"], m)
                        dve.max_index(i8[w][:, :], m8[w][:, :], lg[:, 0:ne]).then_inc(RT["ix"], 1)
                    if l == 1 and on(t, 3):
                        combine(t + 3, 3)
                    if on(t, -1):
                        wait_apart(dve, T["x"], n)
                        row_stats(RT, 2 + par(-1), t - 1)
                    if on(t, 3):
                        if l == 1:
                            wait_apart(dve, TL["x_comb"], t + 4)
                        row_stats(T, par(3), t + 3)
                    if l == 0 and on(t, -2):
                        dve.tensor_scalar(wgt[:, bass.ds((t - 2) * TOPK, TOPK)], m8[w][:, 0:TOPK], m8[w][:, 0:1],
                                          None, ALU.subtract).then_inc(RT["below"], 1)
                    if on(t, -1):
                        mean_var(RT, n - 1, 2 + par(-1))
                    if on(t, 3):
                        mean_var(T, n + 3, par(3))
                    if l == 1 and on(t, -3):
                        dve.wait_ge(TL["rank"], t - 2)
                        dve.scalar_tensor_tensor(out=slot[:, bass.ds(t - 3, 1)], in0=ef[:, bass.ds(t - 3, 1)],
                                                 scalar=float(N), in1=rk[:, 0:1], op0=ALU.mult,
                                                 op1=ALU.add).then_inc(TL["slot"], 1)
                    if on(t, -2):
                        dve.wait_ge(RT["ix"], m)
                        dve.tensor_copy(ef[:, bass.ds((t - 2) * nk, nk)], i8[w][:, 0:nk]).then_inc(RT["ef"], 1)
                    if l == 1 and on(t, -2):
                        dve.wait_ge(RT["ef"], m)
                        dve.tensor_tensor(oh1[w], iota_e[:, 0:E1], ef[:, bass.ds(t - 2, 1)].to_broadcast([P, E1]),
                                          ALU.is_equal).then_inc(TL["chosen"], 1)
                    if on(t, -1):
                        var_eps(RT, n - 1, 2 + par(-1))
                    if on(t, 3):
                        var_eps(T, n + 3, par(3))
                    if on(t, 0):
                        dve.wait_ge(T["pv_mm"], n + 1)
                        o3 = bank[7][:, 0:H * VC].rearrange("p (h d) -> p h d", h=H)
                        dve.reciprocal(rs[:, :].unsqueeze(2), o3[:, :, DH:DH + 1]).then_inc(T["rs"], 1)
                        dve.wait_ge(T["rs"], n + 1)
                        dve.tensor_tensor(o_sb[:, :].rearrange("p (h d) -> p h d", h=H), o3[:, :, 0:DH],
                                          rs[:, :].unsqueeze(2).to_broadcast([P, H, DH]),
                                          ALU.mult).then_inc(T["on"], 1)
                    if on(t, -1):
                        u = par(-1)
                        need(dve, RT["xt_mm"], n - 2)
                        need(dve, RT["saved"][u], 16 * ((n - 1) // 2))
                        layer_norm(RT, xr[u], t - 1, n - 1, 2 + u)
                    if l == 1 and on(t, -2):
                        dve.wait_ge(TL["chosen"], t - 1)
                        dve.tensor_tensor(before1[:, bass.ds((t - 1) * E1, E1)], before1[:, bass.ds((t - 2) * E1, E1)],
                                          oh1[w], ALU.add).then_inc(TL["before"], 1)
                    if on(t, 3):
                        u = par(3)
                        need(dve, T["xt_mm"], n + 2)
                        layer_norm(T, xn[u], t + 3, n + 3, u)
                    if on(t, 2):
                        u = par(2)
                        if l == 0:
                            bt = bias[0][:, bass.ds(tile_in_batch(t, 2), 1), :]
                        else:
                            bt = bias[1][:, bass.ds(t + 2, 1), :]
                        s3 = sc[u].rearrange("p (h k) -> p h k", h=H)
                        for g in range(2):
                            dve.wait_ge(T["sc_mm"], 2 * n + 5 + g)
                            for a in range(2):
                                q = 2 * g + a
                                ins = dve.tensor_tensor(s3[:, HG * q:HG * q + HG, :],
                                                        bank[q][:, 0:HG * S2].rearrange("p (h k) -> p h k", h=HG),
                                                        bt.to_broadcast([P, HG, S2]), ALU.add)
                                if a == 1:
                                    ins.then_inc(T["copied"], 1)
                                elif l == 1 and on(t, 4):
                                    combine(t + 4, g)
                        maxima(n + 2, u, 0)
                    elif l == 1 and on(t, 4):
                        for j in range(2):
                            combine(t + 4, j)
                attention_steps(dve, step)

            attention(0)
            kv(1)
            phase_barrier(dve, 1)

            def route():
                k_all = NT * TOPK
                dve.wait_ge(RT["ef"], NT)
                dve.tensor_tensor(oh, iota_e[:, :].unsqueeze(1).to_broadcast([P, k_all, E0]),
                                  ef[:, :].unsqueeze(2).to_broadcast([P, k_all, E0]),
                                  ALU.is_equal).then_inc(RT["routed"], 1)
                dve.wait_ge(RT["routed"], 1)
                with nc.allow_low_precision("zeros and ones, exact in bfloat16"):
                    dve.tensor_reduce(chosen[:, :, :], oh.rearrange("p (t j) e -> p t e j", t=NT), AX.X,
                                      ALU.add).then_inc(RT["chosen"], 1)
                dve.wait_ge(RT["rk_mm"], 1)
                dve.tensor_tensor(ohr.rearrange("p (t j) e -> p t j e", t=NT),
                                  bank[7][:, :].rearrange("p (t e) -> p t e", t=NT).unsqueeze(2).to_broadcast(
                                      [P, NT, TOPK, E0]),
                                  oh.rearrange("p (t j) e -> p t j e", t=NT), ALU.mult).then_inc(RT["ohr"], 1)
                dve.wait_ge(RT["ohr"], 1)
                dve.tensor_reduce(rk, ohr, AX.X, ALU.add).then_inc(RT["routed"], 1)
                dve.wait_ge(RT["routed"], 2)
                dve.scalar_tensor_tensor(out=slot[:, :], in0=ef[:, :], scalar=float(N), in1=rk, op0=ALU.mult,
                                         op1=ALU.add).then_inc(RT["slot"], 1)

            def plan(l, ne):
                RL, rows, tiles = RTL[l], (ROWS0, ROWS1)[l], (PLAN0, PLAN1)[l]
                planned = RT["planned"]
                dve.wait_ge(RT["c_mm"], l + 1)
                dve.tensor_scalar(cnt[:, 0:ne], bank[7][:, 0:ne], float(P - 1), None, ALU.add).then_inc(planned, 1)
                dve.wait_ge(planned, 8 * l + 1)
                dve.tensor_scalar(cnt[:, 0:ne], cnt[:, 0:ne], P.bit_length() - 1, None,
                                  ALU.logical_shift_right).then_inc(planned, 1)
                dve.wait_ge(planned, 8 * l + 2)
                dve.tensor_copy(cntf[:, 0:ne], cnt[:, 0:ne]).then_inc(planned, 1)
                dve.wait_ge(planned, 8 * l + 3)
                dve.tensor_tensor_scan(end[:, 0:ne], cntf[:, 0:ne], cntf[:, 0:ne], 0.0, ALU.add,
                                       ALU.bypass).then_inc(planned, 1)
                dve.wait_ge(planned, 8 * l + 4)
                dve.tensor_tensor(later[:, 0:ne], part_id[:, :].to_broadcast([P, ne]), end[:, 0:ne],
                                  ALU.is_ge).then_inc(planned, 1)
                dve.wait_ge(planned, 8 * l + 5)
                dve.tensor_reduce(past, later[:, 0:ne], AX.X, ALU.add).then_inc(RT["routed"], 1)
                dve.tensor_tensor(later[:, 0:ne], later[:, 0:ne], cntf[:, 0:ne], ALU.mult).then_inc(RT["routed"], 1)
                dve.wait_ge(RT["routed"], 4 * l + 4)
                dve.tensor_reduce(tiles_past, later[:, 0:ne], AX.X, ALU.add).then_inc(RT["routed"], 1)
                dve.tensor_scalar(tile_e[:, :], past, float(ne - 1), None, ALU.min).then_inc(planned, 1)
                dve.wait_ge(RT["routed"], 4 * l + 5)
                dve.tensor_tensor(tiles_past, part_id[:, :], tiles_past, ALU.subtract).then_inc(RT["routed"], 1)
                dve.wait_ge(RT["routed"], 4 * l + 6)
                dve.scalar_tensor_tensor(out=tile_row, in0=past, scalar=float(JT),
                                         in1=tiles_past, op0=ALU.mult, op1=ALU.add).then_inc(planned, 1)
                dve.wait_ge(planned, 8 * l + 7)
                dve.tensor_scalar(plan_row[:, :], tile_row, float(rows), None, ALU.min).then_inc(planned, 1)

            def weights():
                w3 = wgt[:, :].rearrange("p (t j) -> p t j", t=NT)
                dve.wait_ge(RTL[0]["exp"], 1)
                dve.tensor_reduce(es, w3, AX.X, ALU.add).then_inc(RTL[0]["weighing"], 1)
                dve.wait_ge(RTL[0]["weighing"], 1)
                dve.reciprocal(er, es).then_inc(RTL[0]["weighing"], 1)
                dve.wait_ge(RTL[0]["weighing"], 2)
                dve.tensor_tensor(w3, w3, er.unsqueeze(2).to_broadcast([P, NT, TOPK]), ALU.mult)

            def plan_ends(l):
                RL, tiles = RTL[l], (PLAN0, PLAN1)[l]
                dve.wait_ge(RT["turned"], 2 * l + 1)
                dve.tensor_copy(plan_e[:, 0:tiles], bank[7][0:1, 0:tiles])
                dve.wait_ge(RT["table"], 16 * (l + 1))
                dve.tensor_copy(places_f[0:tiles, :], places[0:tiles, :]).then_inc(RT["places"], 1)
                dve.wait_ge(RT["turned"], 2 * (l + 1))
                dve.tensor_copy(idx_all[:, 0:tiles], bank[7][:, 0:tiles]).then_inc(RT["idx_all"], 1)
                dve.wait_ge(RT["idx_all"], l + 1)

            route()

            def shared(t):
                if isinstance(t, int) and t == 2:
                    plan(0, E0)
                    weights()
                if isinstance(t, int) and t == NT - 1:
                    plan_ends(0)
                    for i in range(4):
                        column(idx[i], i, EX[0]["idx"])
                    rows_of_results(0)
                if on(t, 0):
                    dve.wait_ge(SH["dn_mm"], t + 1)
                    xt_ = x[:, bass.ds(t, 1), :].rearrange("p a n -> p (a n)")
                    dve.tensor_tensor(xt_, bank[6][:, 0:D], xt_, ALU.add).then_inc(SH["x"], 1)

            def rows_of_results(part):
                moved = RTL[0]["shifting"]
                if part == 0:
                    dve.tensor_tensor(shift[:, :], end[:, :], cntf[:, :], ALU.subtract).then_inc(moved, 1)
                    dve.tensor_tensor(picked, iota_e[:, :].unsqueeze(1).to_broadcast([P, NT * TOPK, E0]),
                                      ef[:, :].unsqueeze(2).to_broadcast([P, NT * TOPK, E0]),
                                      ALU.is_equal).then_inc(moved, 1)
                    dve.wait_ge(moved, 2)
                    dve.scalar_tensor_tensor(out=shift[:, :], in0=iota_e[:, :], scalar=float(-JT), in1=shift[:, :],
                                             op0=ALU.mult, op1=ALU.add).then_inc(moved, 1)
                if part == 1:
                    dve.wait_ge(moved, 3)
                    dve.tensor_tensor(picked, picked, shift[:, :].unsqueeze(1).to_broadcast([P, NT * TOPK, E0]),
                                      ALU.mult).then_inc(moved, 1)
                if part == 2:
                    dve.wait_ge(moved, 4)
                    dve.tensor_reduce(shift_of[:, :], picked, AX.X, ALU.add).then_inc(moved, 1)
                if part == 3:
                    dve.wait_ge(moved, 5)
                    dve.scalar_tensor_tensor(out=slot[:, :], in0=shift_of[:, :], scalar=float(P), in1=slot[:, :],
                                             op0=ALU.mult, op1=ALU.add).then_inc(moved, 1)

            def shared_hidden(t):
                u = par(1)
                if on(t, 1):
                    dve.wait_ge(SH["th"], t + 2)
                    dve.scalar_tensor_tensor(out=hs[u], in0=th, scalar=1.0, in1=bank[2 * u][:, :],
                                             op0=ALU.add, op1=ALU.mult).then_inc(SH["act"], 1)
                    dve.wait_ge(SH["act"], t + 2)
                    dve.wait_ge(SH["gu_mm"][1], t + 2)
                    dve.scalar_tensor_tensor(out=hs[u], in0=hs[u], scalar=0.5, in1=bank[2 * u + 1][:, :],
                                             op0=ALU.mult, op1=ALU.mult).then_inc(SH["h"], 1)

            def shared_step(t):
                shared_hidden(t)
                shared(t)
            shared_steps(dve, shared_step)
            X0 = EX[0]
            phase_barrier(dve, 2)

            def experts0(s):
                u = par(0)
                if isinstance(s, int) and s == -2:
                    for part in range(1, 4):
                        rows_of_results(part)
                if isinstance(s, int) and s == 0:
                    dve.wait_ge(bias_in[1], 16)
                    dve.tensor_scalar(bias[1], bias[1].bitcast(I32), 0.0, MASKED, ALU.is_equal,
                                      ALU.mult).then_inc(KV["mask"], 1)
                if isinstance(s, int) and 0 <= s < 4:
                    values(1, s * B * PC // 4, (s + 1) * B * PC // 4)
                if on(s, 6, TILES0) and not (isinstance(s, int) and s < -2):
                    need(dve, X0["xt_mm"], s + 3)
                    column(idx[par(6, 4)], s + 6, X0["idx"])
                if on(s, 2, TILES0):
                    dve.wait_ge(X0["th"], s + 3)
                    dve.scalar_tensor_tensor(out=t0_[u], in0=th0[u], scalar=1.0, in1=bank[2 + u][:, 0:F0],
                                             op0=ALU.add, op1=ALU.mult).then_inc(X0["act"], 1)
                    dve.wait_ge(X0["act"], s + 3)
                    dve.scalar_tensor_tensor(out=h0[u], in0=t0_[u], scalar=0.5, in1=bank[2 + u][:, F0:2 * F0],
                                             op0=ALU.mult, op1=ALU.mult).then_inc(X0["h"], 1)
                if on(s, 0, TILES0):
                    dve.wait_ge(X0["dn_mm"], s + 1)
                    need(dve, X0["out"][par(0, 4)], 16 * (s // 4))
                    dve.tensor_copy(y0[par(0, 4)], bank[6 + u][:, 0:D]).then_inc(X0["y"], 1)
            experts0_steps(dve, experts0)
            phase_barrier(dve, 3)
            attention(1)
            phase_barrier(dve, 4)
            plan(1, E1)
            plan_ends(1)
            phase_barrier(dve, 5)
            X1 = EX[1]
            dve.wait_ge(b12_in, 32)
            dve_experts = [dve.alloc_register(f"dve_expert{i}") for i in range(4)]

            def experts1(s):
                u = par(0)
                v = 1 - u
                if on(s, 5, TILES1):
                    need(dve, X1["xt_mm"], s + 2)
                    column(idx[par(5, 4)], s + 5, X1["idx"])
                if on(s, 1, TILES1):
                    need(dve, X1["out"][par(1, 4)], 16 * ((s + 1) // 4))
                    column(idx_out[par(1, 4)], s + 1, X1["idx_out"])
                if on(s, 1, TILES1):
                    e = load_expert(dve, dve_experts, s + 1, par(1, 4), E1)
                    need(dve, X1["ht"], 2 * (s - 1) + 2)
                    dve.tensor_copy(b1_of[v], b1T[:, bass.ds(e, 1), :].rearrange("p a n -> p (a n)")).then_inc(
                        X1["b1"], 1)
                    for a in range(2):
                        dve.wait_ge(X1["h_mm"], 2 * s + a + 3)
                        dve.tensor_copy(h1[v][:, a * 512:(a + 1) * 512], bank[1 + 2 * v + a][:, :]).then_inc(X1["h"], 1)
                if on(s, 0, TILES1):
                    e = expert(dve, dve_experts, par(0, 4), E1)
                    dve.wait_ge(X1["dn_mm"], s + 1)
                    need(dve, X1["out"][par(2, 4)], landed(s - 2, 4))
                    dve.tensor_tensor(y1[u], bank[7][:, 0:D], b2_b[:, bass.ds(e, 1), :].rearrange("p a n -> p (a n)"),
                                      ALU.add).then_inc(X1["y"], 1)
                    dve.wait_ge(X1["y"], s + 1)
                    dve.wait_ge(X1["gath3"][u], landed(s, 2))
                    dve.tensor_tensor(y1[u], y1[u], x3g[u], ALU.add).then_inc(X1["y2"], 1)
            experts1_steps(dve, experts1)
            phase_barrier(dve, 6)


def constants():
    p = np.arange(P)
    f = P * np.arange(PC)[None, :] + p[:, None]
    return {
        "ident": np.eye(P, dtype=np.float32),
        "mask_k": ((p[:, None] % 64) // DH == np.arange(HG)).astype(np.float32),
        "mask_v": ((f // S2)[:, :, None] == (np.array(HEAD0)[None, :, None] + np.arange(3))).astype(np.float32)
        * (f < H * S2)[:, :, None].astype(np.float32),
        "neg_half": np.full((P, 1), -0.5, np.float32),
        "tri": (p[:, None] < p[None, :]).astype(np.float32),
        "iota_e": np.tile(np.arange(E0, dtype=np.float32), (P, 1)),
        "part_id": p[:, None].astype(np.float32),
        "tok_id": (P * np.arange(NT)[None, :] + p[:, None]).astype(np.int32),
        "skip_id": np.tile((SKIP + p)[:, None], (1, ROWS1)).astype(np.int32),
        "ones_row": np.ones((1, P), np.float32),
    }


def rows_of(a, p=P):
    return a.reshape(-1, p, *a.shape[1:]).swapaxes(0, 1)


def kernel(**inputs):
    import concourse.bacc as bacc
    from concourse.bass_utils import run_bass_kernel_spmd

    a = {k: np.asarray(v) for k, v in inputs.items()}
    arrays = dict(constants())
    arrays["x"] = rows_of(a["x"].reshape(N, D))
    arrays["ctxT"] = rows_of(a["ctx_1024"].reshape(B * S2, D).T)
    for l in range(2):
        for w in ("Wq", "Wk", "Wv", "Wo"):
            arrays[f"L{l}_{w}"] = rows_of(a[f"L{l}_xattn_{w}"].T)
    arrays["bias0"] = rows_of(a["fside_1x1xSxS2_0"].reshape(S, S2))
    arrays["mask1"] = rows_of(a["mask_BxSxS2_if1"].reshape(N, S2))
    arrays["bqk"] = np.stack([a["L1_xattn_bq"].reshape(KC, P).T, a["L1_xattn_bk"].reshape(KC, P).T], 1)
    arrays["bv"] = a["L1_xattn_bv"].reshape(1, D)
    arrays["bo"] = a["L1_xattn_bo"].reshape(1, D)
    arrays["rw0"] = rows_of(a["L0_ffn_router_w"].T)
    arrays["rb0"] = a["L0_ffn_router_bias"].reshape(1, 1, E0)
    arrays["rw1"] = rows_of(a["L1_ffn_gate_w"].T)
    arrays["rb1"] = np.stack([a["L1_ffn_gate_b"], a["L1_ffn_expert_bias"]])[None]
    arrays["gu"] = rows_of(np.concatenate([a["L0_ffn_gate_w"], a["L0_ffn_up_w"]], 1).transpose(2, 0, 1))
    arrays["down"] = a["L0_ffn_down_w"].transpose(2, 0, 1)
    arrays["sgu"] = rows_of(np.concatenate([a["L0_ffn_sgate_w"], a["L0_ffn_sup_w"]], 0).T)
    arrays["sdown"] = rows_of(a["L0_ffn_sdown_w"].T)
    arrays["w1"] = a["L1_ffn_w1"].reshape(E1, KC, P, F1).transpose(2, 1, 0, 3)
    arrays["b1"] = a["L1_ffn_b1"].reshape(E1, FC1, P).transpose(2, 0, 1)
    arrays["w2"] = a["L1_ffn_w2"].reshape(E1, FC1, P, D).transpose(2, 0, 1, 3)
    arrays["b2"] = a["L1_ffn_b2"].reshape(1, E1, D)
    arrays = {k: np.ascontiguousarray(v) for k, v in arrays.items()}

    nc = bacc.Bacc("TRN2", target_bir_lowering=False, num_devices=1)
    aps = {k: nc.dram_tensor(f"in_{k}", v.shape, mybir.dt.from_np(v.dtype), kind="ExternalInput").ap()
           for k, v in arrays.items()}
    aps["out"] = nc.dram_tensor("out", (N, D), F32, kind="ExternalOutput").ap()
    build(nc, aps)
    r = run_bass_kernel_spmd(nc, [{f"in_{k}": v for k, v in arrays.items()}], core_ids=[0])
    return r.results[0]["out"].reshape(B, S, D)
```
